# Optimizing a Trainium2 kernel written in Bass

```python
import numpy as np
import jax
import jax.numpy as jnp

def _softmax(x, axis=-1):
    return jax.nn.softmax(x, axis=axis)

def _gelu(x):
    return jax.nn.gelu(x, approximate=True)

def _silu(x):
    return jax.nn.silu(x)

def _sigmoid(x):
    return jax.nn.sigmoid(x)

def _layernorm(x, axis=-1, eps=1e-05):
    m = jnp.mean(x, axis=axis, keepdims=True)
    v = jnp.var(x, axis=axis, keepdims=True)
    return (x - m) / jnp.sqrt(v + eps)

def _scatter_add(tgt, idx, src, axis=0):
    return tgt.at[idx].add(src)

def _segment_sum(src, seg, n):
    return jax.ops.segment_sum(src, seg, n)
kernel_name = 'mk_xattn_ffn_d1_seqx_r2_a94c8f'

def setup_inputs(seed: int=0):
    np.random.seed(seed)
    _w = jnp.asarray

    def _rec_inputs():
        import jax
        import jax.numpy as jnp
        _rk = jax.random.key(seed)
        x = -0.0003929 + 0.9999 * jax.random.normal(jax.random.fold_in(_rk, 1), (4, 2048, 512), jnp.float32)
        _lenS = 2048 - jax.random.randint(jax.random.fold_in(_rk, 7), (4,), 0, max(1, 2048 // 4) + 1, jnp.int32)
        _lenS2 = 77 - jax.random.randint(jax.random.fold_in(_rk, 8), (4,), 0, max(1, 77 // 4) + 1, jnp.int32)
        _ctx_768P = jax.random.normal(jax.random.fold_in(_rk, 11), (4, 16, 384), jnp.float32)
        _ctx_768c = jax.random.dirichlet(jax.random.fold_in(_rk, 511), 0.3 * jnp.ones((16,), jnp.float32), (4, 77))
        _ctx_768t = jnp.einsum('bsk,bkd->bsd', _ctx_768c, _ctx_768P)
        _ctx_768t = _ctx_768t * jax.lax.rsqrt(jnp.mean(jnp.square(_ctx_768t)) + 1e-12) * 0.953939
        ctx_768 = -0.00055796 + 0.999787 * (_ctx_768t + 0.3 * jax.random.normal(jax.random.fold_in(_rk, 611), (4, 77, 384), jnp.float32))
        return (x, ctx_768)
    x, ctx_768 = _rec_inputs()

    def _L0_xattn_setup():
        import jax, jax.numpy as jnp
        import numpy as np
        IMAGE_DIM = 512
        TEXT_DIM = 384
        NUM_HEADS = 16
        HEAD_DIM = IMAGE_DIM // NUM_HEADS
        key = jax.random.key(seed)
        ks = jax.random.split(key, 14)
        B, N, M = (4, 2048, 256)
        s_img = 1.0 / np.sqrt(IMAGE_DIM)
        s_txt = 1.0 / np.sqrt(TEXT_DIM)
        s_ff = 1.0 / np.sqrt(2 * IMAGE_DIM)
        return {'x': jax.random.normal(ks[0], (B, N, IMAGE_DIM), jnp.float32), 'y': jax.random.normal(ks[1], (B, M, TEXT_DIM), jnp.float32), 'Wq': jax.random.normal(ks[2], (IMAGE_DIM, IMAGE_DIM), jnp.float32) * s_img, 'bq': jax.random.normal(ks[3], (IMAGE_DIM,), jnp.float32) * s_img, 'Wk': jax.random.normal(ks[4], (TEXT_DIM, IMAGE_DIM), jnp.float32) * s_txt, 'bk': jax.random.normal(ks[5], (IMAGE_DIM,), jnp.float32) * s_txt, 'Wv': jax.random.normal(ks[6], (TEXT_DIM, IMAGE_DIM), jnp.float32) * s_txt, 'bv': jax.random.normal(ks[7], (IMAGE_DIM,), jnp.float32) * s_txt, 'W1': jax.random.normal(ks[8], (IMAGE_DIM, 2 * IMAGE_DIM), jnp.float32) * s_img, 'b1': jax.random.normal(ks[9], (2 * IMAGE_DIM,), jnp.float32) * s_img, 'W2': jax.random.normal(ks[10], (2 * IMAGE_DIM, IMAGE_DIM), jnp.float32) * s_ff, 'b2': jax.random.normal(ks[11], (IMAGE_DIM,), jnp.float32) * s_ff}
    _L0_xattn_all = _L0_xattn_setup()
    _L0_xattn_in = {k: v for k, v in _L0_xattn_all.items() if k in ('Wq', 'bq', 'Wk', 'bk', 'Wv', 'bv', 'W1', 'b1', 'W2', 'b2')}
    del _L0_xattn_all

    def _L0_ffn_setup():
        import jax, jax.numpy as jnp
        import numpy as np
        B, T, D, E, H = (8, 1024, 512, 8, 128)
        LN_EPS = 1e-05
        key = jax.random.key(seed)
        ks = jax.random.split(key, 4)
        return {'x': jax.random.normal(ks[0], (B, T, D), dtype=jnp.float32), 'Wg': jax.random.normal(ks[1], (E, D), dtype=jnp.float32) * 0.02, 'ln_scale': jnp.ones((E, D), dtype=jnp.float32), 'ln_bias': jnp.zeros((E, D), dtype=jnp.float32), 'W1': jax.random.normal(ks[2], (E, D, H), dtype=jnp.float32) * 0.02, 'b1': jnp.zeros((E, H), dtype=jnp.float32), 'W2': jax.random.normal(ks[3], (E, H, D), dtype=jnp.float32) * 0.02, 'b2': jnp.zeros((E, D), dtype=jnp.float32)}
    _L0_ffn_all = _L0_ffn_setup()
    _L0_ffn_in = {k: v for k, v in _L0_ffn_all.items() if k in ('Wg', 'ln_scale', 'ln_bias', 'W1', 'b1', 'W2', 'b2')}
    del _L0_ffn_all
    return {'x': x, 'ctx_768': ctx_768, 'L0_xattn_Wq': _L0_xattn_in['Wq'], 'L0_xattn_bq': _L0_xattn_in['bq'], 'L0_xattn_Wk': _L0_xattn_in['Wk'], 'L0_xattn_bk': _L0_xattn_in['bk'], 'L0_xattn_Wv': _L0_xattn_in['Wv'], 'L0_xattn_bv': _L0_xattn_in['bv'], 'L0_xattn_W1': _L0_xattn_in['W1'], 'L0_xattn_b1': _L0_xattn_in['b1'], 'L0_xattn_W2': _L0_xattn_in['W2'], 'L0_xattn_b2': _L0_xattn_in['b2'], 'L0_ffn_Wg': _L0_ffn_in['Wg'], 'L0_ffn_ln_scale': _L0_ffn_in['ln_scale'], 'L0_ffn_ln_bias': _L0_ffn_in['ln_bias'], 'L0_ffn_W1': _L0_ffn_in['W1'], 'L0_ffn_b1': _L0_ffn_in['b1'], 'L0_ffn_W2': _L0_ffn_in['W2'], 'L0_ffn_b2': _L0_ffn_in['b2']}

def reference(x, ctx_768, L0_xattn_Wq, L0_xattn_bq, L0_xattn_Wk, L0_xattn_bk, L0_xattn_Wv, L0_xattn_bv, L0_xattn_W1, L0_xattn_b1, L0_xattn_W2, L0_xattn_b2, L0_ffn_Wg, L0_ffn_ln_scale, L0_ffn_ln_bias, L0_ffn_W1, L0_ffn_b1, L0_ffn_W2, L0_ffn_b2):
    import jax
    import jax.numpy as jnp

    def _L0_xattn_ref(x, y, Wq, bq, Wk, bk, Wv, bv, W1, b1, W2, b2):
        import jax, jax.numpy as jnp
        import numpy as np
        IMAGE_DIM = 512
        TEXT_DIM = 384
        NUM_HEADS = 16
        HEAD_DIM = IMAGE_DIM // NUM_HEADS
        B, N, _ = x.shape
        M = y.shape[1]
        q = (x @ Wq + bq).reshape(B, N, NUM_HEADS, HEAD_DIM)
        k = (y @ Wk + bk).reshape(B, M, NUM_HEADS, HEAD_DIM)
        v = (y @ Wv + bv).reshape(B, M, NUM_HEADS, HEAD_DIM)
        scale = 1.0 / np.sqrt(HEAD_DIM)
        scores = jnp.einsum('bnhd,bmhd->bhnm', q, k) * scale
        attn = jax.nn.softmax(scores, axis=-1)
        out = jnp.einsum('bhnm,bmhd->bnhd', attn, v).reshape(B, N, IMAGE_DIM)
        h = jax.nn.relu(out @ W1 + b1)
        return h @ W2 + b2

    def _L0_ffn_ref(x, Wg, ln_scale, ln_bias, W1, b1, W2, b2):
        import jax, jax.numpy as jnp
        import numpy as np
        B, T, D, E, H = (8, 1024, 512, 8, 128)
        LN_EPS = 1e-05
        Bs, Ts, Ds = x.shape
        xt = x.reshape(Bs * Ts, Ds)
        logits = xt @ Wg.T
        top1 = jnp.argmax(logits, axis=-1)
        mu = jnp.mean(xt, axis=-1, keepdims=True)
        var = jnp.mean(jnp.square(xt - mu), axis=-1, keepdims=True)
        xhat = (xt - mu) * jax.lax.rsqrt(var + LN_EPS)
        n_experts = Wg.shape[0]

        def body(y, p):
            s_e, b_e, w1, bb1, w2, bb2, eid = p
            h = jax.nn.gelu((xhat * s_e + b_e) @ w1 + bb1, approximate=False)
            out = h @ w2 + bb2
            mask = (top1 == eid)[:, None].astype(out.dtype)
            return (y + mask * out, None)
        y0 = jnp.zeros_like(xt)
        y, _ = jax.lax.scan(body, y0, (ln_scale, ln_bias, W1, b1, W2, b2, jnp.arange(n_experts)))
        return y.reshape(Bs, Ts, Ds)
    x = x + _L0_xattn_ref(_layernorm(x, axis=-1), ctx_768, L0_xattn_Wq, L0_xattn_bq, L0_xattn_Wk, L0_xattn_bk, L0_xattn_Wv, L0_xattn_bv, L0_xattn_W1, L0_xattn_b1, L0_xattn_W2, L0_xattn_b2)
    x = x + _L0_ffn_ref(_layernorm(x, axis=-1), L0_ffn_Wg, L0_ffn_ln_scale, L0_ffn_ln_bias, L0_ffn_W1, L0_ffn_b1, L0_ffn_W2, L0_ffn_b2)
    return x

_drawn_inputs = setup_inputs


def setup_inputs(seed=0):
    import zlib

    import numpy as np

    out = dict(_drawn_inputs(seed))
    spreads = {'L0_ffn_ln_scale': (1.0, 0.6),
     'L0_ffn_ln_bias': (0.0, 0.8),
     'L0_ffn_b1': (0.0, 0.662),
     'L0_ffn_b2': (0.0, 0.1)}
    factors = {'L0_xattn_bq': 5.45, 'L0_xattn_bk': 8.0}
    for name, (base, spread) in spreads.items():
        noise = np.random.default_rng([zlib.crc32(name.encode()), seed]).standard_normal(out[name].shape)
        drawn = base * np.exp(spread * noise) if base else spread * noise
        out[name] = jnp.asarray(drawn.astype(out[name].dtype))
    for name, factor in factors.items():
        out[name] = (out[name] * factor).astype(out[name].dtype)
    return out
```

```python
from contextlib import ExitStack

import concourse.bass as bass
from concourse import mybir

F32 = mybir.dt.float32
F32R = mybir.dt.float32r
BF16 = mybir.dt.bfloat16
U32 = mybir.dt.uint32
I32 = mybir.dt.int32
ALU = mybir.AluOpType
ACT = mybir.ActivationFunctionType
AX = mybir.AxisListType.X

P = 128
D = 512
KD = D // P
TD = 384
KT = TD // P
NB = 4
TOK = 2048
M = 77
HEADS = 16
HD = D // HEADS
HG = P // HD
SCALE = float(HD) ** -0.5
F = 1024
MF = F // P
NE = 8
EH = 128
EPS = 1e-5
N = NB * TOK
BLK = 512
SUB = BLK // P
NBLK = N // BLK
BPB = TOK // BLK
SC = HG * M
CH = [103, 103, 102]
CO = [0, 103, 206]
NC = len(CH)
SLOTS = 8
ROW = 516
REG = N + P
NT = N // P + NE - 1
NROW = 14
PIECES = []
for _h in range(HG):
    for _c in range(NC):
        _a, _z = max(M * _h, CO[_c]), min(M * _h + M, CO[_c] + CH[_c])
        if _a < _z:
            PIECES.append((_c, _a - CO[_c], _a - M * _h, _z - _a, _h))


def xattn_moe_kernel(nc, A, out):
    region = nc.dram_tensor("region", [NE * REG + P, ROW], F32).ap()
    k_parts = nc.dram_tensor("k_parts", [NB, 2, KD, P, M], F32).ap()
    v_parts = nc.dram_tensor("v_parts", [NB, 2, M, D], F32).ap()

    end = [nc.sbuf_base]

    def at(name, shape, dt, offset):
        return nc.alloc_sbuf_tensor_at(name, shape, dt, offset=offset)

    def size(shape, dt):
        n = 2 if dt == BF16 else 4
        for s in shape[1:]:
            n *= s
        return (n + 31) // 32 * 32

    def sb(name, shape, dt=F32):
        o = (end[0] + 31) // 32 * 32
        end[0] = o + size(shape, dt)
        return at(name, shape, dt, o), o

    wq, wq_at = sb("wq", [P, 2, KD, D], F32R)
    w1, w1_at = sb("w1", [P, 2, KD, F], F32R)
    w2, w2_at = sb("w2", [P, 2, MF, D], F32R)
    wg, _ = sb("wg", [P, 2, KD, NE], F32R)
    kbd, kbd_at = sb("kbd", [P, 2, KD, SC], F32R)
    vbd, _ = sb("vbd", [P, 2, KD, NC, P], F32R)
    rows = [sb(f"rows{i}", [P, SUB, ROW]) for i in range(2)]
    rows_at = [r[1] for r in rows]
    rows = [r[0] for r in rows]
    actA, actA_at = sb("actA", [P, 2, KD, BLK], F32R)
    actQ, _ = sb("actQ", [P, 2, KD, BLK], F32R)
    actH, actH_at = sb("actH", [P, 2, SLOTS, BLK], F32R)
    E, E_at = sb("E", [P, KD, SUB, SC])
    xn = [sb(f"xn{i}", [P, D]) for i in range(2)]
    xn_at = xn[0][1]
    xn = [t[0] for t in xn]
    htmp = [sb(f"htmp{i}", [P, BLK]) for i in range(2)]
    htmp_at = htmp[0][1]
    htmp = [t[0] for t in htmp]
    b2bc, _ = sb("b2bc", [P, D])
    ident, _ = sb("ident", [P, P])
    tri, _ = sb("tri", [P, P], BF16)
    ones, _ = sb("ones", [P, P], BF16)
    prio, _ = sb("prio", [P, SUB, NE])
    base, _ = sb("base", [P, SUB, NE])
    ids, _ = sb("ids", [P, N // P], U32)
    bq, _ = sb("bq", [P, KD])
    bk, _ = sb("bk", [P, KD])
    b1, _ = sb("b1", [P, MF])
    mx, _ = sb("mx", [P, KD * SUB, HG])
    sm, _ = sb("sm", [P, KD, SUB * HG])
    rc, _ = sb("rc", [P, KD, SUB * HG])
    bn, _ = sb("bn", [P, SUB, 6])
    bn2, _ = sb("bn2", [P, SUB, 6])
    mv, _ = sb("mv", [P, SUB, 2])
    mvx, _ = sb("mvx", [P, SUB, 2])
    nw, _ = sb("nw", [P, 3, SUB])
    rx, _ = sb("rx", [P, SUB])
    r1, _ = sb("r1", [P, SUB])
    r2, _ = sb("r2", [P, SUB])
    nmr, _ = sb("nmr", [P, SUB])
    tB, _ = sb("tB", [P, SUB])
    lg, _ = sb("lg", [P, SUB, NE])
    lw, _ = sb("lw", [P, SUB, NE])
    lm, _ = sb("lm", [P, SUB])
    oh, _ = sb("oh", [P, SUB, NE], BF16)
    cum, _ = sb("cum", [P, NE], BF16)
    rk, _ = sb("rk", [P, SUB, NE])
    posf, _ = sb("posf", [P, SUB])
    pos = [sb(f"pos{i}", [P, SUB], U32)[0] for i in range(2)]
    assert end[0] <= nc.sbuf_usable_end, (end[0], nc.sbuf_usable_end)
    xt = lambda s: E[:, s, :, :].rearrange("p a c -> p (a c)")[:, 0:D]
    lgT = E[0:NE, 0, :, :].rearrange("p a c -> p (a c)")[:, D + 64:D + 64 + BLK]

    wk_raw = at("wk_raw", [P, KT, D], F32, E_at)
    wv_raw = at("wv_raw", [P, KT, D], F32, E_at + 4 * KT * D)
    ctxT = at("ctxT", [P, KT, NB * M], F32, E_at + 8 * KT * D)
    wq_raw = at("wq_raw", [P, KD * D], F32, actH_at)
    w1_raw = at("w1_raw", [P, KD * F], F32, actH_at + 4 * KD * D)
    w2_raw = [at("w2_raw0", [P, MF * D // 2], F32, actH_at + 4 * KD * D + 4 * KD * F),
              at("w2_raw1", [P, MF * D // 2], F32, rows_at[1])]
    c_raw = at("c_raw", [P, 2 * P], F32, actA_at)
    wg_raw = at("wg_raw", [P, KD * NE], F32, actA_at + 8 * P)
    k_hl = at("k_hl", [P, 2, KD, NB * M], F32R, w1_at)
    v_hl = [at(f"v_hl{i}", [M, 2, D], F32R, w1_at + size([P, 2, KD, NB * M], F32) + 8 * D * i) for i in range(2)]
    v_f = [at(f"v_f{i}", [M, D], F32, w1_at + size([P, 2, KD, NB * M], F32) + 16 * D + 4 * D * i) for i in range(2)]
    bvbc = at("bvbc", [M, D], F32, w1_at + size([P, 2, KD, NB * M], F32) + 24 * D)

    e1 = at("e1", [P, KD, NE, EH], F32, wq_at)
    e2_raw = at("e2_raw", [P, NE, D], F32, actA_at)
    e2 = at("e2", [P, 2, NE, D], F32R, w1_at)
    b2e = at("b2e", [P, NE, D], F32, kbd_at)
    b1e = at("b1e", [P, NE, EH], F32, kbd_at + 4 * NE * D)
    assert 4 * NE * (D + EH) <= size([P, 2, KD, SC], F32) + size([P, 2, KD, NC, P], F32)
    o = [w2_at]

    def sb2(name, shape, dt=F32):
        o[0] += size(shape, dt)
        return at(name, shape, dt, o[0] - size(shape, dt))

    rowB = [sb2(f"rowB{i}", [P, ROW]) for i in range(NROW)]
    assert o[0] <= w2_at + size([P, 2, MF, D], F32)
    o[0] = E_at
    xh = [sb2(f"xh{i}", [P, D]) for i in range(2)]
    xhT = [sb2(f"xhT{i}", [P, KD, P]) for i in range(2)]
    hb = [sb2(f"hb{i}", [P, EH]) for i in range(2)]
    gl = [sb2(f"gl{i}", [P, EH]) for i in range(2)]
    gT = [sb2(f"gT{i}", [P, 2, P], F32R) for i in range(2)]
    assert o[0] <= E_at + size([P, KD, SUB, SC], F32)
    o[0] = rows_at[0]
    lns = sb2("lns", [P, KD, NE])
    lnb = sb2("lnb", [P, KD, NE])
    lnbb = sb2("lnbb", [P, P])
    padrow = sb2("padrow", [P, ROW])
    padoff = sb2("padoff", [P, NE])
    padf = sb2("padf", [P, NE])
    padu = sb2("padu", [P, NE], U32)
    cnt = sb2("cnt", [P, NE])
    cti = sb2("cti", [P, NE], I32)
    ctl = sb2("ctl", [P, NE])
    cinc = sb2("cinc", [P, NE])
    stp = sb2("stp", [P, NE])
    ex = sb2("ex", [1, NT])
    rw = sb2("rw", [1, NT])
    exi = sb2("exi", [1, NT], I32)
    rwi = sb2("rwi", [1, NT], I32)
    assert o[0] <= rows_at[0] + size([P, SUB, ROW], F32)
    jt = at("jt", [1, NT, NE], F32, xn_at)
    ge = at("ge", [1, NT, NE], F32, htmp_at)

    with ExitStack() as ctx:
        bank = [ctx.enter_context(nc.psum_tensor(f"bank{i}", [P, 512], F32)) for i in range(8)]

        def sem(name):
            return ctx.enter_context(nc.semaphore(name))

        L = {n: sem(f"ld_{n}") for n in (
            "consts", "wk", "wv", "ctx", "wq", "w1", "w2a", "w2b", "e1", "e2", "eb", "ln", "tab", "pad0")}
        ld_x = [sem(f"ld_x{i}") for i in range(2)]
        st_k, st_v, ld_k, ld_v = sem("st_k"), sem("st_v0"), sem("ld_k"), sem("ld_v")
        st_vs = [st_v, sem("st_v1")]
        scat = [sem(f"scat{i}") for i in range(2)]
        st_pad = sem("st_pad")
        ld_row = [sem(f"ld_row{i}") for i in range(NROW)]
        st_out = [sem(f"st_out{i}") for i in range(NROW)]
        dve_chain, act_chain, pool_chain = sem("dve_chain"), sem("act_chain"), sem("pool_chain")
        S = {n: sem(n) for n in (
            "pe_k act_k dve_k pe_v dve_vf act_v dve_v pool_zero dve_const "
            "act_wq dve_wq act_w1 dve_w1 act_w2a dve_w2a act_w2b dve_w2b "
            "dve_xn pool_xb pe_xT act_xT dve_xT pe_q act_q dve_q pe_s dve_max dve_sub act_exp dve_rc pool_p "
            "pe_pt act_pt dve_pt pe_av act_o dve_o pe_h act_h act_hh dve_h pe_y dve_x2 dve_s2 act_xt dve_row "
            "pe_tt act_tt dve_tt pe_l act_l pe_lt dve_lg dve_oh pe_rk dve_rk dve_cum dve_pos "
            "pe_cnt dve_pad dve_tab dve_e1 pe_b1 dve_b1 act_e2 dve_e2 "
            "b_xh b_xT b_xTs b_h b_hb b_gl b_g b_ghi b_glo b_y b_out").split()}
        pe_k, pe_v = S["pe_k"], S["pe_v"]
        b_xb = [sem("b_xb0"), sem("b_xb1")]

        sched = []

        def step(kind, *i):
            sched.append((kind, *i))

        def attention_tail(b):
            for c in range(NC):
                step("PT", b, 0, c)
            if b:
                step("X2STAT", b - 1)
            for g in range(KD):
                if g + 1 < KD:
                    for c in range(NC):
                        step("PT", b, g + 1, c)
                step("AV", b, g)

        step("SETUP")
        step("XLOAD", 0)
        for m in range(KD):
            step("KP", m)
        step("KSTORE")
        step("CONV_WQ")
        step("XSTAT", 0)
        for s in range(SUB):
            step("XT", 0, s)
        for m in range(KD):
            step("Q", 0, m)
        step("KLOAD", 0)
        for i in range(NB):
            step("VP", i)
        step("VLOAD", 0)
        for g in range(KD):
            for s in range(SUB):
                step("S", 0, g, s)
            step("EXP", 0, g)
            step("SUM", 0, g)
        step("CONV_W12")
        step("XLOAD", 1)
        for b in range(NBLK):
            last = b == NBLK - 1
            if (b + 1) % BPB == 0 and not last:
                step("KLOAD", (b + 1) // BPB)
            attention_tail(b)
            if (b + 1) % BPB == 0 and not last:
                step("VLOAD", (b + 1) // BPB)
            if last:
                step("EB_LOAD")
            for m in range(MF):
                if b and m == 0:
                    step("XTT", b - 1)
                    step("DRAIN")
                step("H", b, m)
                if b and m == 0:
                    for s in range(SUB):
                        step("TT", b - 1, s)
                    step("ROWTAIL", b - 1)
                if b and m == 2:
                    step("L", b - 1)
                if b and m == 3:
                    step("LT", b - 1)
                if b and m == 4:
                    step("RK", b - 1)
                    step("DRAIN")
                    step("SCAT", b - 1)
                    if not last:
                        step("XLOAD", b + 1)
            if last:
                step("E2_LOAD")
            else:
                step("XSTAT", b + 1)
            step("Y", b, 0)
            if not last:
                for s in range(SUB):
                    step("XT", b + 1, s)
            step("Y", b, 1)
            if not last:
                step("Q", b + 1, 0)
                for g in range(KD):
                    if g + 1 < KD:
                        step("Q", b + 1, g + 1)
                    if g == KD - 1:
                        step("Y", b, 2)
                    for s in range(SUB):
                        step("S", b + 1, g, s)
                    step("EXP", b + 1, g)
                    if g:
                        step("SUM", b + 1, g - 1)
                if b + 2 == NBLK:
                    step("E1_LOAD")
            else:
                step("Y", b, 2)
                step("E2_CONV")
            if not last:
                step("SUM", b + 1, KD - 1)
            step("Y", b, 3)
        step("X2STAT", NBLK - 1)
        step("DRAIN")
        step("XTT", NBLK - 1)
        for s in range(SUB):
            step("TT", NBLK - 1, s)
        step("ROWTAIL", NBLK - 1)
        step("B1")
        step("L", NBLK - 1)
        step("LT", NBLK - 1)
        step("RK", NBLK - 1)
        step("DRAIN")
        step("SCAT", NBLK - 1)
        step("TABLE")
        for t in range(-2, NT + 1):
            if t + 2 < NT:
                step("B_XT", t + 2)
            if 0 <= t + 1 < NT:
                step("B_H", t + 1)
            if 0 <= t - 1:
                step("B_Y", t - 1)
            if 0 <= t < NT:
                step("B_G", t)

        freed = {
            "KP": lambda m: (S["dve_k"], m + 1),
            "VP": lambda i: (S["dve_vf"], i + 1),
            "XT": lambda b, s: (S["dve_xT"], SUB * b + s + 1),
            "Q": lambda b, m: (S["dve_q"], KD * b + m + 1),
            "S": lambda b, g, s: (S["dve_sub"], SUB * (KD * b + g) + s + 1),
            "PT": lambda b, g, c: (S["dve_pt"], NC * (KD * b + g) + c + 1),
            "AV": lambda b, g: (S["dve_o"], KD * b + g + 1),
            "H": lambda b, m: (S["act_hh"], MF * b + m + 1),
            "Y": lambda b, s: (S["dve_x2"], SUB * b + s + 1),
            "TT": lambda b, s: (S["dve_tt"], SUB * b + s + 1),
            "L": lambda b: (S["act_l"], b + 1),
            "LT": lambda b: (S["dve_lg"], b + 1),
            "RK": lambda b: (S["dve_rk"], b + 1),
            "TABLE": lambda: (S["dve_pad"], 1),
            "B1": lambda: (S["dve_b1"], 1),
            "B_XT": lambda t: (S["b_xTs"], t + 1),
            "B_H": lambda t: (S["b_hb"], t + 1),
            "B_G": lambda t: (S["b_glo"], t + 1),
            "B_Y": lambda t: (S["b_out"], t + 1),
        }
        bank_of, before, users = {}, {}, [None] * 8
        n = 0
        for kind, *i in sched:
            if kind in freed:
                for _ in range(2 if kind == "B1" else 1):
                    key = (kind, *i)
                    bank_of.setdefault(key, []).append(n % 8)
                    if users[n % 8] is not None:
                        before.setdefault(key, []).append(users[n % 8])
                    users[n % 8] = freed[kind](*i)
                    n += 1

        def own_bank(eng, *key):
            for s, v in before.get(key, []):
                eng.wait_ge(s, v)
            return bank[bank_of[key][0]]

        def of(*key):
            return bank[bank_of[key][0]]

        def split3(a, b):
            return ((a[0], b[0]), (a[0], b[1]), (a[1], b[0]))

        def f32(ap):
            return ap.bitcast(F32)

        counts = {"dve": 0, "act": 0, "pool": 0}

        def dve_link(eng, ins):
            counts["dve"] += 1
            ins.then_inc(dve_chain, 1)
            eng.wait_ge(dve_chain, counts["dve"])

        chains = []
        DRIP = {"Q": 2, "S": 0, "PT": 2, "AV": 2, "H": 8, "Y": 1, "TT": 1, "XT": 0}

        def drip(n):
            while chains and n > 0:
                n -= 1
                if next(chains[0], "end") == "end":
                    chains.pop(0)

        def drain():
            while chains:
                drip(1)

        def issued(ins):
            counts["dve"] += 1
            ins.then_inc(dve_chain, 1)
            return counts["dve"]

        def grouped(ap, n):
            return ap.rearrange("p (h k) -> p h k", h=n)

        def spread(ap, n):
            return ap.unsqueeze(2).to_broadcast([ap.shape[0], ap.shape[1], n])

        def sp_setup(sp):
            sp.dma_start(ctxT[:], A["ctxT"]).then_inc(L["ctx"], 16)
            sp.dma_start(wk_raw[:], A["Wk"]).then_inc(L["wk"], 16)
            small = [(ident[:], A["ident"]), (c_raw[:], A["masks"]), (prio[:], A["prio"]), (base[:], A["base"]),
                     (ids[:], A["ids"]), (bq[:], A["bq"]), (bk[:], A["bk"]), (b1[:], A["b1"]),
                     (wg_raw[:], A["WgT"]), (b2bc[:], A["b2"].to_broadcast([P, D])), (bvbc[:], A["bv"].to_broadcast([M, D]))]
            for dst, src in small:
                sp.dma_start(dst, src).then_inc(L["consts"], 16)
            return len(small)

        NSMALL = 11

        def sp_setup2(sp):
            sp.dma_start(wq_raw[:], A["Wq"]).then_inc(L["wq"], 16)
            sp.dma_start(wv_raw[:], A["Wv"]).then_inc(L["wv"], 16)
            sp.dma_start(w1_raw[:], A["W1"]).then_inc(L["w1"], 16)
            sp.dma_start(w2_raw[0][:], A["W2"][:, 0:MF * D // 2]).then_inc(L["w2a"], 16)
            sp.dma_start(w2_raw[1][:], A["W2"][:, MF * D // 2:]).then_inc(L["w2b"], 16)

        def sp_xload(sp, b):
            if b == 1:
                sp.wait_ge(S["dve_w2b"], 1)
                sp.wait_ge(S["pool_zero"], 4)
            if b >= 2:
                sp.wait_ge(scat[b % 2], 16 * SUB * (b // 2))
            src = A["x"][b * BLK:(b + 1) * BLK, :].rearrange("(s p) d -> p s d", p=P)
            sp.dma_start(rows[b % 2][:, :, 0:D], src).then_inc(ld_x[b % 2], 16)
            if b == 0:
                sp_setup2(sp)

        def sp_kstore(sp):
            sp.wait_ge(S["act_k"], KD)
            sp.wait_ge(S["dve_k"], KD)
            for h in range(2):
                for i in range(NB):
                    sp.dma_start(k_parts[i, h].rearrange("g p k -> p g k"),
                                 f32(k_hl[:, h, :, M * i:M * i + M])).then_inc(st_k, 16)

        def sp_kload(sp, i):
            if i == 0:
                sp.wait_ge(st_k, 16 * 2 * NB)
                sp.wait_ge(S["pool_zero"], 1)
            else:
                sp.wait_ge(S["pe_s"], KD * SUB * BPB * i)
            for h in range(HG):
                for g in range(KD):
                    sp.dma_start(f32(kbd[HD * h:HD * h + HD, :, g, M * h:M * h + M]),
                                 k_parts[i, :, g, HD * h:HD * h + HD, :].rearrange("s p k -> p s k")
                                 ).then_inc(ld_k, 16)

        def sp_vload(sp, i):
            if i == 0:
                for n_, s_ in enumerate(st_vs):
                    sp.wait_ge(s_, 16 * (NB // 2))
                sp.wait_ge(S["pool_zero"], 2)
            else:
                sp.wait_ge(S["pe_av"], KD * BPB * i)
            for c, r, k, m, h in PIECES:
                for part in range(2):
                    src = v_parts[i, part, k:k + m, :].rearrange("k (g h f) -> k g h f", g=KD, h=HG)[:, :, h, :]
                    sp.dma_start(f32(vbd[r:r + m, part, :, c, HD * h:HD * h + HD]), src).then_inc(ld_v, 16)

        KLOADS, VLOADS = HG * KD, 2 * len(PIECES)

        def sp_vstore(sp, i):
            sp.wait_ge(S["act_v"], i + 1)
            sp.wait_ge(S["dve_v"], i + 1)
            sp.dma_start(v_parts[i].rearrange("s k f -> k s f"), f32(v_hl[i % 2][:])).then_inc(st_vs[i % 2], 16)

        def sp_e1load(sp):
            sp.wait_ge(S["pe_q"], KD * NBLK)
            sp.dma_start(e1[:], A["E1"]).then_inc(L["e1"], 16)

        def sp_ebload(sp):
            sp.wait_ge(S["pe_s"], KD * SUB * NBLK)
            sp.wait_ge(S["pe_av"], KD * NBLK)
            sp.dma_start(b2e[:], A["Eb2"].to_broadcast([P, NE, D])).then_inc(L["eb"], 16)
            sp.dma_start(b1e[:], A["Eb1"].to_broadcast([P, NE, EH])).then_inc(L["eb"], 16)

        def sp_e2load(sp):
            sp.wait_ge(S["pe_h"], MF * NBLK)
            sp.dma_start(e2_raw[:], A["E2"]).then_inc(L["e2"], 16)
            sp.wait_ge(scat[0], 16 * SUB * (NBLK // 2))
            sp.wait_ge(S["pe_xT"], SUB * NBLK)
            sp.dma_start(lns[:], A["lns"]).then_inc(L["ln"], 16)
            sp.dma_start(lnb[:], A["lnb"]).then_inc(L["ln"], 16)
            sp.dma_start(padrow[:], A["padrow"]).then_inc(L["tab"], 16)
            sp.dma_start(padoff[:], A["padoff"]).then_inc(L["tab"], 16)
            sp.dma_start(jt[:], A["jt"]).then_inc(L["tab"], 16)
            sp.wait_ge(L["tab"], 48)
            sp.dma_start(region[NE * REG:NE * REG + P, :], padrow[:]).then_inc(L["pad0"], 16)

        def pool_setup(pool):
            z = lambda ap: nc.gpsimd.memset(ap, 0.0)
            z(f32(kbd[:])).then_inc(S["pool_zero"], 1)
            z(f32(vbd[:])).then_inc(S["pool_zero"], 1)
            z(rows[0][:, :, D:ROW]).then_inc(S["pool_zero"], 1)

        def dve_setup(dve):
            dve.memset(cum[:], 0.0)
            dve.wait_ge(L["consts"], 16 * NSMALL)
            dve.tensor_copy(tri[:], c_raw[:, 0:P])
            dve.tensor_copy(ones[:], c_raw[:, P:2 * P])
            wgr = wg_raw[:].rearrange("p (k e) -> p k e", e=NE)
            dve_link(dve, dve.tensor_copy(wg[:, 0], wgr))
            dve.tensor_tensor(wg[:, 1], wgr, f32(wg[:, 0]), ALU.subtract).then_inc(S["dve_const"], 1)

        def pe_kp(pe, m):
            p = own_bank(pe, "KP", m)
            if m == 0:
                pe.wait_ge(L["ctx"], 16)
                pe.wait_ge(L["wk"], 16)
            for k in range(KT):
                mm = pe.matmul(p[:, 0:NB * M], wk_raw[:, k, P * m:P * m + P], ctxT[:, k, :],
                               start=k == 0, stop=k == KT - 1)
            mm.then_inc(pe_k, 1)

        def act_kp(act, m):
            if m == 0:
                act.wait_ge(L["consts"], 16 * NSMALL)
            act.wait_ge(pe_k, m + 1)
            act.activation(k_hl[:, 0, m, :], of("KP", m)[:, 0:NB * M], ACT.Identity,
                           bias=bk[:, m:m + 1]).then_inc(S["act_k"], 1)

        def dve_kp(dve, m):
            dve.wait_ge(S["act_k"], m + 1)
            dve.scalar_tensor_tensor(k_hl[:, 1, m, :], of("KP", m)[:, 0:NB * M], bk[:, m:m + 1],
                                     f32(k_hl[:, 0, m, :]), ALU.add, ALU.subtract).then_inc(S["dve_k"], 1)

        def pe_vp(pe, i):
            p = own_bank(pe, "VP", i)
            pe.wait_ge(L["wv"], 16)
            for k in range(KT):
                mm = pe.matmul(p[0:M, :], ctxT[:, k, M * i:M * i + M], wv_raw[:, k, :],
                               start=k == 0, stop=k == KT - 1)
            mm.then_inc(pe_v, 1)

        def dve_vp(dve, i):
            dve.wait_ge(pe_v, i + 1)
            if i >= 2:
                dve.wait_ge(st_vs[i % 2], 16 * (i // 2))
            dve.tensor_tensor(v_f[i % 2][:], of("VP", i)[0:M, :], bvbc[:], ALU.add).then_inc(S["dve_vf"], 1)
            dve.wait_ge(S["act_v"], i + 1)
            dve.tensor_tensor(v_hl[i % 2][:, 1], v_f[i % 2][:], f32(v_hl[i % 2][:, 0]),
                              ALU.subtract).then_inc(S["dve_v"], 1)

        def act_vp(act, i):
            act.wait_ge(S["dve_vf"], i + 1)
            if i >= 2:
                act.wait_ge(st_vs[i % 2], 16 * (i // 2))
            act.activation(v_hl[i % 2][:, 0], v_f[i % 2][:], ACT.Identity).then_inc(S["act_v"], 1)

        def act_convert(act, w, raw, ld, done):
            act.wait_ge(ld, 16)
            act.activation(w, raw, ACT.Identity).then_inc(done, 1)

        def dve_convert(dve, lo, hi, raw, hi_done, done):
            dve.wait_ge(hi_done, 1)
            dve.tensor_tensor(lo, raw, f32(hi), ALU.subtract).then_inc(done, 1)

        wq_hl = [wq[:, h].rearrange("p k n -> p (k n)") for h in range(2)]
        w1_hl = [w1[:, h].rearrange("p k n -> p (k n)") for h in range(2)]
        w2_hl = [[w2[:, h, MF // 2 * j:MF // 2 * (j + 1)].rearrange("p k n -> p (k n)") for h in range(2)]
                 for j in range(2)]

        def act_conv_wq(act):
            act_convert(act, wq_hl[0], wq_raw[:], L["wq"], S["act_wq"])

        def dve_conv_wq(dve):
            dve_convert(dve, wq_hl[1], wq_hl[0], wq_raw[:], S["act_wq"], S["dve_wq"])

        def act_conv_w12(act):
            for s_ in st_vs:
                act.wait_ge(s_, 16 * (NB // 2))
            act.wait_ge(st_k, 16 * 2 * NB)
            act_convert(act, w1_hl[0], w1_raw[:], L["w1"], S["act_w1"])
            act_convert(act, w2_hl[1][0], w2_raw[1][:], L["w2b"], S["act_w2b"])
            act_convert(act, w2_hl[0][0], w2_raw[0][:], L["w2a"], S["act_w2a"])

        def dve_conv_w12(dve):
            dve_convert(dve, w1_hl[1], w1_hl[0], w1_raw[:], S["act_w1"], S["dve_w1"])
            dve_convert(dve, w2_hl[1][1], w2_hl[1][0], w2_raw[1][:], S["act_w2b"], S["dve_w2b"])
            dve_convert(dve, w2_hl[0][1], w2_hl[0][0], w2_raw[0][:], S["act_w2a"], S["dve_w2a"])

        def pool_conv_w12(pool):
            pool.wait_ge(S["dve_w2b"], 1)
            nc.gpsimd.memset(rows[1][:, :, D:ROW], 0.0).then_inc(S["pool_zero"], 1)

        def rsqrt(dve, var, y, n):
            v, t = nw[:, 0, :], nw[:, 1, :]
            steps = [lambda: dve.tensor_scalar(v, var, EPS, None, ALU.add),
                     lambda: dve.tensor_scalar(t.bitcast(I32), v.bitcast(I32), 1, None, ALU.logical_shift_right),
                     lambda: dve.tensor_scalar(y.bitcast(I32), t.bitcast(I32), -1, float(0x5F3759DF),
                                               ALU.mult, ALU.add)]
            steps += [lambda: dve.tensor_tensor(t, y, y, ALU.mult),
                      lambda: dve.scalar_tensor_tensor(t, t, -0.5, v, ALU.mult, ALU.mult),
                      lambda: dve.scalar_tensor_tensor(y, t, 1.5, y, ALU.add, ALU.mult)] * 3
            for f in steps:
                dve.wait_ge(dve_chain, n)
                n = issued(f())
                yield
            return n

        def aggregate(dve, raw, into, n):
            dve.wait_ge(dve_chain, n)
            for s in range(SUB):
                n = issued(dve.bn_aggr(into[:, s, :], raw[:, s, :]))
                yield
            return n

        def dve_xstat(dve, b):
            def chain():
                dve.wait_ge(ld_x[b % 2], 16 * (b // 2 + 1))
                for s in range(SUB):
                    n = issued(dve.bn_stats(bn[:, s, :], rows[b % 2][:, s, 0:D]))
                    yield
                n = yield from aggregate(dve, bn, mvx, n)
                n = yield from rsqrt(dve, mvx[:, :, 1], rx[:], n)
                dve.wait_ge(dve_chain, n)
                for s in range(2):
                    dve_xn(dve, b, s)
                    yield
            chains.append(chain())

        def dve_xn(dve, b, s):
            i = SUB * b + s
            if i >= 2:
                dve.wait_ge(S["pe_xT"], i - 1)
            dve.tensor_scalar(xn[s % 2][:], rows[b % 2][:, s, 0:D], mvx[:, s, 0:1], rx[:, s:s + 1],
                              ALU.subtract, ALU.mult).then_inc(S["dve_xn"], 1)

        def pe_xT(pe, b, s):
            p = own_bank(pe, "XT", b, s)
            if b == 0 and s == 0:
                pe.wait_ge(L["consts"], 16 * NSMALL)
            pe.wait_ge(S["dve_xn"], SUB * b + s + 1)
            for k in range(KD):
                mm = pe.transpose(p[:, P * k:P * k + P], xn[s % 2][:, P * k:P * k + P], ident[:])
            mm.then_inc(S["pe_xT"], 1)

        def act_xT(act, b, s):
            if b == 0 and s == 0:
                act.wait_ge(S["dve_const"], 1)
            act.wait_ge(S["pe_xT"], SUB * b + s + 1)
            act.activation(actA[:, 0, :, P * s:P * s + P], of("XT", b, s)[:].rearrange("p (k t) -> p k t", k=KD),
                           ACT.Identity).then_inc(S["act_xT"], 1)

        def dve_xT(dve, b, s):
            if s == 0:
                drain()
            dve.wait_ge(S["act_xT"], SUB * b + s + 1)
            dve.tensor_tensor(actA[:, 1, :, P * s:P * s + P], of("XT", b, s)[:].rearrange("p (k t) -> p k t", k=KD),
                              f32(actA[:, 0, :, P * s:P * s + P]), ALU.subtract).then_inc(S["dve_xT"], 1)
            if s + 2 < SUB:
                dve_xn(dve, b, s + 2)

        def pool_xT(pool, b, s):
            pool.wait_ge(S["dve_xn"], SUB * b + s + 1)
            r = rows[b % 2][:, s, 0:D]
            nc.gpsimd.tensor_tensor(r, r, b2bc[:], ALU.add).then_inc(S["pool_xb"], 1)

        def pe_q(pe, b, m):
            p = own_bank(pe, "Q", b, m)
            if b == 0:
                pe.wait_ge(S["dve_wq"], 1)
            pe.wait_ge(S["dve_xT"], SUB * (b + 1))
            for k in range(KD):
                for j, (w, a) in enumerate(split3([wq[:, h, k, P * m:P * m + P] for h in range(2)],
                                                  [actA[:, h, k, :] for h in range(2)])):
                    mm = pe.matmul(p[:], w, a, start=k == 0 and j == 0, stop=k == KD - 1 and j == 2)
            mm.then_inc(S["pe_q"], 1)

        def act_q(act, b, m):
            act.wait_ge(S["pe_q"], KD * b + m + 1)
            if b >= 2:
                act.wait_ge(S["pe_l"], b - 1)
            act.activation(actQ[:, 0, m, :], of("Q", b, m)[:], ACT.Identity, bias=bq[:, m:m + 1]
                           ).then_inc(S["act_q"], 1)

        def dve_q(dve, b, m):
            dve.wait_ge(S["act_q"], KD * b + m + 1)
            dve.scalar_tensor_tensor(actQ[:, 1, m, :], of("Q", b, m)[:], bq[:, m:m + 1], f32(actQ[:, 0, m, :]),
                                     ALU.add, ALU.subtract).then_inc(S["dve_q"], 1)

        def pe_s(pe, b, g, s):
            p = own_bank(pe, "S", b, g, s)
            if s == 0:
                pe.wait_ge(S["dve_q"], KD * b + g + 1)
                pe.wait_ge(ld_k, 16 * KLOADS * (b // BPB + 1))
            for j, (q, k) in enumerate(split3([actQ[:, h, g, P * s:P * s + P] for h in range(2)],
                                              [kbd[:, h, g, :] for h in range(2)])):
                mm = pe.matmul(p[:, 0:SC], q, k, start=j == 0, stop=j == 2)
            mm.then_inc(S["pe_s"], 1)

        def dve_s(dve, b, g, s):
            dve.wait_ge(S["pe_s"], SUB * (KD * b + g) + s + 1)
            p = grouped(of("S", b, g, s)[:, 0:SC], HG)
            dve.tensor_reduce(mx[:, SUB * g + s, :], p, AX, ALU.max).then_inc(S["dve_max"], 1)
            if s:
                dve_sub(dve, b, g, s - 1)
            if s == SUB - 1:
                drip(1)
                dve_sub(dve, b, g, s)

        def dve_sub(dve, b, g, s):
            if b and s == 0:
                dve.wait_ge(S["pe_pt"], NC * KD * b)
            dve.wait_ge(S["dve_max"], SUB * (KD * b + g) + s + 1)
            dve.tensor_tensor(grouped(E[:, g, s, :], HG), grouped(of("S", b, g, s)[:, 0:SC], HG),
                              spread(mx[:, SUB * g + s, :], M), ALU.subtract).then_inc(S["dve_sub"], 1)

        def act_soft(act, b, g):
            act.wait_ge(S["dve_sub"], SUB * (KD * b + g + 1))
            act.activation(E[:, g], E[:, g], ACT.Exp, scale=SCALE).then_inc(S["act_exp"], 1)

        def dve_sum(dve, b, g):
            i = KD * b + g
            dve.wait_ge(S["act_exp"], i + 1)
            if i >= KD:
                dve.wait_ge(S["pool_p"], i - KD + 1)
            n = issued(dve.tensor_reduce(sm[:, g, :], grouped(E[:, g].rearrange("p s c -> p (s c)"), SUB * HG), AX,
                                         ALU.add))
            drip(1)
            dve.wait_ge(dve_chain, n)
            dve.reciprocal(rc[:, g, :], sm[:, g, :]).then_inc(S["dve_rc"], 1)

        def pool_soft(pool, b, g):
            pool.wait_ge(S["dve_rc"], KD * b + g + 1)
            e = grouped(E[:, g].rearrange("p s c -> p (s c)"), SUB * HG)
            nc.gpsimd.tensor_tensor(e, e, spread(rc[:, g, :], M), ALU.mult).then_inc(S["pool_p"], 1)

        def pe_pt(pe, b, g, c):
            p = own_bank(pe, "PT", b, g, c)
            pe.wait_ge(S["pool_p"], KD * b + g + 1)
            for s in range(SUB):
                mm = pe.transpose(p[0:CH[c], P * s:P * s + P], E[:, g, s, CO[c]:CO[c] + CH[c]], ident[:])
            mm.then_inc(S["pe_pt"], 1)

        def act_pt(act, b, g, c):
            j = NC * g + c
            if b == 0 and j == 0:
                act.wait_ge(S["dve_w1"], 1)
                act.wait_ge(S["dve_w2a"], 1)
                act.wait_ge(S["dve_wq"], 1)
            if j >= SLOTS:
                act.wait_ge(S["pe_av"], KD * b + (j - SLOTS) // NC + 1)
            act.wait_ge(S["pe_pt"], NC * KD * b + j + 1)
            act.activation(actH[0:CH[c], 0, j % SLOTS, :], of("PT", b, g, c)[0:CH[c], :], ACT.Identity
                           ).then_inc(S["act_pt"], 1)

        def dve_pt(dve, b, g, c):
            j = NC * g + c
            dve.wait_ge(S["act_pt"], NC * KD * b + j + 1)
            dve.tensor_tensor(actH[0:CH[c], 1, j % SLOTS, :], of("PT", b, g, c)[0:CH[c], :],
                              f32(actH[0:CH[c], 0, j % SLOTS, :]), ALU.subtract).then_inc(S["dve_pt"], 1)

        def pe_av(pe, b, g):
            p = own_bank(pe, "AV", b, g)
            pe.wait_ge(ld_v, 16 * VLOADS * (b // BPB + 1))
            for c in range(NC):
                j = NC * g + c
                pe.wait_ge(S["dve_pt"], NC * KD * b + j + 1)
                for i, (v, w) in enumerate(split3([vbd[0:CH[c], h, g, c, :] for h in range(2)],
                                                  [actH[0:CH[c], h, j % SLOTS, :] for h in range(2)])):
                    mm = pe.matmul(p[:], v, w, start=c == 0 and i == 0, stop=c == NC - 1 and i == 2)
            mm.then_inc(S["pe_av"], 1)

        def act_av(act, b, g):
            act.wait_ge(S["pe_av"], KD * b + g + 1)
            act.activation(actA[:, 0, g, :], of("AV", b, g)[:], ACT.Identity).then_inc(S["act_o"], 1)

        def dve_av(dve, b, g):
            dve.wait_ge(S["act_o"], KD * b + g + 1)
            dve.tensor_tensor(actA[:, 1, g, :], of("AV", b, g)[:], f32(actA[:, 0, g, :]), ALU.subtract
                              ).then_inc(S["dve_o"], 1)

        def pe_h(pe, b, m):
            p = own_bank(pe, "H", b, m)
            if b == 0:
                pe.wait_ge(S["dve_w1"], 1)
            for k in range(KD):
                pe.wait_ge(S["dve_o"], KD * b + k + 1)
                for j, (w, a) in enumerate(split3([w1[:, h, k, P * m:P * m + P] for h in range(2)],
                                                  [actA[:, h, k, :] for h in range(2)])):
                    mm = pe.matmul(p[:], w, a, start=k == 0 and j == 0, stop=k == KD - 1 and j == 2)
            mm.then_inc(S["pe_h"], 1)

        def act_h(act, b, m):
            i = MF * b + m
            act.wait_ge(S["pe_h"], i + 1)
            if i >= 2:
                act.wait_ge(S["dve_h"], i - 1)
            act.activation(htmp[m % 2][:], of("H", b, m)[:], ACT.Relu, bias=b1[:, m:m + 1]).then_inc(S["act_h"], 1)
            act.activation(actH[:, 0, m, :], of("H", b, m)[:], ACT.Relu, bias=b1[:, m:m + 1]).then_inc(S["act_hh"], 1)

        def dve_h(dve, b, m):
            dve.wait_ge(S["act_hh"], MF * b + m + 1)
            dve.tensor_tensor(actH[:, 1, m, :], htmp[m % 2][:], f32(actH[:, 0, m, :]), ALU.subtract
                              ).then_inc(S["dve_h"], 1)

        def pe_y(pe, b, s):
            p = own_bank(pe, "Y", b, s)
            if b == 0:
                pe.wait_ge(S["dve_w2a"], 1)
                pe.wait_ge(S["dve_w2b"], 1)
            for m in range(MF):
                pe.wait_ge(S["dve_h"], MF * b + m + 1)
                for j, (a, w) in enumerate(split3([actH[:, h, m, P * s:P * s + P] for h in range(2)],
                                                  [w2[:, h, m, :] for h in range(2)])):
                    mm = pe.matmul(p[:], a, w, start=m == 0 and j == 0, stop=m == MF - 1 and j == 2)
            mm.then_inc(S["pe_y"], 1)

        bn2_done = {}

        def dve_y(dve, b, s):
            dve.wait_ge(S["pe_y"], SUB * b + s + 1)
            dve.wait_ge(S["pool_xb"], SUB * b + s + 1)
            r = rows[b % 2][:, s, 0:D]
            dve.tensor_tensor(r, of("Y", b, s)[:], r, ALU.add).then_inc(S["dve_x2"], 1)

            def chain():
                dve.wait_ge(S["dve_x2"], SUB * b + s + 1)
                bn2_done[b] = issued(dve.bn_stats(bn2[:, s, :], r))
                yield
            chains.append(chain())

        def dve_x2stat(dve, b):
            def chain():
                n = yield from aggregate(dve, bn2, mv, bn2_done[b])
                n = yield from rsqrt(dve, mv[:, :, 1], r1[:], n)
                dve.wait_ge(dve_chain, n)
                dve.scalar_tensor_tensor(nmr[:], mv[:, :, 0], -1.0, r1[:], ALU.mult, ALU.mult
                                         ).then_inc(S["dve_s2"], 1)
                yield
            if bn2_done.get(b) is None:
                drain()
            chains.append(chain())

        def act_x2stat(act, b):
            act.wait_ge(S["dve_s2"], b + 1)
            if b + 1 < NBLK:
                act.wait_ge(S["pe_pt"], NC * KD * (b + 2))
            for s in range(SUB):
                act.activation(xt(s), rows[b % 2][:, s, 0:D], ACT.Identity, bias=nmr[:, s:s + 1],
                               scale=r1[:, s:s + 1]).then_inc(S["act_xt"], 1)

        def pe_tt(pe, b, s):
            p = own_bank(pe, "TT", b, s)
            pe.wait_ge(S["act_xt"], SUB * b + s + 1)
            for k in range(KD):
                mm = pe.transpose(p[:, P * k:P * k + P], xt(s)[:, P * k:P * k + P], ident[:])
            mm.then_inc(S["pe_tt"], 1)

        def act_tt(act, b, s):
            act.wait_ge(S["pe_tt"], SUB * b + s + 1)
            act.activation(actQ[:, 0, :, P * s:P * s + P], of("TT", b, s)[:].rearrange("p (k t) -> p k t", k=KD),
                           ACT.Identity).then_inc(S["act_tt"], 1)

        def dve_tt(dve, b, s):
            dve.wait_ge(S["act_tt"], SUB * b + s + 1)
            dve.tensor_tensor(actQ[:, 1, :, P * s:P * s + P], of("TT", b, s)[:].rearrange("p (k t) -> p k t", k=KD),
                              f32(actQ[:, 0, :, P * s:P * s + P]), ALU.subtract).then_inc(S["dve_tt"], 1)

        def dve_rowtail(dve, b):
            def chain():
                for s in range(SUB):
                    dve.wait_ge(S["act_xt"], SUB * b + s + 1)
                    n = issued(dve.bn_stats(bn[:, s, :], xt(s)))
                    yield
                n = yield from aggregate(dve, bn, mv, n)
                n = yield from rsqrt(dve, mv[:, :, 1], r2[:], n)
                r = rows[b % 2]
                dve.wait_ge(dve_chain, n)
                dve.tensor_tensor(r[:, :, D], r1[:], r2[:], ALU.mult)
                n = issued(dve.tensor_tensor(tB[:], nmr[:], mv[:, :, 0], ALU.subtract))
                yield
                dve.wait_ge(dve_chain, n)
                dve.tensor_tensor(r[:, :, D + 1], tB[:], r2[:], ALU.mult)
                dve.tensor_copy(r[:, :, D + 2].bitcast(U32), ids[:, SUB * b:SUB * b + SUB]).then_inc(S["dve_row"], 1)
                yield
            chains.append(chain())

        def pe_l(pe, b):
            p = own_bank(pe, "L", b)
            if b == 0:
                pe.wait_ge(S["dve_const"], 1)
            pe.wait_ge(S["dve_tt"], SUB * (b + 1))
            for k in range(KD):
                for j, (w, a) in enumerate(split3([wg[:, h, k, :] for h in range(2)],
                                                  [actQ[:, h, k, :] for h in range(2)])):
                    mm = pe.matmul(p[0:NE, :], w, a, start=k == 0 and j == 0, stop=k == KD - 1 and j == 2)
            mm.then_inc(S["pe_l"], 1)

        def act_l(act, b):
            act.wait_ge(S["pe_l"], b + 1)
            act.activation(lgT, of("L", b)[0:NE, :], ACT.Identity).then_inc(S["act_l"], 1)

        def pe_lt(pe, b):
            p = own_bank(pe, "LT", b)
            pe.wait_ge(S["act_l"], b + 1)
            for s in range(SUB):
                mm = pe.transpose(p[:, NE * s:NE * s + NE], lgT[:, P * s:P * s + P], ident[0:NE, 0:NE])
            mm.then_inc(S["pe_lt"], 1)

        def dve_lt(dve, b):
            dve.wait_ge(S["pe_lt"], b + 1)
            dve.tensor_copy(lg[:], of("LT", b)[:, 0:SUB * NE].rearrange("p (s e) -> p s e", e=NE)
                            ).then_inc(S["dve_lg"], 1)
            drip(1)
            dve.wait_ge(S["dve_lg"], b + 1)
            for f in (lambda: dve.tensor_reduce(lm[:], lg[:], AX, ALU.max),
                      lambda: dve.tensor_tensor(lw[:], lg[:], spread(lm[:], NE), ALU.is_equal),
                      lambda: dve.tensor_tensor(lw[:], lw[:], prio[:], ALU.mult),
                      lambda: dve.tensor_reduce(lm[:], lw[:], AX, ALU.max)):
                n = issued(f())
                drip(1)
                dve.wait_ge(dve_chain, n)
            dve.tensor_tensor(oh[:], prio[:], spread(lm[:], NE), ALU.is_equal).then_inc(S["dve_oh"], 1)

        def pe_rk(pe, b):
            p = own_bank(pe, "RK", b)
            w = SUB * NE
            pe.wait_ge(S["dve_oh"], b + 1)
            if b:
                pe.wait_ge(S["dve_cum"], b)
            o_ = oh[:].rearrange("p s e -> p (s e)")
            pe.matmul(p[:, 0:w], tri[:], o_, start=True, stop=False)
            for s in range(1, SUB):
                pe.matmul(p[:, NE * s:w], ones[:], o_[:, 0:w - NE * s], start=False, stop=False)
            for s in range(SUB):
                mm = pe.matmul(p[:, NE * s:NE * s + NE], ones[:], cum[:], start=False, stop=s == SUB - 1)
            mm.then_inc(S["pe_rk"], 1)

        def dve_rk(dve, b):
            dve.wait_ge(S["pe_rk"], b + 1)
            if b >= 2:
                dve.wait_ge(scat[b % 2], 16 * SUB * (b // 2))
            dve.tensor_tensor(rk[:], of("RK", b)[:, 0:SUB * NE].rearrange("p (s e) -> p s e", e=NE), base[:], ALU.add
                              ).then_inc(S["dve_rk"], 1)
            n1 = issued(dve.tensor_reduce(lw[:, 0, :], oh[:].rearrange("p s e -> p e s"), AX, ALU.add))
            dve.wait_ge(S["dve_rk"], b + 1)
            n2 = issued(dve.tensor_tensor(rk[:], rk[:], oh[:], ALU.mult))
            dve.wait_ge(dve_chain, n1)
            dve.tensor_tensor(cum[:], cum[:], lw[:, 0, :], ALU.add).then_inc(S["dve_cum"], 1)
            dve.wait_ge(dve_chain, n2)
            n3 = issued(dve.tensor_reduce(posf[:], rk[:], AX, ALU.add))
            drip(1)
            dve.wait_ge(dve_chain, n3)
            dve.tensor_copy(pos[b % 2][:], posf[:]).then_inc(S["dve_pos"], 1)

        def pool_scat(pool, b):
            pool.wait_ge(S["dve_pos"], b + 1)
            pool.wait_ge(S["dve_row"], b + 1)
            for s in range(SUB):
                nc.gpsimd.indirect_dma_start(
                    out=region, out_offset=bass.IndirectOffsetOnAxis(ap=pos[b % 2][:, s:s + 1], axis=0),
                    in_=rows[b % 2][:, s, :], in_offset=None).then_inc(scat[b % 2], 16)

        def pe_b1(pe):
            own_bank(pe, "B1")
            for e in range(NE):
                pe.wait_ge(S["dve_b1"], 0)
            pe.wait_ge(S["dve_e1"], 1)
            for e in range(NE):
                p = bank[bank_of[("B1",)][e // 4]]
                for k in range(KD):
                    mm = pe.matmul(p[:, EH * (e % 4):EH * (e % 4) + EH], lnb[:, k, e:e + 1].to_broadcast([P, P]),
                                   e1[:, k, e, :], start=k == 0, stop=k == KD - 1)
            mm.then_inc(S["pe_b1"], 1)

        def dve_b1(dve):
            dve.wait_ge(L["ln"], 32)
            dve.wait_ge(L["e1"], 16)
            dve.tensor_copy(lnbb[:], lnb[:, 0, 0:1].to_broadcast([P, P])).then_inc(S["dve_e1"], 1)
            dve.wait_ge(S["pe_b1"], 1)
            dve.wait_ge(L["eb"], 32)
            for j in range(2):
                t = b1e[:, 4 * j:4 * j + 4, :].rearrange("p e h -> p (e h)")
                ins = dve.tensor_tensor(t, bank[bank_of[("B1",)][j]][:], t, ALU.add)
            ins.then_inc(S["dve_b1"], 1)
            for k in range(KD):
                ins = dve.tensor_tensor(e1[:, k], e1[:, k], spread(lns[:, k, :], EH), ALU.mult)
            ins.then_inc(S["dve_e1"], 1)

        def act_e2conv(act):
            act.wait_ge(S["pe_h"], MF * NBLK)
            act.wait_ge(L["e2"], 16)
            act.activation(e2[:, 0], e2_raw[:], ACT.Identity).then_inc(S["act_e2"], 1)

        def dve_e2conv(dve):
            dve.wait_ge(S["act_e2"], 1)
            dve.tensor_tensor(e2[:, 1], e2_raw[:], f32(e2[:, 0]), ALU.subtract).then_inc(S["dve_e2"], 1)

        def pe_table(pe):
            p = own_bank(pe, "TABLE")
            pe.wait_ge(S["dve_cum"], NBLK)
            pe.matmul(p[:, 0:NE], ones[:], cum[:], start=True, stop=True).then_inc(S["pe_cnt"], 1)

        def dve_table(dve):
            dve.wait_ge(S["pe_cnt"], 1)
            dve.wait_ge(L["tab"], 48)
            dve_link(dve, dve.tensor_copy(cnt[:], of("TABLE")[:, 0:NE]))
            dve_link(dve, dve.tensor_tensor(padf[:], padoff[:], cnt[:], ALU.add))
            dve.tensor_copy(padu[:], padf[:]).then_inc(S["dve_pad"], 1)
            dve_link(dve, dve.tensor_scalar(cti[:], cnt[:], float(P - 1), None, ALU.add))
            dve_link(dve, dve.tensor_scalar(cti[:], cti[:], 7, None, ALU.logical_shift_right))
            dve_link(dve, dve.tensor_copy(ctl[:], cti[:]))
            dve.tensor_scalar(stp[:], ctl[:], -float(P), float(REG), ALU.mult, ALU.add)
            dve_link(dve, dve.tensor_copy(cinc[:], ctl[:]))
            for e in range(1, NE):
                dve_link(dve, dve.tensor_tensor(cinc[:, e:e + 1], cinc[:, e:e + 1], cinc[:, e - 1:e], ALU.add))
            bc = lambda t: t[0:1, :].unsqueeze(1).to_broadcast([1, NT, NE])
            dve_link(dve, dve.tensor_tensor(ge[:], jt[:], bc(cinc), ALU.is_ge))
            dve_link(dve, dve.tensor_reduce(ex[:], ge[:], AX, ALU.add))
            dve_link(dve, dve.tensor_scalar(exi[:], ex[:], float(NE - 1), None, ALU.min))
            dve_link(dve, dve.tensor_tensor(ge[:], ge[:], bc(stp), ALU.mult))
            dve_link(dve, dve.tensor_reduce(rw[:], ge[:], AX, ALU.add))
            dve_link(dve, dve.scalar_tensor_tensor(rw[:], jt[:, :, 0], float(P), rw[:], ALU.mult, ALU.add))
            dve.tensor_scalar(rwi[:], rw[:], float(NE * REG), None, ALU.min).then_inc(S["dve_tab"], 1)

        def pool_table(pool):
            pool.wait_ge(S["dve_pad"], 1)
            for e in range(NE):
                nc.gpsimd.indirect_dma_start(
                    out=region, out_offset=bass.IndirectOffsetOnAxis(ap=padu[:, e:e + 1], axis=0),
                    in_=padrow[:], in_offset=None).then_inc(st_pad, 16)

        regs = {}

        def load_reg(eng, name, ap, hi):
            if name not in regs:
                regs[name] = eng.alloc_register(name)
                eng.wait_ge(S["dve_tab"], 1)
            eng.reg_load(regs[name], ap)
            return eng.snap(regs[name], min_val=0, max_val=hi)

        def expert(eng, who, t):
            return load_reg(eng, f"expert_{who}", exi[0:1, t:t + 1], NE - 1)

        def pick(ap, e):
            return ap[:, bass.ds(e, 1), :].rearrange("p e n -> p (e n)")

        def sp_bload(sp, t):
            if t == 0:
                for i in range(2):
                    sp.wait_ge(scat[i], 16 * SUB * (NBLK // 2))
                sp.wait_ge(st_pad, 16 * NE)
                sp.wait_ge(L["pad0"], 16)
                sp.wait_ge(S["pe_y"], SUB * NBLK)
            if t >= NROW:
                sp.wait_ge(st_out[t % NROW], 16 * (t // NROW))
            r = load_reg(sp, "row", rwi[0:1, t:t + 1], NE * REG)
            sp.dma_start(rowB[t % NROW][:], region[bass.ds(r, P), :]).then_inc(ld_row[t % NROW], 16)

        def dve_bx(dve, t):
            r = rowB[t % NROW]
            dve.wait_ge(ld_row[t % NROW], 16 * (t // NROW + 1))
            if t >= 2:
                dve.wait_ge(S["b_xT"], t - 1)
            dve.tensor_scalar(xh[t % 2][:], r[:, 0:D], r[:, D:D + 1], r[:, D + 1:D + 2], ALU.mult, ALU.add
                              ).then_inc(S["b_xh"], 1)

        def add_b2(eng, who, t):
            eng.wait_ge(S["b_xh"], t + 1)
            if t < 2:
                eng.wait_ge(L["eb"], 32)
            r = rowB[t % NROW][:, 0:D]
            eng.tensor_tensor(r, r, pick(b2e, expert(eng, who, t)), ALU.add).then_inc(b_xb[t % 2], 1)

        def pool_bx(pool, t):
            if t % 2 == 0:
                add_b2(pool, "pool", t)

        def pe_bx(pe, t):
            p = own_bank(pe, "B_XT", t)
            pe.wait_ge(S["b_xh"], t + 1)
            for k in range(KD):
                mm = pe.transpose(p[:, P * k:P * k + P], xh[t % 2][:, P * k:P * k + P], ident[:])
            mm.then_inc(S["b_xT"], 1)

        def act_bx(act, t):
            act.wait_ge(S["b_xT"], t + 1)
            if t >= 2:
                act.wait_ge(S["b_h"], t - 1)
            act.activation(xhT[t % 2][:], of("B_XT", t)[:].rearrange("p (k t) -> p k t", k=KD), ACT.Identity
                           ).then_inc(S["b_xTs"], 1)

        def pe_bh(pe, t):
            p = own_bank(pe, "B_H", t)
            pe.wait_ge(S["b_xTs"], t + 1)
            if t == 0:
                pe.wait_ge(S["dve_e1"], 2)
            e = expert(pe, "pe1", t)
            for k in range(KD):
                mm = pe.matmul(p[:, 0:EH], xhT[t % 2][:, k, :], pick(e1[:, k], e), start=k == 0, stop=k == KD - 1)
            mm.then_inc(S["b_h"], 1)

        def dve_bh(dve, t):
            dve.wait_ge(S["b_h"], t + 1)
            if t >= 2:
                dve.wait_ge(S["b_gl"], t - 1)
            dve.tensor_tensor(hb[t % 2][:], of("B_H", t)[:, 0:EH], pick(b1e, expert(dve, "dve", t)), ALU.add
                              ).then_inc(S["b_hb"], 1)
            if t % 2:
                add_b2(dve, "dve", t)

        def act_bh(act, t):
            act.wait_ge(S["b_hb"], t + 1)
            if t >= 2:
                act.wait_ge(S["b_g"], t - 1)
            act.activation(gl[t % 2][:], hb[t % 2][:], ACT.Gelu).then_inc(S["b_gl"], 1)

        def pe_bg(pe, t):
            p = own_bank(pe, "B_G", t)
            pe.wait_ge(S["b_gl"], t + 1)
            pe.transpose(p[:, 0:P], gl[t % 2][:], ident[:]).then_inc(S["b_g"], 1)

        def act_bg(act, t):
            act.wait_ge(S["b_g"], t + 1)
            if t >= 2:
                act.wait_ge(S["b_y"], t - 1)
            act.activation(gT[t % 2][:, 0, :], of("B_G", t)[:, 0:P], ACT.Identity).then_inc(S["b_ghi"], 1)

        def dve_bg(dve, t):
            dve.wait_ge(S["b_ghi"], t + 1)
            dve.tensor_tensor(gT[t % 2][:, 1, :], of("B_G", t)[:, 0:P], f32(gT[t % 2][:, 0, :]), ALU.subtract
                              ).then_inc(S["b_glo"], 1)

        def pe_by(pe, t):
            p = own_bank(pe, "B_Y", t)
            pe.wait_ge(S["b_glo"], t + 1)
            if t == 0:
                pe.wait_ge(S["dve_e2"], 1)
            e = expert(pe, "pe2", t)
            for j, (g, w) in enumerate(split3([gT[t % 2][:, h, :] for h in range(2)],
                                              [pick(e2[:, h], e) for h in range(2)])):
                mm = pe.matmul(p[:], g, w, start=j == 0, stop=j == 2)
            mm.then_inc(S["b_y"], 1)

        def dve_by(dve, t):
            dve.wait_ge(S["b_y"], t + 1)
            dve.wait_ge(b_xb[t % 2], t // 2 + 1)
            r = rowB[t % NROW][:, 0:D]
            dve.tensor_tensor(r, of("B_Y", t)[:], r, ALU.add).then_inc(S["b_out"], 1)

        def pool_by(pool, t):
            pool.wait_ge(S["b_out"], t + 1)
            r = rowB[t % NROW]
            nc.gpsimd.indirect_dma_start(
                out=out, out_offset=bass.IndirectOffsetOnAxis(ap=r[:, D + 2:D + 3].bitcast(U32), axis=0),
                in_=r[:, 0:D], in_offset=None, bounds_check=N - 1, oob_is_err=False).then_inc(st_out[t % NROW], 16)

        parts = {
            "SETUP": {"sp": sp_setup, "pool": pool_setup, "dve": dve_setup},
            "XLOAD": {"sp": sp_xload},
            "KP": {"pe": pe_kp, "act": act_kp, "dve": dve_kp},
            "KSTORE": {"sp": sp_kstore},
            "CONV_WQ": {"act": act_conv_wq, "dve": dve_conv_wq},
            "CONV_W12": {"act": act_conv_w12, "dve": dve_conv_w12, "pool": pool_conv_w12},
            "KLOAD": {"sp": sp_kload},
            "VP": {"pe": pe_vp, "dve": dve_vp, "act": act_vp, "sp": sp_vstore},
            "VLOAD": {"sp": sp_vload},
            "XSTAT": {"dve": dve_xstat},
            "XT": {"pe": pe_xT, "act": act_xT, "dve": dve_xT, "pool": pool_xT},
            "Q": {"pe": pe_q, "act": act_q, "dve": dve_q},
            "S": {"pe": pe_s, "dve": dve_s},
            "EXP": {"act": act_soft},
            "SUM": {"dve": dve_sum, "pool": pool_soft},
            "PT": {"pe": pe_pt, "act": act_pt, "dve": dve_pt},
            "AV": {"pe": pe_av, "act": act_av, "dve": dve_av},
            "H": {"pe": pe_h, "act": act_h, "dve": dve_h},
            "Y": {"pe": pe_y, "dve": dve_y},
            "X2STAT": {"dve": dve_x2stat},
            "XTT": {"act": act_x2stat},
            "TT": {"pe": pe_tt, "act": act_tt, "dve": dve_tt},
            "L": {"pe": pe_l, "act": act_l},
            "ROWTAIL": {"dve": dve_rowtail},
            "DRAIN": {"dve": lambda dve: drain()},
            "LT": {"pe": pe_lt, "dve": dve_lt},
            "RK": {"pe": pe_rk, "dve": dve_rk},
            "SCAT": {"pool": pool_scat},
            "E1_LOAD": {"sp": sp_e1load},
            "EB_LOAD": {"sp": sp_ebload},
            "E2_LOAD": {"sp": sp_e2load},
            "E2_CONV": {"act": act_e2conv, "dve": dve_e2conv},
            "B1": {"pe": pe_b1, "dve": dve_b1},
            "TABLE": {"pe": pe_table, "dve": dve_table, "pool": pool_table},
            "B_XT": {"sp": sp_bload, "dve": dve_bx, "pool": pool_bx, "pe": pe_bx, "act": act_bx},
            "B_H": {"pe": pe_bh, "dve": dve_bh, "act": act_bh},
            "B_G": {"pe": pe_bg, "act": act_bg, "dve": dve_bg},
            "B_Y": {"pe": pe_by, "dve": dve_by, "pool": pool_by},
        }

        def walk(eng, who):
            for kind, *i in sched:
                if who in parts[kind]:
                    parts[kind][who](eng, *i)
                if who == "dve":
                    drip(DRIP.get(kind, 0))

        block = ctx.enter_context(nc.Block())

        @block.sync
        def _(sp):
            walk(sp, "sp")
            for i in range(NROW):
                sp.wait_ge(st_out[i], 16 * len(range(i, NT, NROW)))

        @block.gpsimd
        def _(pool):
            walk(pool, "pool")

        @block.scalar
        def _(act):
            walk(act, "act")

        @block.vector
        def _(dve):
            walk(dve, "dve")

        @block.tensor
        def _(pe):
            walk(pe, "pe")


def kernel(**inputs):
    import numpy as np
    import concourse.bacc as _bacc
    from concourse import mybir as _mybir
    from concourse.bass_utils import run_bass_kernel_spmd as _run

    a = {k: np.asarray(v) for k, v in inputs.items()}

    def chunks(w, k):
        return w.reshape(k, P, -1).transpose(1, 0, 2)

    p = np.arange(P)
    f = np.float32
    dev = {
        "x": a["x"].reshape(N, D),
        "ctxT": chunks(a["ctx_768"].transpose(2, 0, 1).reshape(TD, NB * M), KT),
        "Wq": chunks(a["L0_xattn_Wq"], KD).reshape(P, -1),
        "Wk": chunks(a["L0_xattn_Wk"], KT),
        "Wv": chunks(a["L0_xattn_Wv"], KT),
        "W1": chunks(a["L0_xattn_W1"], KD).reshape(P, -1),
        "W2": chunks(a["L0_xattn_W2"], MF).reshape(P, -1),
        "bq": a["L0_xattn_bq"].reshape(KD, P).T,
        "bk": a["L0_xattn_bk"].reshape(KD, P).T,
        "bv": a["L0_xattn_bv"].reshape(1, D),
        "b1": a["L0_xattn_b1"].reshape(MF, P).T,
        "b2": a["L0_xattn_b2"].reshape(1, D),
        "WgT": chunks(a["L0_ffn_Wg"].T, KD).reshape(P, -1),
        "lns": chunks(a["L0_ffn_ln_scale"].T, KD),
        "lnb": chunks(a["L0_ffn_ln_bias"].T, KD),
        "E1": a["L0_ffn_W1"].reshape(NE, KD, P, EH).transpose(2, 1, 0, 3),
        "Eb1": a["L0_ffn_b1"].reshape(1, NE, EH),
        "E2": a["L0_ffn_W2"].transpose(1, 0, 2),
        "Eb2": a["L0_ffn_b2"].reshape(1, NE, D),
        "ident": np.eye(P, dtype=f),
        "masks": np.concatenate([(p[:, None] < p[None, :]).astype(f), np.ones((P, P), f)], 1),
        "prio": np.broadcast_to((NE - np.arange(NE)).astype(f), (P, SUB, NE)),
        "base": np.broadcast_to((REG * np.arange(NE)).astype(f), (P, SUB, NE)),
        "ids": (p[:, None] + P * np.arange(N // P)[None, :]).astype(np.uint32),
        "padoff": (p[:, None] + REG * np.arange(NE)[None, :]).astype(f),
        "jt": np.broadcast_to(np.arange(NT, dtype=f)[None, :, None], (1, NT, NE)),
    }
    pad = np.zeros((P, ROW), f)
    pad[:, D + 2] = np.full(P, N, np.uint32).view(f)
    dev["padrow"] = pad
    dev = {k: np.ascontiguousarray(v) for k, v in dev.items()}

    nc = _bacc.Bacc("TRN2", target_bir_lowering=False, num_devices=1, dynamic_dma_scratch_size=8192)
    A = {k: nc.dram_tensor(f"in_{k}", v.shape, _mybir.dt.from_np(v.dtype), kind="ExternalInput").ap()
         for k, v in dev.items()}
    out = nc.dram_tensor("out_0", (N, D), F32, kind="ExternalOutput").ap()
    xattn_moe_kernel(nc, A, out)
    r = _run(nc, [{f"in_{k}": v for k, v in dev.items()}], core_ids=[0])
    return r.results[0]["out_0"].reshape(NB, TOK, D)
```

```python
from contextlib import ExitStack

import concourse.bass as bass
from concourse import mybir

F32 = mybir.dt.float32
F32R = mybir.dt.float32r
BF16 = mybir.dt.bfloat16
U32 = mybir.dt.uint32
I32 = mybir.dt.int32
ALU = mybir.AluOpType
ACT = mybir.ActivationFunctionType
AX = mybir.AxisListType.X

P = 128
D = 512
KD = D // P
TD = 384
KT = TD // P
NB = 4
TOK = 2048
M = 77
HEADS = 16
HD = D // HEADS
HG = P // HD
SCALE = float(HD) ** -0.5
F = 1024
MF = F // P
NE = 8
EH = 128
EPS = 1e-5
N = NB * TOK
BLK = 512
SUB = BLK // P
NBLK = N // BLK
BPB = TOK // BLK
SC = HG * M
CH = [103, 103, 102]
CO = [0, 103, 206]
NC = len(CH)
SLOTS = 8
ROW = 516
REG = N + P
NT = N // P + NE - 1
NROW = 14
B2LO = 32
PIECES = []
for _h in range(HG):
    for _c in range(NC):
        _a, _z = max(M * _h, CO[_c]), min(M * _h + M, CO[_c] + CH[_c])
        if _a < _z:
            PIECES.append((_c, _a - CO[_c], _a - M * _h, _z - _a, _h))


def xattn_moe_kernel(nc, A, out):
    region = nc.dram_tensor("region", [NE * REG + P, ROW], F32).ap()
    k_parts = nc.dram_tensor("k_parts", [NB, 2, KD, P, M], F32).ap()
    v_parts = nc.dram_tensor("v_parts", [NB, 2, M, D], F32).ap()

    end = [nc.sbuf_base]

    def at(name, shape, dt, offset):
        return nc.alloc_sbuf_tensor_at(name, shape, dt, offset=offset)

    def size(shape, dt):
        n = 2 if dt == BF16 else 4
        for s in shape[1:]:
            n *= s
        return (n + 31) // 32 * 32

    def sb(name, shape, dt=F32):
        o = (end[0] + 31) // 32 * 32
        end[0] = o + size(shape, dt)
        return at(name, shape, dt, o), o

    wq, wq_at = sb("wq", [P, 2, KD, D], F32R)
    w1, w1_at = sb("w1", [P, 2, KD, F], F32R)
    w2, w2_at = sb("w2", [P, 2, MF, D], F32R)
    wg, _ = sb("wg", [P, 2, KD, NE], F32R)
    kbd, kbd_at = sb("kbd", [P, 2, KD, SC], F32R)
    vbd, _ = sb("vbd", [P, 2, KD, NC, P], F32R)
    rows = [sb(f"rows{i}", [P, SUB, ROW]) for i in range(2)]
    rows_at = [r[1] for r in rows]
    rows = [r[0] for r in rows]
    actA, actA_at = sb("actA", [P, 2, KD, BLK], F32R)
    actQ, _ = sb("actQ", [P, 2, KD, BLK], F32R)
    actH, actH_at = sb("actH", [P, 2, SLOTS, BLK], F32R)
    E, E_at = sb("E", [P, KD, SUB, SC])
    xn = [sb(f"xn{i}", [P, D]) for i in range(2)]
    xn_at = xn[0][1]
    xn = [t[0] for t in xn]
    htmp = [sb(f"htmp{i}", [P, BLK]) for i in range(2)]
    htmp_at = htmp[0][1]
    htmp = [t[0] for t in htmp]
    b2bc, _ = sb("b2bc", [P, D])
    ident, _ = sb("ident", [P, P])
    tri, _ = sb("tri", [P, P], BF16)
    ones, _ = sb("ones", [P, P], BF16)
    sel, _ = sb("sel", [B2LO + 1, P], F32R)
    prio, _ = sb("prio", [P, SUB, NE])
    base, _ = sb("base", [P, SUB, NE])
    ids, _ = sb("ids", [P, N // P], U32)
    bq, _ = sb("bq", [P, KD])
    bk, _ = sb("bk", [P, KD])
    bks, _ = sb("bks", [P, KD])
    b1, _ = sb("b1", [P, MF])
    mx, _ = sb("mx", [P, KD * SUB, HG])
    sm, _ = sb("sm", [P, KD, SUB * HG])
    rc, _ = sb("rc", [P, KD, SUB * HG])
    bn, _ = sb("bn", [P, SUB, 6])
    bn2, _ = sb("bn2", [P, SUB, 6])
    mv, _ = sb("mv", [P, SUB, 2])
    mvx, _ = sb("mvx", [P, SUB, 2])
    nw, _ = sb("nw", [P, 3, SUB])
    rx, _ = sb("rx", [P, SUB])
    r1, _ = sb("r1", [P, SUB])
    r2, _ = sb("r2", [P, SUB])
    nmr, _ = sb("nmr", [P, SUB])
    tB, _ = sb("tB", [P, SUB])
    lg, _ = sb("lg", [P, SUB, NE])
    lw, _ = sb("lw", [P, SUB, NE])
    lm, _ = sb("lm", [P, SUB])
    oh, _ = sb("oh", [P, SUB, NE], BF16)
    cum, _ = sb("cum", [P, NE], BF16)
    rk, _ = sb("rk", [P, SUB, NE])
    posf, _ = sb("posf", [P, SUB])
    pos = [sb(f"pos{i}", [P, SUB], U32)[0] for i in range(2)]
    assert end[0] <= nc.sbuf_usable_end, (end[0], nc.sbuf_usable_end)
    xt = lambda s: E[:, s, :, :].rearrange("p a c -> p (a c)")[:, 0:D]
    lgT = E[0:NE, 0, :, :].rearrange("p a c -> p (a c)")[:, D + 64:D + 64 + BLK]

    wk_raw = at("wk_raw", [P, KT, D], F32, E_at)
    wv_raw = at("wv_raw", [P, KT, D], F32, E_at + 4 * KT * D)
    ctxT = at("ctxT", [P, KT, NB * M], F32, E_at + 8 * KT * D)
    wq_raw = at("wq_raw", [P, KD * D], F32, actH_at)
    w1_raw = at("w1_raw", [P, KD * F], F32, actH_at + 4 * KD * D)
    w2_raw = [at("w2_raw0", [P, MF * D // 2], F32, actH_at + 4 * KD * D + 4 * KD * F),
              at("w2_raw1", [P, MF * D // 2], F32, rows_at[1])]
    c_raw = at("c_raw", [P, 3 * P], F32, actA_at)
    wg_raw = at("wg_raw", [P, KD * NE], F32, actA_at + 12 * P)
    k_hl = at("k_hl", [P, 2, KD, NB * M], F32R, w1_at)
    v_hl = [at(f"v_hl{i}", [M, 2, D], F32R, w1_at + size([P, 2, KD, NB * M], F32) + 8 * D * i) for i in range(2)]
    v_f = [at(f"v_f{i}", [M, D], F32, w1_at + size([P, 2, KD, NB * M], F32) + 16 * D + 4 * D * i) for i in range(2)]
    k_f = at("k_f", [P, KD, NB * M], F32, w1_at + size([P, 2, KD, NB * M], F32) + 28 * D)
    bvbc = at("bvbc", [M, D], F32, w1_at + size([P, 2, KD, NB * M], F32) + 24 * D)

    e1 = at("e1", [P, KD, NE, EH], F32, wq_at)
    e2_raw = at("e2_raw", [P, NE, D], F32, actA_at)
    e2 = at("e2", [P, 2, NE, D], F32R, w1_at)
    b2e_raw = at("b2e_raw", [B2LO + 1, NE, D], F32, wq_at)
    b2e = at("b2e", [B2LO + 1, NE, D], F32R, kbd_at)
    assert 4 * NE * D <= size([P, 2, KD, SC], F32) + size([P, 2, KD, NC, P], F32)
    o = [w2_at]

    def sb2(name, shape, dt=F32):
        o[0] += size(shape, dt)
        return at(name, shape, dt, o[0] - size(shape, dt))

    rowB = [sb2(f"rowB{i}", [P, ROW]) for i in range(NROW)]
    assert o[0] <= w2_at + size([P, 2, MF, D], F32)
    o[0] = E_at
    xh = [sb2(f"xh{i}", [P, D]) for i in range(2)]
    xhT = [sb2(f"xhT{i}", [P, KD, P]) for i in range(2)]
    gl = [sb2(f"gl{i}", [P, EH]) for i in range(2)]
    gT = [sb2(f"gT{i}", [P, 2, P], F32R) for i in range(2)]
    assert o[0] <= E_at + size([P, KD, SUB, SC], F32)
    o[0] = rows_at[0]
    lns = sb2("lns", [P, KD, NE])
    lnb = sb2("lnb", [P, KD, NE])
    b1e = sb2("b1e", [1, NE, EH])
    padrow = sb2("padrow", [P, ROW])
    padoff = sb2("padoff", [P, NE])
    padf = sb2("padf", [P, NE])
    padu = sb2("padu", [P, NE], U32)
    cnt = sb2("cnt", [P, NE])
    cti = sb2("cti", [P, NE], I32)
    ctl = sb2("ctl", [P, NE])
    cinc = sb2("cinc", [P, NE])
    stp = sb2("stp", [P, NE])
    ex = sb2("ex", [1, NT])
    rw = sb2("rw", [1, NT])
    exi = sb2("exi", [1, NT], I32)
    rwi = sb2("rwi", [1, NT], I32)
    assert o[0] <= rows_at[0] + size([P, SUB, ROW], F32)
    jt = at("jt", [1, NT, NE], F32, xn_at)
    ge = at("ge", [1, NT, NE], F32, htmp_at)

    with ExitStack() as ctx:
        bank = [ctx.enter_context(nc.psum_tensor(f"bank{i}", [P, 512], F32)) for i in range(8)]

        def sem(name):
            return ctx.enter_context(nc.semaphore(name))

        L = {n: sem(f"ld_{n}") for n in (
            "consts", "wk", "wv", "ctx", "wq", "w1", "w2a", "w2b", "e1", "e2", "b2e", "eb", "ln", "tab", "pad0")}
        ld_x = [[sem(f"ld_x{i}_{s}") for s in range(SUB)] for i in range(2)]
        st_k, st_v, ld_k, ld_v = sem("st_k"), sem("st_v0"), sem("ld_k"), sem("ld_v")
        st_vs = [st_v, sem("st_v1")]
        scat = [[sem(f"scat{i}_{s}") for s in range(SUB)] for i in range(2)]
        st_pad = sem("st_pad")
        ld_row = [sem(f"ld_row{i}") for i in range(NROW)]
        st_out = [sem(f"st_out{i}") for i in range(NROW)]
        dve_chain, act_chain, pool_chain = sem("dve_chain"), sem("act_chain"), sem("pool_chain")
        S = {n: sem(n) for n in (
            "dve_bks pe_k act_kf act_k dve_k pe_v dve_vf act_v dve_v pool_zero dve_const "
            "act_wq dve_wq act_w1 dve_w1 act_w2a dve_w2a act_w2b dve_w2b "
            "dve_xn pool_xb pe_xT act_xT dve_xT pe_q act_q dve_q pe_s dve_max dve_sub act_es act_exp dve_rc pool_p "
            "pe_pt act_pt dve_pt pe_av act_o dve_o pe_h act_h act_hh dve_h pe_y dve_x2 dve_s2 act_xt dve_row "
            "pe_tt act_tt dve_tt pe_l act_l pe_lt dve_lg dve_oh pe_rk dve_rk dve_cum dve_pos "
            "pe_cnt dve_pad dve_tab dve_e1 pe_b1 dve_b1 act_e2 dve_e2 act_b2 dve_b2 "
            "b_xh b_xT b_xTs b_h b_gl b_g b_ghi b_glo b_y b_out").split()}
        pe_k, pe_v = S["pe_k"], S["pe_v"]

        sched = []

        def step(kind, *i):
            sched.append((kind, *i))

        def attention_tail(b):
            for c in range(NC):
                step("PT", b, 0, c)
            step("SUM", b, KD - 1)
            if b:
                step("X2STAT", b - 1)
            for g in range(KD):
                if g + 1 < KD:
                    for c in range(NC):
                        step("PT", b, g + 1, c)
                if b and g == KD - 1:
                    for s in range(2):
                        step("XTT", b - 1, s)
                step("AV", b, g)

        step("SETUP")
        step("XLOAD", 0)
        for m in range(KD):
            step("KP", m)
        step("KSTORE")
        step("CONV_WQ")
        step("XSTAT", 0)
        for s in range(SUB):
            step("XT", 0, s)
        for m in range(KD):
            step("Q", 0, m)
        step("KLOAD", 0)
        for i in range(NB):
            step("VP", i)
        step("VLOAD", 0)
        for g in range(KD):
            for s in range(SUB):
                step("S", 0, g, s)
            step("EXP", 0, g)
            if g < KD - 1:
                step("SUM", 0, g)
        step("CONV_W12")
        step("XLOAD", 1)
        for b in range(NBLK):
            last = b == NBLK - 1
            if (b + 1) % BPB == 0 and not last:
                step("KLOAD", (b + 1) // BPB)
            attention_tail(b)
            if (b + 1) % BPB == 0 and not last:
                step("VLOAD", (b + 1) // BPB)
            if last:
                step("B2_CONV")
                step("E1_LOAD")
            for m in range(MF):
                if b and m == 0:
                    for s in range(2, SUB):
                        step("XTT", b - 1, s)
                    step("DRAIN")
                step("H", b, m)
                if not (b and m == 2):
                    step("HLO", b, m)
                if b and m == 0:
                    for s in range(SUB):
                        step("TT", b - 1, s)
                    step("ROWTAIL", b - 1)
                    step("DRIP", 2)
                if b and m == 1:
                    step("DRAIN")
                    step("L", b - 1)
                if b and m == 2:
                    step("LT", b - 1)
                    step("HLO", b, m)
                if b and m == 3:
                    step("RK", b - 1)
                    step("SCAT", b - 1)
                    if not last:
                        step("XLOAD", b + 1)
                if m == MF - 3 and not last:
                    step("XSTAT", b + 1)
                    step("DRIP", 3)
            if last:
                step("E2_LOAD")
                for s in range(SUB):
                    step("YA", b, s)
                    if s == SUB - 1:
                        step("E2_CONV")
                    step("Y", b, s)
            else:
                step("DRAIN")
                step("YA", b, 0)
                step("Y", b, 0)
                for s in range(2):
                    step("XT", b + 1, s)
                step("YA", b, 1)
                for s in range(2, SUB):
                    step("XT", b + 1, s)
                step("Y", b, 1)
                step("Q", b + 1, 0)
                step("Q", b + 1, 1)
                for g, (first, y) in enumerate((("YA", 2), ("Y", 2), ("YA", 3), ("Y", 3))):
                    for s in range(SUB):
                        step("S", b + 1, g, s)
                    step("EXP", b + 1, g)
                    if g:
                        step("SUM", b + 1, g - 1)
                    step(first, b, y)
                    if g + 2 < KD:
                        step("Q", b + 1, g + 2)
                if b + 2 == NBLK:
                    step("B2_LOAD")
        step("X2STAT", NBLK - 1)
        step("DRAIN")
        for s in range(SUB):
            step("XTT", NBLK - 1, s)
        for s in range(SUB):
            step("TT", NBLK - 1, s)
        step("ROWTAIL", NBLK - 1)
        step("B1")
        step("L", NBLK - 1)
        step("LT", NBLK - 1)
        step("RK", NBLK - 1)
        step("DRAIN")
        step("SCAT", NBLK - 1)
        step("TABLE")
        for t in range(-4, NT):
            for kind, ahead in (("B_X", 4), ("B_Y", 0), ("B_G", 1), ("B_H", 2), ("B_XT", 3)):
                if 0 <= t + ahead < NT:
                    step(kind, t + ahead)

        ON_ACT = (0, 1, 2)
        ON_DVE = tuple(g for g in range(KD) if g not in ON_ACT)

        def score_done(b, g, s):
            mine, name = (ON_ACT, "act_es") if g in ON_ACT else (ON_DVE, "dve_sub")
            return S[name], SUB * (len(mine) * b + mine.index(g)) + s + 1

        freed = {
            "KP": lambda m: (S["act_kf"], m + 1),
            "VP": lambda i: (S["dve_vf"], i + 1),
            "XT": lambda b, s: (S["dve_xT"], SUB * b + s + 1),
            "Q": lambda b, m: (S["dve_q"], KD * b + m + 1),
            "S": lambda b, g, s: score_done(b, g, s),
            "PT": lambda b, g, c: (S["dve_pt"], NC * (KD * b + g) + c + 1),
            "AV": lambda b, g: (S["dve_o"], KD * b + g + 1),
            "H": lambda b, m: (S["act_hh"], MF * b + m + 1),
            "YA": lambda b, s: (S["dve_x2"], SUB * b + s + 1),
            "TT": lambda b, s: (S["dve_tt"], SUB * b + s + 1),
            "L": lambda b: (S["act_l"], b + 1),
            "LT": lambda b: (S["dve_lg"], b + 1),
            "RK": lambda b: (S["dve_rk"], b + 1),
            "TABLE": lambda: (S["dve_pad"], 1),
            "B1": lambda: (S["dve_b1"], 1),
            "B_XT": lambda t: (S["b_xTs"], t + 1),
            "B_H": lambda t: (S["b_gl"], t + 1),
            "B_G": lambda t: (S["b_glo"], t + 1),
            "B_Y": lambda t: (S["b_out"], t + 1),
        }
        bank_of, before, users = {}, {}, [None] * 8
        n = 0
        for kind, *i in sched:
            if kind in freed:
                for _ in range(2 if kind == "B1" else 1):
                    key = (kind, *i)
                    bank_of.setdefault(key, []).append(n % 8)
                    if users[n % 8] is not None:
                        before.setdefault(key, []).append(users[n % 8])
                    users[n % 8] = freed[kind](*i)
                    n += 1

        def own_bank(eng, *key):
            for s, v in before.get(key, []):
                eng.wait_ge(s, v)
            return bank[bank_of[key][0]]

        def of(*key):
            return bank[bank_of[key][0]]

        def split3(a, b):
            return ((a[0], b[0]), (a[0], b[1]), (a[1], b[0]))

        def f32(ap):
            return ap.bitcast(F32)

        counts = {"dve": 0, "act": 0, "pool": 0}

        def dve_link(eng, ins):
            counts["dve"] += 1
            ins.then_inc(dve_chain, 1)
            eng.wait_ge(dve_chain, counts["dve"])

        chains = []
        DRIP = {"Q": 2, "S": 0, "PT": 2, "AV": 2, "HLO": 12, "Y": 1, "TT": 1, "XT": 0}

        def drip(n):
            while chains and n > 0:
                n -= 1
                if next(chains[0], "end") == "end":
                    chains.pop(0)

        def drain():
            while chains:
                drip(1)

        def issued(ins):
            counts["dve"] += 1
            ins.then_inc(dve_chain, 1)
            return counts["dve"]

        def grouped(ap, n):
            return ap.rearrange("p (h k) -> p h k", h=n)

        def spread(ap, n):
            return ap.unsqueeze(2).to_broadcast([ap.shape[0], ap.shape[1], n])

        def sp_setup(sp):
            sp.dma_start(ctxT[:], A["ctxT"]).then_inc(L["ctx"], 16)
            sp.dma_start(wk_raw[:], A["Wk"]).then_inc(L["wk"], 16)
            small = [(ident[:], A["ident"]), (c_raw[:], A["masks"]), (prio[:], A["prio"]), (base[:], A["base"]),
                     (ids[:], A["ids"]), (bq[:], A["bq"]), (bk[:], A["bk"]), (b1[:], A["b1"]),
                     (wg_raw[:], A["WgT"]), (b2bc[:], A["b2"].to_broadcast([P, D])), (bvbc[:], A["bv"].to_broadcast([M, D]))]
            for dst, src in small:
                sp.dma_start(dst, src).then_inc(L["consts"], 16)
            return len(small)

        NSMALL = 11

        def sp_setup2(sp):
            sp.dma_start(wq_raw[:], A["Wq"]).then_inc(L["wq"], 16)
            sp.dma_start(wv_raw[:], A["Wv"]).then_inc(L["wv"], 16)
            sp.dma_start(w1_raw[:], A["W1"]).then_inc(L["w1"], 16)
            sp.dma_start(w2_raw[0][:], A["W2"][:, 0:MF * D // 2]).then_inc(L["w2a"], 16)
            sp.dma_start(w2_raw[1][:], A["W2"][:, MF * D // 2:]).then_inc(L["w2b"], 16)

        def sp_xload(sp, b):
            if b == 1:
                sp.wait_ge(S["dve_w2b"], 1)
                sp.wait_ge(S["pool_zero"], 4)
            for s in range(SUB):
                if b >= 2:
                    sp.wait_ge(scat[b % 2][s], 16 * (b // 2))
                src = A["x"][b * BLK + P * s:b * BLK + P * s + P, :]
                sp.dma_start(rows[b % 2][:, s, 0:D], src).then_inc(ld_x[b % 2][s], 16)
            if b == 0:
                sp_setup2(sp)

        def sp_kstore(sp):
            sp.wait_ge(S["act_k"], KD)
            sp.wait_ge(S["dve_k"], KD)
            for h in range(2):
                for i in range(NB):
                    sp.dma_start(k_parts[i, h].rearrange("g p k -> p g k"),
                                 f32(k_hl[:, h, :, M * i:M * i + M])).then_inc(st_k, 16)

        def sp_kload(sp, i):
            if i == 0:
                sp.wait_ge(st_k, 16 * 2 * NB)
                sp.wait_ge(S["pool_zero"], 1)
            else:
                sp.wait_ge(S["pe_s"], KD * SUB * BPB * i)
            for h in range(HG):
                for g in range(KD):
                    sp.dma_start(f32(kbd[HD * h:HD * h + HD, :, g, M * h:M * h + M]),
                                 k_parts[i, :, g, HD * h:HD * h + HD, :].rearrange("s p k -> p s k")
                                 ).then_inc(ld_k, 16)

        def sp_vload(sp, i):
            if i == 0:
                for n_, s_ in enumerate(st_vs):
                    sp.wait_ge(s_, 16 * (NB // 2))
                sp.wait_ge(S["pool_zero"], 2)
            else:
                sp.wait_ge(S["pe_av"], KD * BPB * i)
            for c, r, k, m, h in PIECES:
                for part in range(2):
                    src = v_parts[i, part, k:k + m, :].rearrange("k (g h f) -> k g h f", g=KD, h=HG)[:, :, h, :]
                    sp.dma_start(f32(vbd[r:r + m, part, :, c, HD * h:HD * h + HD]), src).then_inc(ld_v, 16)

        KLOADS, VLOADS = HG * KD, 2 * len(PIECES)

        def sp_vstore(sp, i):
            sp.wait_ge(S["act_v"], i + 1)
            sp.wait_ge(S["dve_v"], i + 1)
            sp.dma_start(v_parts[i].rearrange("s k f -> k s f"), f32(v_hl[i % 2][:])).then_inc(st_vs[i % 2], 16)

        def sp_b2load(sp):
            sp.wait_ge(S["pe_q"], KD * NBLK)
            sp.dma_start(b2e_raw[:], A["Eb2"].to_broadcast([B2LO + 1, NE, D])).then_inc(L["b2e"], 16)

        def sp_e1load(sp):
            sp.wait_ge(S["dve_b2"], 1)
            sp.dma_start(e1[:], A["E1"]).then_inc(L["e1"], 16)

        def sp_e2load(sp):
            sp.wait_ge(S["pe_h"], MF * NBLK)
            sp.dma_start(e2_raw[:], A["E2"]).then_inc(L["e2"], 16)
            for s in range(SUB):
                sp.wait_ge(scat[0][s], 16 * (NBLK // 2))
            sp.wait_ge(S["pe_xT"], SUB * NBLK)
            sp.dma_start(lns[:], A["lns"]).then_inc(L["ln"], 16)
            sp.dma_start(lnb[:], A["lnb"]).then_inc(L["ln"], 16)
            sp.dma_start(b1e[:], A["Eb1"]).then_inc(L["eb"], 16)
            sp.dma_start(padrow[:], A["padrow"]).then_inc(L["tab"], 16)
            sp.dma_start(padoff[:], A["padoff"]).then_inc(L["tab"], 16)
            sp.dma_start(jt[:], A["jt"]).then_inc(L["tab"], 16)
            sp.wait_ge(L["tab"], 48)
            sp.dma_start(region[NE * REG:NE * REG + P, :], padrow[:]).then_inc(L["pad0"], 16)

        def pool_setup(pool):
            z = lambda ap: nc.gpsimd.memset(ap, 0.0)
            z(f32(kbd[:])).then_inc(S["pool_zero"], 1)
            z(f32(vbd[:])).then_inc(S["pool_zero"], 1)
            z(rows[0][:, :, D:ROW]).then_inc(S["pool_zero"], 1)

        def dve_setup(dve):
            dve.memset(cum[:], 0.0)
            dve.wait_ge(L["consts"], 16 * NSMALL)
            dve.tensor_scalar(bks[:], bk[:], SCALE, None, ALU.mult).then_inc(S["dve_bks"], 1)
            dve.tensor_copy(tri[:], c_raw[:, 0:P])
            dve.tensor_copy(ones[:], c_raw[:, P:2 * P])
            dve.tensor_copy(sel[:], c_raw[0:B2LO + 1, 2 * P:3 * P])
            wgr = wg_raw[:].rearrange("p (k e) -> p k e", e=NE)
            dve_link(dve, dve.tensor_copy(wg[:, 0], wgr))
            dve.tensor_tensor(wg[:, 1], wgr, f32(wg[:, 0]), ALU.subtract).then_inc(S["dve_const"], 1)

        def pe_kp(pe, m):
            p = own_bank(pe, "KP", m)
            if m == 0:
                pe.wait_ge(L["ctx"], 16)
                pe.wait_ge(L["wk"], 16)
            for k in range(KT):
                mm = pe.matmul(p[:, 0:NB * M], wk_raw[:, k, P * m:P * m + P], ctxT[:, k, :],
                               start=k == 0, stop=k == KT - 1)
            mm.then_inc(pe_k, 1)

        def act_kp(act, m):
            if m == 0:
                act.wait_ge(S["dve_bks"], 1)
            act.wait_ge(pe_k, m + 1)
            act.activation(k_f[:, m, :], of("KP", m)[:, 0:NB * M], ACT.Identity, bias=bks[:, m:m + 1], scale=SCALE
                           ).then_inc(S["act_kf"], 1)
            act.wait_ge(S["act_kf"], m + 1)
            act.activation(k_hl[:, 0, m, :], k_f[:, m, :], ACT.Identity).then_inc(S["act_k"], 1)

        def dve_kp(dve, m):
            dve.wait_ge(S["act_k"], m + 1)
            dve.tensor_tensor(k_hl[:, 1, m, :], k_f[:, m, :], f32(k_hl[:, 0, m, :]), ALU.subtract
                              ).then_inc(S["dve_k"], 1)

        def pe_vp(pe, i):
            p = own_bank(pe, "VP", i)
            pe.wait_ge(L["wv"], 16)
            for k in range(KT):
                mm = pe.matmul(p[0:M, :], ctxT[:, k, M * i:M * i + M], wv_raw[:, k, :],
                               start=k == 0, stop=k == KT - 1)
            mm.then_inc(pe_v, 1)

        def dve_vp(dve, i):
            dve.wait_ge(pe_v, i + 1)
            if i >= 2:
                dve.wait_ge(st_vs[i % 2], 16 * (i // 2))
            dve.tensor_tensor(v_f[i % 2][:], of("VP", i)[0:M, :], bvbc[:], ALU.add).then_inc(S["dve_vf"], 1)
            dve.wait_ge(S["act_v"], i + 1)
            dve.tensor_tensor(v_hl[i % 2][:, 1], v_f[i % 2][:], f32(v_hl[i % 2][:, 0]),
                              ALU.subtract).then_inc(S["dve_v"], 1)

        def act_vp(act, i):
            act.wait_ge(S["dve_vf"], i + 1)
            if i >= 2:
                act.wait_ge(st_vs[i % 2], 16 * (i // 2))
            act.activation(v_hl[i % 2][:, 0], v_f[i % 2][:], ACT.Identity).then_inc(S["act_v"], 1)

        def act_convert(act, w, raw, ld, done):
            act.wait_ge(ld, 16)
            act.activation(w, raw, ACT.Identity).then_inc(done, 1)

        def dve_convert(dve, lo, hi, raw, hi_done, done):
            dve.wait_ge(hi_done, 1)
            dve.tensor_tensor(lo, raw, f32(hi), ALU.subtract).then_inc(done, 1)

        wq_hl = [wq[:, h].rearrange("p k n -> p (k n)") for h in range(2)]
        w1_hl = [w1[:, h].rearrange("p k n -> p (k n)") for h in range(2)]
        w2_hl = [[w2[:, h, MF // 2 * j:MF // 2 * (j + 1)].rearrange("p k n -> p (k n)") for h in range(2)]
                 for j in range(2)]

        def act_conv_wq(act):
            act_convert(act, wq_hl[0], wq_raw[:], L["wq"], S["act_wq"])

        def dve_conv_wq(dve):
            dve_convert(dve, wq_hl[1], wq_hl[0], wq_raw[:], S["act_wq"], S["dve_wq"])

        def act_conv_w12(act):
            for s_ in st_vs:
                act.wait_ge(s_, 16 * (NB // 2))
            act.wait_ge(st_k, 16 * 2 * NB)
            act_convert(act, w1_hl[0], w1_raw[:], L["w1"], S["act_w1"])
            act_convert(act, w2_hl[1][0], w2_raw[1][:], L["w2b"], S["act_w2b"])
            act_convert(act, w2_hl[0][0], w2_raw[0][:], L["w2a"], S["act_w2a"])

        def dve_conv_w12(dve):
            dve_convert(dve, w1_hl[1], w1_hl[0], w1_raw[:], S["act_w1"], S["dve_w1"])
            dve_convert(dve, w2_hl[1][1], w2_hl[1][0], w2_raw[1][:], S["act_w2b"], S["dve_w2b"])
            dve_convert(dve, w2_hl[0][1], w2_hl[0][0], w2_raw[0][:], S["act_w2a"], S["dve_w2a"])

        def pool_conv_w12(pool):
            pool.wait_ge(S["dve_w2b"], 1)
            nc.gpsimd.memset(rows[1][:, :, D:ROW], 0.0).then_inc(S["pool_zero"], 1)

        def rsqrt(dve, var, y, n):
            v, t = nw[:, 0, :], nw[:, 1, :]
            steps = [lambda: dve.tensor_scalar(v, var, EPS, None, ALU.add),
                     lambda: dve.tensor_scalar(t.bitcast(I32), v.bitcast(I32), 1, None, ALU.logical_shift_right),
                     lambda: dve.tensor_scalar(y.bitcast(I32), t.bitcast(I32), -1, float(0x5F3759DF),
                                               ALU.mult, ALU.add)]
            steps += [lambda: dve.tensor_tensor(t, y, y, ALU.mult),
                      lambda: dve.scalar_tensor_tensor(t, t, -0.5, v, ALU.mult, ALU.mult),
                      lambda: dve.scalar_tensor_tensor(y, t, 1.5, y, ALU.add, ALU.mult)] * 3
            for f in steps:
                dve.wait_ge(dve_chain, n)
                n = issued(f())
                yield
            return n

        def aggregate(dve, raw, into, n):
            dve.wait_ge(dve_chain, n)
            for s in range(SUB):
                n = issued(dve.bn_aggr(into[:, s, :], raw[:, s, :]))
                yield
            return n

        def dve_xstat(dve, b):
            def chain():
                for s in range(SUB):
                    dve.wait_ge(ld_x[b % 2][s], 16 * (b // 2 + 1))
                    n = issued(dve.bn_stats(bn[:, s, :], rows[b % 2][:, s, 0:D]))
                    yield
                n = yield from aggregate(dve, bn, mvx, n)
                n = yield from rsqrt(dve, mvx[:, :, 1], rx[:], n)
                dve.wait_ge(dve_chain, n)
                for s in range(2):
                    dve_xn(dve, b, s)
                    yield
            chains.append(chain())

        def dve_xn(dve, b, s):
            i = SUB * b + s
            if i >= 2:
                dve.wait_ge(S["pe_xT"], i - 1)
            dve.tensor_scalar(xn[s % 2][:], rows[b % 2][:, s, 0:D], mvx[:, s, 0:1], rx[:, s:s + 1],
                              ALU.subtract, ALU.mult).then_inc(S["dve_xn"], 1)

        def pe_xT(pe, b, s):
            p = own_bank(pe, "XT", b, s)
            if b == 0 and s == 0:
                pe.wait_ge(L["consts"], 16 * NSMALL)
            pe.wait_ge(S["dve_xn"], SUB * b + s + 1)
            for k in range(KD):
                mm = pe.transpose(p[:, P * k:P * k + P], xn[s % 2][:, P * k:P * k + P], ident[:])
            mm.then_inc(S["pe_xT"], 1)

        def act_xT(act, b, s):
            if b == 0 and s == 0:
                act.wait_ge(S["dve_const"], 1)
            act.wait_ge(S["pe_xT"], SUB * b + s + 1)
            act.activation(actA[:, 0, :, P * s:P * s + P], of("XT", b, s)[:].rearrange("p (k t) -> p k t", k=KD),
                           ACT.Identity).then_inc(S["act_xT"], 1)

        def dve_xT(dve, b, s):
            if s == 0:
                drain()
            dve.wait_ge(S["act_xT"], SUB * b + s + 1)
            dve.tensor_tensor(actA[:, 1, :, P * s:P * s + P], of("XT", b, s)[:].rearrange("p (k t) -> p k t", k=KD),
                              f32(actA[:, 0, :, P * s:P * s + P]), ALU.subtract).then_inc(S["dve_xT"], 1)
            if s + 2 < SUB:
                dve_xn(dve, b, s + 2)

        def pool_xT(pool, b, s):
            pool.wait_ge(S["dve_xn"], SUB * b + s + 1)
            r = rows[b % 2][:, s, 0:D]
            nc.gpsimd.tensor_tensor(r, r, b2bc[:], ALU.add).then_inc(S["pool_xb"], 1)

        def pe_q(pe, b, m):
            p = own_bank(pe, "Q", b, m)
            if b == 0:
                pe.wait_ge(S["dve_wq"], 1)
            pe.wait_ge(S["dve_xT"], SUB * (b + 1))
            for k in range(KD):
                for j, (w, a) in enumerate(split3([wq[:, h, k, P * m:P * m + P] for h in range(2)],
                                                  [actA[:, h, k, :] for h in range(2)])):
                    mm = pe.matmul(p[:], w, a, start=k == 0 and j == 0, stop=k == KD - 1 and j == 2)
            mm.then_inc(S["pe_q"], 1)

        def act_q(act, b, m):
            act.wait_ge(S["pe_q"], KD * b + m + 1)
            if b >= 2:
                act.wait_ge(S["pe_l"], b - 1)
            act.activation(actQ[:, 0, m, :], of("Q", b, m)[:], ACT.Identity, bias=bq[:, m:m + 1]
                           ).then_inc(S["act_q"], 1)

        def dve_q(dve, b, m):
            dve.wait_ge(S["act_q"], KD * b + m + 1)
            dve.scalar_tensor_tensor(actQ[:, 1, m, :], of("Q", b, m)[:], bq[:, m:m + 1], f32(actQ[:, 0, m, :]),
                                     ALU.add, ALU.subtract).then_inc(S["dve_q"], 1)

        def pe_s(pe, b, g, s):
            p = own_bank(pe, "S", b, g, s)
            if s == 0:
                pe.wait_ge(S["dve_q"], KD * b + g + 1)
                pe.wait_ge(ld_k, 16 * KLOADS * (b // BPB + 1))
            for j, (q, k) in enumerate(split3([actQ[:, h, g, P * s:P * s + P] for h in range(2)],
                                              [kbd[:, h, g, :] for h in range(2)])):
                mm = pe.matmul(p[:, 0:SC], q, k, start=j == 0, stop=j == 2)
            mm.then_inc(S["pe_s"], 1)

        def dve_s(dve, b, g, s):
            dve.wait_ge(S["pe_s"], SUB * (KD * b + g) + s + 1)
            if b and s == 0 and g in ON_ACT:
                dve.wait_ge(S["act_es"], SUB * (len(ON_ACT) * (b - 1) + ON_ACT.index(g) + 1))
            p = grouped(of("S", b, g, s)[:, 0:SC], HG)
            dve.tensor_reduce(mx[:, SUB * g + s, :], p, AX, ALU.max, negate=True).then_inc(S["dve_max"], 1)
            if g in ON_DVE:
                if s:
                    dve_sub(dve, b, g, s - 1)
                if s == SUB - 1:
                    drip(1)
                    dve_sub(dve, b, g, s)

        def dve_sub(dve, b, g, s):
            if b and s == 0:
                dve.wait_ge(S["pe_pt"], NC * KD * b)
            dve.wait_ge(S["dve_max"], SUB * (KD * b + g) + s + 1)
            dve.tensor_tensor(grouped(E[:, g, s, :], HG), grouped(of("S", b, g, s)[:, 0:SC], HG),
                              spread(mx[:, SUB * g + s, :], M), ALU.add).then_inc(S["dve_sub"], 1)

        def act_s(act, b, g, s):
            if g not in ON_ACT:
                return
            if b and s == 0:
                act.wait_ge(S["pe_pt"], NC * KD * b)
                act.wait_ge(S["dve_rc"], KD * (b - 1) + g + 1)
            act.wait_ge(S["dve_max"], SUB * (KD * b + g) + s + 1)
            for h in range(HG):
                ins = act.activation(E[:, g, s, M * h:M * h + M], of("S", b, g, s)[:, M * h:M * h + M], ACT.Exp,
                                     bias=mx[:, SUB * g + s, h:h + 1],
                                     accum_out=sm[:, g, HG * s + h:HG * s + h + 1])
            ins.then_inc(S["act_es"], 1)

        def act_soft(act, b, g):
            if g in ON_DVE:
                act.wait_ge(score_done(b, g, SUB - 1)[0], score_done(b, g, SUB - 1)[1])
                act.activation(E[:, g], E[:, g], ACT.Exp).then_inc(S["act_exp"], 1)

        def dve_sum(dve, b, g):
            i = KD * b + g
            if g in ON_ACT:
                dve.wait_ge(score_done(b, g, SUB - 1)[0], score_done(b, g, SUB - 1)[1])
            else:
                dve.wait_ge(S["act_exp"], len(ON_DVE) * b + ON_DVE.index(g) + 1)
                n = issued(dve.tensor_reduce(sm[:, g, :], grouped(E[:, g].rearrange("p s c -> p (s c)"), SUB * HG),
                                             AX, ALU.add))
                drip(1)
                dve.wait_ge(dve_chain, n)
            if i >= KD:
                dve.wait_ge(S["pool_p"], i - KD + 1)
            dve.reciprocal(rc[:, g, :], sm[:, g, :]).then_inc(S["dve_rc"], 1)

        def pool_soft(pool, b, g):
            pool.wait_ge(S["dve_rc"], KD * b + g + 1)
            e = grouped(E[:, g].rearrange("p s c -> p (s c)"), SUB * HG)
            nc.gpsimd.tensor_tensor(e, e, spread(rc[:, g, :], M), ALU.mult).then_inc(S["pool_p"], 1)

        def pe_pt(pe, b, g, c):
            p = own_bank(pe, "PT", b, g, c)
            pe.wait_ge(S["pool_p"], KD * b + g + 1)
            for s in range(SUB):
                mm = pe.transpose(p[0:CH[c], P * s:P * s + P], E[:, g, s, CO[c]:CO[c] + CH[c]], ident[:])
            mm.then_inc(S["pe_pt"], 1)

        def act_pt(act, b, g, c):
            j = NC * g + c
            if b == 0 and j == 0:
                act.wait_ge(S["dve_w1"], 1)
                act.wait_ge(S["dve_w2a"], 1)
                act.wait_ge(S["dve_wq"], 1)
            if j >= SLOTS:
                act.wait_ge(S["pe_av"], KD * b + (j - SLOTS) // NC + 1)
            act.wait_ge(S["pe_pt"], NC * KD * b + j + 1)
            act.activation(actH[0:CH[c], 0, j % SLOTS, :], of("PT", b, g, c)[0:CH[c], :], ACT.Identity
                           ).then_inc(S["act_pt"], 1)

        def dve_pt(dve, b, g, c):
            j = NC * g + c
            dve.wait_ge(S["act_pt"], NC * KD * b + j + 1)
            dve.tensor_tensor(actH[0:CH[c], 1, j % SLOTS, :], of("PT", b, g, c)[0:CH[c], :],
                              f32(actH[0:CH[c], 0, j % SLOTS, :]), ALU.subtract).then_inc(S["dve_pt"], 1)

        def pe_av(pe, b, g):
            p = own_bank(pe, "AV", b, g)
            pe.wait_ge(ld_v, 16 * VLOADS * (b // BPB + 1))
            for c in range(NC):
                j = NC * g + c
                pe.wait_ge(S["dve_pt"], NC * KD * b + j + 1)
                for i, (v, w) in enumerate(split3([vbd[0:CH[c], h, g, c, :] for h in range(2)],
                                                  [actH[0:CH[c], h, j % SLOTS, :] for h in range(2)])):
                    mm = pe.matmul(p[:], v, w, start=c == 0 and i == 0, stop=c == NC - 1 and i == 2)
            mm.then_inc(S["pe_av"], 1)

        def act_av(act, b, g):
            act.wait_ge(S["pe_av"], KD * b + g + 1)
            act.activation(actA[:, 0, g, :], of("AV", b, g)[:], ACT.Identity).then_inc(S["act_o"], 1)

        def dve_av(dve, b, g):
            dve.wait_ge(S["act_o"], KD * b + g + 1)
            dve.tensor_tensor(actA[:, 1, g, :], of("AV", b, g)[:], f32(actA[:, 0, g, :]), ALU.subtract
                              ).then_inc(S["dve_o"], 1)

        def pe_h(pe, b, m):
            p = own_bank(pe, "H", b, m)
            if b == 0:
                pe.wait_ge(S["dve_w1"], 1)
            for k in range(KD):
                pe.wait_ge(S["dve_o"], KD * b + k + 1)
                for j, (w, a) in enumerate(split3([w1[:, h, k, P * m:P * m + P] for h in range(2)],
                                                  [actA[:, h, k, :] for h in range(2)])):
                    mm = pe.matmul(p[:], w, a, start=k == 0 and j == 0, stop=k == KD - 1 and j == 2)
            mm.then_inc(S["pe_h"], 1)

        def act_h(act, b, m):
            i = MF * b + m
            act.wait_ge(S["pe_h"], i + 1)
            if i >= 2:
                act.wait_ge(S["dve_h"], i - 1)
            act.activation(htmp[m % 2][:], of("H", b, m)[:], ACT.Relu, bias=b1[:, m:m + 1]).then_inc(S["act_h"], 1)
            act.activation(actH[:, 0, m, :], of("H", b, m)[:], ACT.Relu, bias=b1[:, m:m + 1]).then_inc(S["act_hh"], 1)

        def dve_h(dve, b, m):
            dve.wait_ge(S["act_hh"], MF * b + m + 1)
            dve.tensor_tensor(actH[:, 1, m, :], htmp[m % 2][:], f32(actH[:, 0, m, :]), ALU.subtract
                              ).then_inc(S["dve_h"], 1)

        def y_products(pe, b, s, chunks_):
            p = of("YA", b, s)
            for m in chunks_:
                pe.wait_ge(S["dve_h"], MF * b + m + 1)
                for j, (a, w) in enumerate(split3([actH[:, h, m, P * s:P * s + P] for h in range(2)],
                                                  [w2[:, h, m, :] for h in range(2)])):
                    mm = pe.matmul(p[:], a, w, start=m == 0 and j == 0, stop=m == MF - 1 and j == 2)
            return mm

        def pe_ya(pe, b, s):
            own_bank(pe, "YA", b, s)
            if b == 0:
                pe.wait_ge(S["dve_w2a"], 1)
                pe.wait_ge(S["dve_w2b"], 1)
            y_products(pe, b, s, range(MF // 2))

        def pe_y(pe, b, s):
            y_products(pe, b, s, range(MF // 2, MF)).then_inc(S["pe_y"], 1)

        bn2_done = {}

        def dve_y(dve, b, s):
            dve.wait_ge(S["pe_y"], SUB * b + s + 1)
            dve.wait_ge(S["pool_xb"], SUB * b + s + 1)
            r = rows[b % 2][:, s, 0:D]
            dve.tensor_tensor(r, of("YA", b, s)[:], r, ALU.add).then_inc(S["dve_x2"], 1)

            def chain():
                dve.wait_ge(S["dve_x2"], SUB * b + s + 1)
                bn2_done[b] = issued(dve.bn_stats(bn2[:, s, :], r))
                yield
            chains.append(chain())

        def dve_x2stat(dve, b):
            def chain():
                n = yield from aggregate(dve, bn2, mv, bn2_done[b])
                n = yield from rsqrt(dve, mv[:, :, 1], r1[:], n)
                dve.wait_ge(dve_chain, n)
                dve.scalar_tensor_tensor(nmr[:], mv[:, :, 0], -1.0, r1[:], ALU.mult, ALU.mult
                                         ).then_inc(S["dve_s2"], 1)
                yield
            if bn2_done.get(b) is None:
                drain()
            chains.append(chain())

        def act_xt(act, b, s):
            act.wait_ge(S["dve_s2"], b + 1)
            if b + 1 < NBLK:
                act.wait_ge(S["pe_pt"], NC * KD * (b + 2))
            act.activation(xt(s), rows[b % 2][:, s, 0:D], ACT.Identity, bias=nmr[:, s:s + 1],
                           scale=r1[:, s:s + 1]).then_inc(S["act_xt"], 1)

        def pe_tt(pe, b, s):
            p = own_bank(pe, "TT", b, s)
            pe.wait_ge(S["act_xt"], SUB * b + s + 1)
            for k in range(KD):
                mm = pe.transpose(p[:, P * k:P * k + P], xt(s)[:, P * k:P * k + P], ident[:])
            mm.then_inc(S["pe_tt"], 1)

        def act_tt(act, b, s):
            act.wait_ge(S["pe_tt"], SUB * b + s + 1)
            act.activation(actQ[:, 0, :, P * s:P * s + P], of("TT", b, s)[:].rearrange("p (k t) -> p k t", k=KD),
                           ACT.Identity).then_inc(S["act_tt"], 1)

        def dve_tt(dve, b, s):
            dve.wait_ge(S["act_tt"], SUB * b + s + 1)
            dve.tensor_tensor(actQ[:, 1, :, P * s:P * s + P], of("TT", b, s)[:].rearrange("p (k t) -> p k t", k=KD),
                              f32(actQ[:, 0, :, P * s:P * s + P]), ALU.subtract).then_inc(S["dve_tt"], 1)

        def dve_rowtail(dve, b):
            def chain():
                for s in range(SUB):
                    dve.wait_ge(S["act_xt"], SUB * b + s + 1)
                    n = issued(dve.bn_stats(bn[:, s, :], xt(s)))
                    yield
                n = yield from aggregate(dve, bn, mv, n)
                n = yield from rsqrt(dve, mv[:, :, 1], r2[:], n)
                r = rows[b % 2]
                dve.wait_ge(dve_chain, n)
                dve.tensor_tensor(r[:, :, D], r1[:], r2[:], ALU.mult)
                n = issued(dve.tensor_tensor(tB[:], nmr[:], mv[:, :, 0], ALU.subtract))
                yield
                dve.wait_ge(dve_chain, n)
                dve.tensor_tensor(r[:, :, D + 1], tB[:], r2[:], ALU.mult)
                dve.tensor_copy(r[:, :, D + 2].bitcast(U32), ids[:, SUB * b:SUB * b + SUB]).then_inc(S["dve_row"], 1)
                yield
            chains.append(chain())

        def pe_l(pe, b):
            p = own_bank(pe, "L", b)
            if b == 0:
                pe.wait_ge(S["dve_const"], 1)
            pe.wait_ge(S["dve_tt"], SUB * (b + 1))
            for k in range(KD):
                for j, (w, a) in enumerate(split3([wg[:, h, k, :] for h in range(2)],
                                                  [actQ[:, h, k, :] for h in range(2)])):
                    mm = pe.matmul(p[0:NE, :], w, a, start=k == 0 and j == 0, stop=k == KD - 1 and j == 2)
            mm.then_inc(S["pe_l"], 1)

        def act_l(act, b):
            act.wait_ge(S["pe_l"], b + 1)
            act.activation(lgT, of("L", b)[0:NE, :], ACT.Identity).then_inc(S["act_l"], 1)

        def pe_lt(pe, b):
            p = own_bank(pe, "LT", b)
            pe.wait_ge(S["act_l"], b + 1)
            for s in range(SUB):
                mm = pe.transpose(p[:, NE * s:NE * s + NE], lgT[:, P * s:P * s + P], ident[0:NE, 0:NE])
            mm.then_inc(S["pe_lt"], 1)

        def dve_lt(dve, b):
            dve.wait_ge(S["pe_lt"], b + 1)
            dve.tensor_copy(lg[:], of("LT", b)[:, 0:SUB * NE].rearrange("p (s e) -> p s e", e=NE)
                            ).then_inc(S["dve_lg"], 1)
            drip(1)
            dve.wait_ge(S["dve_lg"], b + 1)
            for f in (lambda: dve.tensor_reduce(lm[:], lg[:], AX, ALU.max),
                      lambda: dve.tensor_tensor(lw[:], lg[:], spread(lm[:], NE), ALU.is_equal),
                      lambda: dve.tensor_tensor(lw[:], lw[:], prio[:], ALU.mult),
                      lambda: dve.tensor_reduce(lm[:], lw[:], AX, ALU.max)):
                n = issued(f())
                drip(1)
                dve.wait_ge(dve_chain, n)
            dve.tensor_tensor(oh[:], prio[:], spread(lm[:], NE), ALU.is_equal).then_inc(S["dve_oh"], 1)

        def pe_rk(pe, b):
            p = own_bank(pe, "RK", b)
            w = SUB * NE
            pe.wait_ge(S["dve_oh"], b + 1)
            if b:
                pe.wait_ge(S["dve_cum"], b)
            o_ = oh[:].rearrange("p s e -> p (s e)")
            pe.matmul(p[:, 0:w], tri[:], o_, start=True, stop=False)
            for s in range(1, SUB):
                pe.matmul(p[:, NE * s:w], ones[:], o_[:, 0:w - NE * s], start=False, stop=False)
            for s in range(SUB):
                mm = pe.matmul(p[:, NE * s:NE * s + NE], ones[:], cum[:], start=False, stop=s == SUB - 1)
            mm.then_inc(S["pe_rk"], 1)

        def dve_rk(dve, b):
            dve.wait_ge(S["pe_rk"], b + 1)
            if b >= 2:
                for s in range(SUB):
                    dve.wait_ge(scat[b % 2][s], 16 * (b // 2))
            dve.tensor_tensor(rk[:], of("RK", b)[:, 0:SUB * NE].rearrange("p (s e) -> p s e", e=NE), base[:], ALU.add
                              ).then_inc(S["dve_rk"], 1)
            n1 = issued(dve.tensor_reduce(lw[:, 0, :], oh[:].rearrange("p s e -> p e s"), AX, ALU.add))
            dve.wait_ge(S["dve_rk"], b + 1)
            n2 = issued(dve.tensor_tensor(rk[:], rk[:], oh[:], ALU.mult))
            dve.wait_ge(dve_chain, n1)
            dve.tensor_tensor(cum[:], cum[:], lw[:, 0, :], ALU.add).then_inc(S["dve_cum"], 1)
            dve.wait_ge(dve_chain, n2)
            n3 = issued(dve.tensor_reduce(posf[:], rk[:], AX, ALU.add))
            drip(1)
            dve.wait_ge(dve_chain, n3)
            dve.tensor_copy(pos[b % 2][:], posf[:]).then_inc(S["dve_pos"], 1)

        def pool_scat(pool, b):
            pool.wait_ge(S["dve_pos"], b + 1)
            pool.wait_ge(S["dve_row"], b + 1)
            for s in range(SUB):
                nc.gpsimd.indirect_dma_start(
                    out=region, out_offset=bass.IndirectOffsetOnAxis(ap=pos[b % 2][:, s:s + 1], axis=0),
                    in_=rows[b % 2][:, s, :], in_offset=None).then_inc(scat[b % 2][s], 16)

        def pe_b1(pe):
            own_bank(pe, "B1")
            pe.wait_ge(L["ln"], 32)
            pe.wait_ge(L["e1"], 16)
            for e in range(NE):
                p = bank[bank_of[("B1",)][e // 4]][0:1, EH * (e % 4):EH * (e % 4) + EH]
                for k in range(KD):
                    mm = pe.matmul(p, lnb[:, k, e:e + 1], e1[:, k, e, :], start=k == 0, stop=k == KD - 1)
            mm.then_inc(S["pe_b1"], 1)

        def dve_b1(dve):
            dve.wait_ge(S["pe_b1"], 1)
            dve.wait_ge(L["eb"], 16)
            for j in range(2):
                t = b1e[:, 4 * j:4 * j + 4, :].rearrange("p e h -> p (e h)")
                ins = dve.tensor_tensor(t, bank[bank_of[("B1",)][j]][0:1, :], t, ALU.add)
            ins.then_inc(S["dve_b1"], 1)
            for k in range(KD):
                ins = dve.tensor_tensor(e1[:, k], e1[:, k], spread(lns[:, k, :], EH), ALU.mult)
            ins.then_inc(S["dve_e1"], 1)

        def act_b2conv(act):
            act.wait_ge(S["pe_av"], KD * NBLK)
            act.wait_ge(L["b2e"], 16)
            act.activation(b2e[:], b2e_raw[:], ACT.Identity).then_inc(S["act_b2"], 1)

        def dve_b2conv(dve):
            dve.wait_ge(S["act_b2"], 1)
            lo = b2e[B2LO:B2LO + 1]
            dve.tensor_tensor(lo, b2e_raw[B2LO:B2LO + 1], f32(lo), ALU.subtract).then_inc(S["dve_b2"], 1)

        def act_e2conv(act):
            act.wait_ge(S["pe_h"], MF * NBLK)
            act.wait_ge(L["e2"], 16)
            act.activation(e2[:, 0], e2_raw[:], ACT.Identity).then_inc(S["act_e2"], 1)

        def dve_e2conv(dve):
            dve.wait_ge(S["act_e2"], 1)
            dve.tensor_tensor(e2[:, 1], e2_raw[:], f32(e2[:, 0]), ALU.subtract).then_inc(S["dve_e2"], 1)

        def pe_table(pe):
            p = own_bank(pe, "TABLE")
            pe.wait_ge(S["dve_cum"], NBLK)
            pe.matmul(p[:, 0:NE], ones[:], cum[:], start=True, stop=True).then_inc(S["pe_cnt"], 1)

        def dve_table(dve):
            dve.wait_ge(S["pe_cnt"], 1)
            dve.wait_ge(L["tab"], 48)
            dve_link(dve, dve.tensor_copy(cnt[:], of("TABLE")[:, 0:NE]))
            dve_link(dve, dve.tensor_tensor(padf[:], padoff[:], cnt[:], ALU.add))
            dve.tensor_copy(padu[:], padf[:]).then_inc(S["dve_pad"], 1)
            dve_link(dve, dve.tensor_scalar(cti[:], cnt[:], float(P - 1), None, ALU.add))
            dve_link(dve, dve.tensor_scalar(cti[:], cti[:], 7, None, ALU.logical_shift_right))
            dve_link(dve, dve.tensor_copy(ctl[:], cti[:]))
            dve.tensor_scalar(stp[:], ctl[:], -float(P), float(REG), ALU.mult, ALU.add)
            dve_link(dve, dve.tensor_copy(cinc[:], ctl[:]))
            for e in range(1, NE):
                dve_link(dve, dve.tensor_tensor(cinc[:, e:e + 1], cinc[:, e:e + 1], cinc[:, e - 1:e], ALU.add))
            bc = lambda t: t[0:1, :].unsqueeze(1).to_broadcast([1, NT, NE])
            dve_link(dve, dve.tensor_tensor(ge[:], jt[:], bc(cinc), ALU.is_ge))
            dve_link(dve, dve.tensor_reduce(ex[:], ge[:], AX, ALU.add))
            dve_link(dve, dve.tensor_scalar(exi[:], ex[:], float(NE - 1), None, ALU.min))
            dve_link(dve, dve.tensor_tensor(ge[:], ge[:], bc(stp), ALU.mult))
            dve_link(dve, dve.tensor_reduce(rw[:], ge[:], AX, ALU.add))
            dve_link(dve, dve.scalar_tensor_tensor(rw[:], jt[:, :, 0], float(P), rw[:], ALU.mult, ALU.add))
            dve.tensor_scalar(rwi[:], rw[:], float(NE * REG), None, ALU.min).then_inc(S["dve_tab"], 1)

        def pool_table(pool):
            pool.wait_ge(S["dve_pad"], 1)
            for e in range(NE):
                nc.gpsimd.indirect_dma_start(
                    out=region, out_offset=bass.IndirectOffsetOnAxis(ap=padu[:, e:e + 1], axis=0),
                    in_=padrow[:], in_offset=None).then_inc(st_pad, 16)

        regs = {}

        def load_reg(eng, name, ap, hi):
            if name not in regs:
                regs[name] = eng.alloc_register(name)
                eng.wait_ge(S["dve_tab"], 1)
            eng.reg_load(regs[name], ap)
            return eng.snap(regs[name], min_val=0, max_val=hi)

        experts = {}

        def expert(pe, t):
            if t not in experts:
                experts[t] = load_reg(pe, f"expert{t % NREG}", exi[0:1, t:t + 1], NE - 1)
            return experts[t]

        NREG = 4

        def pick(ap, e):
            return ap[:, bass.ds(e, 1), :].rearrange("p e n -> p (e n)")

        def sp_bload(sp, t):
            if t == 0:
                for s in range(SUB):
                    for i in range(2):
                        sp.wait_ge(scat[i][s], 16 * (NBLK // 2))
                sp.wait_ge(st_pad, 16 * NE)
                sp.wait_ge(L["pad0"], 16)
                sp.wait_ge(S["pe_y"], SUB * NBLK)
            if t >= NROW:
                sp.wait_ge(st_out[t % NROW], 16 * (t // NROW))
            r = load_reg(sp, "row", rwi[0:1, t:t + 1], NE * REG)
            sp.dma_start(rowB[t % NROW][:], region[bass.ds(r, P), :]).then_inc(ld_row[t % NROW], 16)

        def dve_bx(dve, t):
            r = rowB[t % NROW]
            dve.wait_ge(ld_row[t % NROW], 16 * (t // NROW + 1))
            if t >= 2:
                dve.wait_ge(S["b_xT"], t - 1)
            dve.tensor_scalar(xh[t % 2][:], r[:, 0:D], r[:, D:D + 1], r[:, D + 1:D + 2], ALU.mult, ALU.add
                              ).then_inc(S["b_xh"], 1)

        def pe_bx(pe, t):
            expert(pe, t)
            p = own_bank(pe, "B_XT", t)
            pe.wait_ge(S["b_xh"], t + 1)
            for k in range(KD):
                mm = pe.transpose(p[:, P * k:P * k + P], xh[t % 2][:, P * k:P * k + P], ident[:])
            mm.then_inc(S["b_xT"], 1)

        def act_bx(act, t):
            act.wait_ge(S["b_xT"], t + 1)
            if t >= 2:
                act.wait_ge(S["b_h"], t - 1)
            act.activation(xhT[t % 2][:], of("B_XT", t)[:].rearrange("p (k t) -> p k t", k=KD), ACT.Identity
                           ).then_inc(S["b_xTs"], 1)

        def pe_bh(pe, t):
            p = own_bank(pe, "B_H", t)[:, 0:EH]
            pe.wait_ge(S["b_xTs"], t + 1)
            if t == 0:
                pe.wait_ge(S["dve_e1"], 1)
                pe.wait_ge(S["dve_b1"], 1)
            e = expert(pe, t)
            pe.matmul(p, f32(sel[0:1, :]), pick(b1e[:], e), start=True, stop=False)
            for k in range(KD):
                mm = pe.matmul(p, xhT[t % 2][:, k, :], pick(e1[:, k], e), start=False, stop=k == KD - 1)
            mm.then_inc(S["b_h"], 1)

        def act_bh(act, t):
            act.wait_ge(S["b_h"], t + 1)
            if t >= 2:
                act.wait_ge(S["b_g"], t - 1)
            act.activation(gl[t % 2][:], of("B_H", t)[:, 0:EH], ACT.Gelu).then_inc(S["b_gl"], 1)

        def pe_bg(pe, t):
            p = own_bank(pe, "B_G", t)
            pe.wait_ge(S["b_gl"], t + 1)
            pe.transpose(p[:, 0:P], gl[t % 2][:], ident[:]).then_inc(S["b_g"], 1)

        def act_bg(act, t):
            act.wait_ge(S["b_g"], t + 1)
            if t >= 2:
                act.wait_ge(S["b_y"], t - 1)
            act.activation(gT[t % 2][:, 0, :], of("B_G", t)[:, 0:P], ACT.Identity).then_inc(S["b_ghi"], 1)

        def dve_bg(dve, t):
            dve.wait_ge(S["b_ghi"], t + 1)
            dve.tensor_tensor(gT[t % 2][:, 1, :], of("B_G", t)[:, 0:P], f32(gT[t % 2][:, 0, :]), ALU.subtract
                              ).then_inc(S["b_glo"], 1)

        def pe_by(pe, t):
            p = own_bank(pe, "B_Y", t)
            pe.wait_ge(S["b_glo"], t + 1)
            if t == 0:
                pe.wait_ge(S["dve_e2"], 1)
                pe.wait_ge(S["dve_b2"], 1)
            e = expert(pe, t)
            pe.matmul(p[:], sel[:], pick(b2e[:], e), start=True, stop=False)
            for j, (g, w) in enumerate(split3([gT[t % 2][:, h, :] for h in range(2)],
                                              [pick(e2[:, h], e) for h in range(2)])):
                mm = pe.matmul(p[:], g, w, start=False, stop=j == 2)
            mm.then_inc(S["b_y"], 1)

        def dve_by(dve, t):
            dve.wait_ge(S["b_y"], t + 1)
            r = rowB[t % NROW][:, 0:D]
            dve.tensor_tensor(r, of("B_Y", t)[:], r, ALU.add).then_inc(S["b_out"], 1)

        def pool_by(pool, t):
            pool.wait_ge(S["b_out"], t + 1)
            r = rowB[t % NROW]
            nc.gpsimd.indirect_dma_start(
                out=out, out_offset=bass.IndirectOffsetOnAxis(ap=r[:, D + 2:D + 3].bitcast(U32), axis=0),
                in_=r[:, 0:D], in_offset=None, bounds_check=N - 1, oob_is_err=False).then_inc(st_out[t % NROW], 16)

        parts = {
            "SETUP": {"sp": sp_setup, "pool": pool_setup, "dve": dve_setup},
            "XLOAD": {"sp": sp_xload},
            "KP": {"pe": pe_kp, "act": act_kp, "dve": dve_kp},
            "KSTORE": {"sp": sp_kstore},
            "CONV_WQ": {"act": act_conv_wq, "dve": dve_conv_wq},
            "CONV_W12": {"act": act_conv_w12, "dve": dve_conv_w12, "pool": pool_conv_w12},
            "KLOAD": {"sp": sp_kload},
            "VP": {"pe": pe_vp, "dve": dve_vp, "act": act_vp, "sp": sp_vstore},
            "VLOAD": {"sp": sp_vload},
            "XSTAT": {"dve": dve_xstat},
            "XT": {"pe": pe_xT, "act": act_xT, "dve": dve_xT, "pool": pool_xT},
            "Q": {"pe": pe_q, "act": act_q, "dve": dve_q},
            "S": {"pe": pe_s, "dve": dve_s, "act": act_s},
            "EXP": {"act": act_soft},
            "SUM": {"dve": dve_sum, "pool": pool_soft},
            "PT": {"pe": pe_pt, "act": act_pt, "dve": dve_pt},
            "AV": {"pe": pe_av, "act": act_av, "dve": dve_av},
            "H": {"pe": pe_h, "act": act_h},
            "HLO": {"dve": dve_h},
            "YA": {"pe": pe_ya},
            "Y": {"pe": pe_y, "dve": dve_y},
            "X2STAT": {"dve": dve_x2stat},
            "XTT": {"act": act_xt},
            "TT": {"pe": pe_tt, "act": act_tt, "dve": dve_tt},
            "L": {"pe": pe_l, "act": act_l},
            "ROWTAIL": {"dve": dve_rowtail},
            "DRIP": {"dve": lambda dve, n: drip(n)},
            "DRAIN": {"dve": lambda dve: drain()},
            "LT": {"pe": pe_lt, "dve": dve_lt},
            "RK": {"pe": pe_rk, "dve": dve_rk},
            "SCAT": {"pool": pool_scat},
            "E1_LOAD": {"sp": sp_e1load},
            "E2_LOAD": {"sp": sp_e2load},
            "E2_CONV": {"act": act_e2conv, "dve": dve_e2conv},
            "B1": {"pe": pe_b1, "dve": dve_b1},
            "TABLE": {"pe": pe_table, "dve": dve_table, "pool": pool_table},
            "B2_LOAD": {"sp": sp_b2load},
            "B2_CONV": {"act": act_b2conv, "dve": dve_b2conv},
            "B_X": {"sp": sp_bload, "dve": dve_bx},
            "B_XT": {"pe": pe_bx, "act": act_bx},
            "B_H": {"pe": pe_bh, "act": act_bh},
            "B_G": {"pe": pe_bg, "act": act_bg, "dve": dve_bg},
            "B_Y": {"pe": pe_by, "dve": dve_by, "pool": pool_by},
        }

        def walk(eng, who):
            for kind, *i in sched:
                if who in parts[kind]:
                    parts[kind][who](eng, *i)
                if who == "dve":
                    drip(DRIP.get(kind, 0))

        block = ctx.enter_context(nc.Block())

        @block.sync
        def _(sp):
            walk(sp, "sp")
            for i in range(NROW):
                sp.wait_ge(st_out[i], 16 * len(range(i, NT, NROW)))

        @block.gpsimd
        def _(pool):
            walk(pool, "pool")

        @block.scalar
        def _(act):
            walk(act, "act")

        @block.vector
        def _(dve):
            walk(dve, "dve")

        @block.tensor
        def _(pe):
            walk(pe, "pe")


def kernel(**inputs):
    import numpy as np
    import concourse.bacc as _bacc
    from concourse import mybir as _mybir
    from concourse.bass_utils import run_bass_kernel_spmd as _run

    a = {k: np.asarray(v) for k, v in inputs.items()}

    def chunks(w, k):
        return w.reshape(k, P, -1).transpose(1, 0, 2)

    p = np.arange(P)
    f = np.float32
    dev = {
        "x": a["x"].reshape(N, D),
        "ctxT": chunks(a["ctx_768"].transpose(2, 0, 1).reshape(TD, NB * M), KT),
        "Wq": chunks(a["L0_xattn_Wq"], KD).reshape(P, -1),
        "Wk": chunks(a["L0_xattn_Wk"], KT),
        "Wv": chunks(a["L0_xattn_Wv"], KT),
        "W1": chunks(a["L0_xattn_W1"], KD).reshape(P, -1),
        "W2": chunks(a["L0_xattn_W2"], MF).reshape(P, -1),
        "bq": a["L0_xattn_bq"].reshape(KD, P).T,
        "bk": a["L0_xattn_bk"].reshape(KD, P).T,
        "bv": a["L0_xattn_bv"].reshape(1, D),
        "b1": a["L0_xattn_b1"].reshape(MF, P).T,
        "b2": a["L0_xattn_b2"].reshape(1, D),
        "WgT": chunks(a["L0_ffn_Wg"].T, KD).reshape(P, -1),
        "lns": chunks(a["L0_ffn_ln_scale"].T, KD),
        "lnb": chunks(a["L0_ffn_ln_bias"].T, KD),
        "E1": a["L0_ffn_W1"].reshape(NE, KD, P, EH).transpose(2, 1, 0, 3),
        "Eb1": a["L0_ffn_b1"].reshape(1, NE, EH),
        "E2": a["L0_ffn_W2"].transpose(1, 0, 2),
        "Eb2": a["L0_ffn_b2"].reshape(1, NE, D),
        "ident": np.eye(P, dtype=f),
        "masks": np.concatenate([(p[:, None] < p[None, :]).astype(f), np.ones((P, P), f),
                                 np.isin(p[:, None], [0, B2LO]).repeat(P, 1).astype(f)], 1),
        "prio": np.broadcast_to((NE - np.arange(NE)).astype(f), (P, SUB, NE)),
        "base": np.broadcast_to((REG * np.arange(NE)).astype(f), (P, SUB, NE)),
        "ids": (p[:, None] + P * np.arange(N // P)[None, :]).astype(np.uint32),
        "padoff": (p[:, None] + REG * np.arange(NE)[None, :]).astype(f),
        "jt": np.broadcast_to(np.arange(NT, dtype=f)[None, :, None], (1, NT, NE)),
    }
    pad = np.zeros((P, ROW), f)
    pad[:, D + 2] = np.full(P, N, np.uint32).view(f)
    dev["padrow"] = pad
    dev = {k: np.ascontiguousarray(v) for k, v in dev.items()}

    nc = _bacc.Bacc("TRN2", target_bir_lowering=False, num_devices=1, dynamic_dma_scratch_size=8192)
    A = {k: nc.dram_tensor(f"in_{k}", v.shape, _mybir.dt.from_np(v.dtype), kind="ExternalInput").ap()
         for k, v in dev.items()}
    out = nc.dram_tensor("out_0", (N, D), F32, kind="ExternalOutput").ap()
    xattn_moe_kernel(nc, A, out)
    r = _run(nc, [{f"in_{k}": v for k, v in dev.items()}], core_ids=[0])
    return r.results[0]["out_0"].reshape(NB, TOK, D)
```

```python
from contextlib import ExitStack

import concourse.bass as bass
from concourse import mybir

F32 = mybir.dt.float32
F32R = mybir.dt.float32r
BF16 = mybir.dt.bfloat16
U32 = mybir.dt.uint32
I32 = mybir.dt.int32
ALU = mybir.AluOpType
ACT = mybir.ActivationFunctionType
AX = mybir.AxisListType.X

P = 128
D = 512
KD = D // P
TD = 384
KT = TD // P
NB = 4
TOK = 2048
M = 77
HEADS = 16
HD = D // HEADS
HG = P // HD
SCALE = float(HD) ** -0.5
F = 1024
MF = F // P
NE = 8
EH = 128
EPS = 1e-5
N = NB * TOK
BLK = 512
SUB = BLK // P
NBLK = N // BLK
BPB = TOK // BLK
SC = HG * M
CH = [103, 103, 102]
CO = [0, 103, 206]
NC = len(CH)
SLOTS = 8
ROW = 516
REG = N + P
NT = N // P + NE - 1
NROW = 14
PIECES = []
for _h in range(HG):
    for _c in range(NC):
        _a, _z = max(M * _h, CO[_c]), min(M * _h + M, CO[_c] + CH[_c])
        if _a < _z:
            PIECES.append((_c, _a - CO[_c], _a - M * _h, _z - _a, _h))


def xattn_moe_kernel(nc, A, out):
    region = nc.dram_tensor("region", [NE * REG + P, ROW], F32).ap()
    k_parts = nc.dram_tensor("k_parts", [NB, 2, KD, P, M], F32).ap()
    v_parts = nc.dram_tensor("v_parts", [NB, 2, M, D], F32).ap()

    end = [nc.sbuf_base]

    def at(name, shape, dt, offset):
        return nc.alloc_sbuf_tensor_at(name, shape, dt, offset=offset)

    def size(shape, dt):
        n = 2 if dt == BF16 else 4
        for s in shape[1:]:
            n *= s
        return (n + 31) // 32 * 32

    def sb(name, shape, dt=F32):
        o = (end[0] + 31) // 32 * 32
        end[0] = o + size(shape, dt)
        return at(name, shape, dt, o), o

    wq, wq_at = sb("wq", [P, 2, KD, D], F32R)
    w1, w1_at = sb("w1", [P, 2, KD, F], F32R)
    w2, w2_at = sb("w2", [P, 2, MF, D], F32R)
    wg, _ = sb("wg", [P, KD, 2, NE], F32R)
    kbd, kbd_at = sb("kbd", [P, 2, KD, SC], F32R)
    vbd, _ = sb("vbd", [P, 2, KD, NC, P], F32R)
    rows = [sb(f"rows{i}", [P, SUB, ROW]) for i in range(2)]
    rows_at = [r[1] for r in rows]
    rows = [r[0] for r in rows]
    actA, actA_at = sb("actA", [P, 2, KD, BLK], F32R)
    actQ, _ = sb("actQ", [P, 2, KD, BLK], F32R)
    actH, actH_at = sb("actH", [P, 2, SLOTS, BLK], F32R)
    E, E_at = sb("E", [P, KD, SUB, SC])
    xn = [sb(f"xn{i}", [P, D]) for i in range(2)]
    xn_at = xn[0][1]
    xn = [t[0] for t in xn]
    htmp = [sb(f"htmp{i}", [P, BLK]) for i in range(2)]
    htmp_at = htmp[0][1]
    htmp = [t[0] for t in htmp]
    b2bc, _ = sb("b2bc", [P, D])
    ident, _ = sb("ident", [P, P])
    tri, _ = sb("tri", [P, P], BF16)
    ones, _ = sb("ones", [P, P], BF16)
    prio, _ = sb("prio", [P, SUB, NE])
    base, _ = sb("base", [P, SUB, NE])
    ids, _ = sb("ids", [P, N // P], U32)
    bq, _ = sb("bq", [P, KD])
    bk, _ = sb("bk", [P, KD])
    bks, _ = sb("bks", [P, KD])
    b1, _ = sb("b1", [P, MF])
    mx, _ = sb("mx", [P, KD * SUB, HG])
    sm, _ = sb("sm", [P, KD, SUB * HG])
    rc, _ = sb("rc", [P, KD, SUB * HG])
    bn, _ = sb("bn", [P, SUB, 6])
    bn2, _ = sb("bn2", [P, SUB, 6])
    mv, _ = sb("mv", [P, SUB, 2])
    mvx, _ = sb("mvx", [P, SUB, 2])
    nw, _ = sb("nw", [P, 3, SUB])
    rx, _ = sb("rx", [P, SUB])
    r1, _ = sb("r1", [P, SUB])
    r2, _ = sb("r2", [P, SUB])
    nmr, _ = sb("nmr", [P, SUB])
    tB, _ = sb("tB", [P, SUB])
    lg, _ = sb("lg", [P, SUB, NE])
    lw, _ = sb("lw", [P, SUB, NE])
    lm, _ = sb("lm", [P, SUB])
    oh, _ = sb("oh", [P, SUB, NE], BF16)
    cum, _ = sb("cum", [P, NE], BF16)
    rk, _ = sb("rk", [P, SUB, NE])
    posf, _ = sb("posf", [P, SUB])
    pos = [sb(f"pos{i}", [P, SUB], U32)[0] for i in range(2)]
    assert end[0] <= nc.sbuf_usable_end, (end[0], nc.sbuf_usable_end)
    xt = lambda s: E[:, s, :, :].rearrange("p a c -> p (a c)")[:, 0:D]
    lgT = E[0:2 * NE, 0, :, :].rearrange("p a c -> p (a c)")[:, D + 64:D + 64 + BLK]

    o = [E_at]

    def staged(name, shape, dt=F32):
        o[0] += size(shape, dt)
        return at(name, shape, dt, o[0] - size(shape, dt))

    wk_raw = staged("wk_raw", [P, KT, D])
    wv_raw = staged("wv_raw", [P, KT, D])
    ctxT = staged("ctxT", [P, KT, NB * M])
    c_raw = staged("c_raw", [P, 2 * P])
    wg_raw = staged("wg_raw", [P, KD * NE])
    assert o[0] <= E_at + size([P, KD, SUB, SC], F32)
    wq_raw = at("wq_raw", [P, KD * D], F32, actH_at)
    w1_raw = at("w1_raw", [P, KD * F], F32, actH_at + 4 * KD * D)
    w2_raw = [at("w2_raw0", [P, MF * D // 2], F32, actH_at + 4 * KD * D + 4 * KD * F),
              at("w2_raw1", [P, MF * D // 2], F32, rows_at[1])]
    o[0] = w2_at
    k_hl = staged("k_hl", [P, 2, KD, NB * M], F32R)
    k_f = staged("k_f", [P, KD, NB * M])
    v_hl = [staged(f"v_hl{i}", [M, 2, D], F32R) for i in range(2)]
    v_f = [staged(f"v_f{i}", [M, D]) for i in range(2)]
    bvbc = staged("bvbc", [M, D])
    assert o[0] <= w2_at + size([P, 2, MF, D], F32)

    e1 = at("e1", [P, KD, NE, EH], F32, wq_at)
    e2_raw = at("e2_raw", [P, NE, D], F32, actA_at)
    e2 = at("e2", [P, 2, NE, D], F32R, w1_at)
    b2e = at("b2e", [P, NE, D], F32, kbd_at)
    b1e = at("b1e", [P, NE, EH], F32, kbd_at + 4 * NE * D)
    assert 4 * NE * (D + EH) <= size([P, 2, KD, SC], F32) + size([P, 2, KD, NC, P], F32)
    o = [w2_at]

    def sb2(name, shape, dt=F32):
        o[0] += size(shape, dt)
        return at(name, shape, dt, o[0] - size(shape, dt))

    rowB = [sb2(f"rowB{i}", [P, ROW]) for i in range(NROW)]
    assert o[0] <= w2_at + size([P, 2, MF, D], F32)
    o[0] = E_at
    xh = [sb2(f"xh{i}", [P, D]) for i in range(2)]
    xhT = [sb2(f"xhT{i}", [P, KD, P]) for i in range(2)]
    hb = [sb2(f"hb{i}", [P, EH]) for i in range(2)]
    gl = [sb2(f"gl{i}", [P, EH]) for i in range(2)]
    gT = [sb2(f"gT{i}", [P, 2, P], F32R) for i in range(2)]
    assert o[0] <= E_at + size([P, KD, SUB, SC], F32)
    o[0] = rows_at[0]
    lns = sb2("lns", [P, KD, NE])
    lnb = sb2("lnb", [P, KD, NE])
    padrow = sb2("padrow", [P, ROW])
    regions = sb2("regions", [P, NE])
    padf = sb2("padf", [P, NE])
    padi = sb2("padi", [P, NE], I32)
    cnt = sb2("cnt", [P, NE])
    cti = sb2("cti", [P, NE], I32)
    ctl = sb2("ctl", [P, NE])
    cinc = sb2("cinc", [P, NE])
    stp = sb2("stp", [P, NE])
    ex = sb2("ex", [1, NT])
    rw = sb2("rw", [1, NT])
    exi = sb2("exi", [1, NT], I32)
    rwi = sb2("rwi", [1, NT], I32)
    assert o[0] <= rows_at[0] + size([P, SUB, ROW], F32)
    jt = at("jt", [1, NT, NE], F32, xn_at)
    ge = at("ge", [1, NT, NE], F32, htmp_at)

    with ExitStack() as ctx:
        bank = [ctx.enter_context(nc.psum_tensor(f"bank{i}", [P, 512], F32)) for i in range(8)]

        def sem(name):
            return ctx.enter_context(nc.semaphore(name))

        L = {n: sem(f"ld_{n}") for n in (
            "first", "consts", "wk", "wv", "ctx", "wq", "w1", "w2a", "w2b", "e1", "e2", "eb", "ln", "tab", "pad0")}
        ld_x = [[sem(f"ld_x{i}_{s}") for s in range(SUB)] for i in range(2)]
        st_k, st_v, ld_k, ld_v = sem("st_k"), sem("st_v0"), sem("ld_k"), sem("ld_v")
        st_vs = [st_v, sem("st_v1")]
        scat = [[sem(f"scat{i}_{s}") for s in range(SUB)] for i in range(2)]
        st_pad = sem("st_pad")
        ld_row = [sem(f"ld_row{i}") for i in range(NROW)]
        st_out = [sem(f"st_out{i}") for i in range(NROW)]
        dve_chain = sem("dve_chain")
        S = {n: sem(n) for n in (
            "dve_bks pe_k act_kf act_k dve_k pe_v dve_vf act_v dve_v pool_zero dve_const "
            "act_wq pool_wq act_w1 pool_w1 dve_w2h w2_lo "
            "dve_xn pool_xb pe_xT act_xT dve_xT pe_q act_q dve_q pe_s dve_max dve_sub act_es act_exp dve_rc pool_p "
            "pe_pt act_pt dve_pt pe_av act_o dve_o pe_h act_h act_hh dve_h pe_y dve_x2 dve_s2 act_xt dve_row "
            "pe_tt act_tt dve_tt pe_l act_l pe_lt dve_lg dve_oh pe_rk dve_rk dve_cum dve_pos "
            "pe_cnt dve_cnt dve_pad dve_tab dve_e1 pe_b1 dve_b1 act_e2 dve_e2 "
            "b_xh b_xT b_xTs b_h b_hb b_gl b_g b_ghi b_glo b_y b_out").split()}
        pe_k, pe_v = S["pe_k"], S["pe_v"]
        b_xb = [sem("b_xb0"), sem("b_xb1")]

        sched = []

        def step(kind, *i):
            sched.append((kind, *i))

        def attention_tail(b):
            for c in range(NC):
                step("PT", b, 0, c)
            step("SUM", b, KD - 1)
            if b:
                step("X2STAT", b - 1)
            for g in range(KD):
                if g + 1 < KD:
                    for c in range(NC):
                        step("PT", b, g + 1, c)
                if b and g == KD - 1:
                    for s in range(2):
                        step("XTT", b - 1, s)
                step("AV", b, g)

        step("SETUP")
        step("XLOAD", 0)
        step("XSTAT", 0)
        for m in range(KD):
            step("KP", m)
        step("DRAIN")
        step("KSTORE")
        step("CONV_WQ")
        for i in range(2):
            step("VP", i)
            step("VSTORE", i)
        step("W1_LOAD")
        for s in range(SUB):
            step("XT", 0, s)
        for i in range(2, NB):
            step("VP", i)
        step("KLOAD", 0)
        for i in range(2, NB):
            step("VSTORE", i)
        step("W2_LOAD")
        step("VLOAD", 0)
        for m in range(KD):
            step("Q", 0, m)
            if m in (1, 2):
                step("CONV_W1", m - 1)
        step("CONSTS")
        for g in range(KD):
            for s in range(SUB):
                step("S", 0, g, s)
            if g == 2:
                step("CONV_W2", 0)
            step("EXP", 0, g)
            if g:
                step("SUM", 0, g - 1)
        step("CONV_W2", 1)
        step("ZERO_ROWS")
        step("XLOAD", 1)
        for b in range(NBLK):
            last = b == NBLK - 1
            if (b + 1) % BPB == 0 and not last:
                step("KLOAD", (b + 1) // BPB)
            attention_tail(b)
            if (b + 1) % BPB == 0 and not last:
                step("VLOAD", (b + 1) // BPB)
            if last:
                step("EB_LOAD")
            for m in range(MF):
                if b and m == 0:
                    for s in range(2, SUB):
                        step("XTT", b - 1, s)
                    step("DRAIN")
                step("H", b, m)
                if b and m == 3:
                    step("RK", b - 1)
                if not (b and m == 2):
                    step("HLO", b, m)
                if b and m == 0:
                    for s in range(SUB):
                        step("TT", b - 1, s)
                    step("ROWTAIL", b - 1)
                    step("DRIP", 2)
                if b and m == 1:
                    step("L", b - 1)
                if b and m == 2:
                    step("LT", b - 1)
                    step("HLO", b, m)
                if b and m == 3:
                    step("DRAIN")
                    step("SCAT", b - 1)
                    if not last:
                        step("XLOAD", b + 1)
                if m == MF - 3 and not last:
                    step("XSTAT", b + 1)
                    step("DRIP", 3)
            if last:
                step("E2_LOAD")
                for s in range(SUB):
                    if s == 2:
                        step("B1")
                    step("YA", b, s)
                    step("Y", b, s)
                    if s == 0:
                        step("E2_CONV")
            else:
                step("DRAIN")
                step("YA", b, 0)
                step("Y", b, 0)
                for s in range(2):
                    step("XT", b + 1, s)
                step("YA", b, 1)
                for s in range(2, SUB):
                    step("XT", b + 1, s)
                step("Y", b, 1)
                step("Q", b + 1, 0)
                step("Q", b + 1, 1)
                for g, (first, y) in enumerate((("YA", 2), ("Y", 2), ("YA", 3), ("Y", 3))):
                    for s in range(SUB):
                        step("S", b + 1, g, s)
                    step("EXP", b + 1, g)
                    if g:
                        step("SUM", b + 1, g - 1)
                    step(first, b, y)
                    if g + 2 < KD:
                        step("Q", b + 1, g + 2)
                if b + 2 == NBLK:
                    step("E1_LOAD")
        step("X2STAT", NBLK - 1)
        step("DRAIN")
        for s in range(SUB):
            step("XTT", NBLK - 1, s)
        for s in range(SUB):
            step("TT", NBLK - 1, s)
        step("ROWTAIL", NBLK - 1)
        step("L", NBLK - 1)
        step("DRIP", 10)
        step("LT", NBLK - 1)
        step("RK", NBLK - 1)
        step("PADS")
        step("DRAIN")
        step("SCAT", NBLK - 1)
        step("TABLE")
        for t in range(-5, NT):
            for kind, ahead in (("B_Y", 0), ("B_G", 1), ("B_X", 5), ("B_XT", 4), ("B_H", 3)):
                if 0 <= t + ahead < NT:
                    step(kind, t + ahead)

        ON_ACT = (0, 2)
        ON_DVE = tuple(g for g in range(KD) if g not in ON_ACT)

        def score_done(b, g, s):
            mine, name = (ON_ACT, "act_es") if g in ON_ACT else (ON_DVE, "dve_sub")
            return S[name], SUB * (len(mine) * b + mine.index(g)) + s + 1

        freed = {
            "KP": lambda m: (S["act_kf"], m + 1),
            "VP": lambda i: (S["dve_vf"], i + 1),
            "XT": lambda b, s: (S["dve_xT"], SUB * b + s + 1),
            "Q": lambda b, m: (S["dve_q"], KD * b + m + 1),
            "S": lambda b, g, s: score_done(b, g, s),
            "PT": lambda b, g, c: (S["dve_pt"], NC * (KD * b + g) + c + 1),
            "AV": lambda b, g: (S["dve_o"], KD * b + g + 1),
            "H": lambda b, m: (S["act_hh"], MF * b + m + 1),
            "YA": lambda b, s: (S["dve_x2"], SUB * b + s + 1),
            "TT": lambda b, s: (S["dve_tt"], SUB * b + s + 1),
            "L": lambda b: (S["act_l"], b + 1),
            "LT": lambda b: (S["dve_lg"], b + 1),
            "RK": lambda b: (S["dve_rk"], b + 1),
            "PADS": lambda: (S["dve_cnt"], 1),
            "B1": lambda: (S["dve_b1"], 1),
            "B_XT": lambda t: (S["b_xTs"], t + 1),
            "B_H": lambda t: (S["b_hb"], t + 1),
            "B_G": lambda t: (S["b_glo"], t + 1),
            "B_Y": lambda t: (S["b_out"], t + 1),
        }
        bank_of, before, users = {}, {}, [None] * 8
        n = 0
        for kind, *i in sched:
            if kind in freed:
                for _ in range(2 if kind == "B1" else 1):
                    key = (kind, *i)
                    bank_of.setdefault(key, []).append(n % 8)
                    if users[n % 8] is not None:
                        before.setdefault(key, []).append(users[n % 8])
                    users[n % 8] = freed[kind](*i)
                    n += 1

        def own_bank(eng, *key):
            for s, v in before.get(key, []):
                eng.wait_ge(s, v)
            return bank[bank_of[key][0]]

        def of(*key):
            return bank[bank_of[key][0]]

        def split3(a, b):
            return ((a[0], b[0]), (a[0], b[1]), (a[1], b[0]))

        def f32(ap):
            return ap.bitcast(F32)

        counts = {"dve": 0}

        def dve_link(eng, ins):
            counts["dve"] += 1
            ins.then_inc(dve_chain, 1)
            eng.wait_ge(dve_chain, counts["dve"])

        chains = []
        DRIP = {"KP": 5, "Q": 2, "PT": 2, "AV": 2, "HLO": 12, "Y": 1, "TT": 1}

        def drip(n):
            while chains and n > 0:
                n -= 1
                if next(chains[0], "end") == "end":
                    chains.pop(0)

        def drain():
            while chains:
                drip(1)

        def issued(ins):
            counts["dve"] += 1
            ins.then_inc(dve_chain, 1)
            return counts["dve"]

        def grouped(ap, n):
            return ap.rearrange("p (h k) -> p h k", h=n)

        def spread(ap, n):
            return ap.unsqueeze(2).to_broadcast([ap.shape[0], ap.shape[1], n])

        def sp_setup(sp):
            sp.dma_start(ctxT[:], A["ctxT"]).then_inc(L["ctx"], 16)
            sp.dma_start(wk_raw[:], A["Wk"]).then_inc(L["wk"], 16)
            for dst, src in ((bk[:], A["bk"]), (ident[:], A["ident"]), (bvbc[:], A["bv"].to_broadcast([M, D]))):
                sp.dma_start(dst, src).then_inc(L["first"], 16)

        def sp_setup2(sp):
            sp.dma_start(wv_raw[:], A["Wv"]).then_inc(L["wv"], 16)
            sp.dma_start(wq_raw[:], A["Wq"]).then_inc(L["wq"], 16)
            for dst, src in ((bq[:], A["bq"]), (b2bc[:], A["b2"].to_broadcast([P, D])), (c_raw[:], A["masks"]),
                             (wg_raw[:], A["WgT"]), (prio[:], A["prio"]), (base[:], A["base"]), (ids[:], A["ids"]),
                             (b1[:], A["b1"])):
                sp.dma_start(dst, src).then_inc(L["consts"], 16)

        NFIRST, NSMALL = 3, 8

        def sp_w1load(sp):
            sp.dma_start(w1_raw[:], A["W1"]).then_inc(L["w1"], 16)

        def sp_w2load(sp):
            sp.dma_start(w2_raw[0][:], A["W2"][:, 0:MF * D // 2]).then_inc(L["w2a"], 16)
            sp.dma_start(w2_raw[1][:], A["W2"][:, MF * D // 2:]).then_inc(L["w2b"], 16)

        def sp_xload(sp, b):
            if b == 1:
                sp.wait_ge(S["pool_zero"], 4)
            for s in range(SUB):
                if b >= 2:
                    sp.wait_ge(scat[b % 2][s], 16 * (b // 2))
                src = A["x"][b * BLK + P * s:b * BLK + P * s + P, :]
                sp.dma_start(rows[b % 2][:, s, 0:D], src).then_inc(ld_x[b % 2][s], 16)
            if b == 0:
                sp_setup2(sp)

        def sp_kstore(sp):
            sp.wait_ge(S["act_k"], KD)
            sp.wait_ge(S["dve_k"], KD)
            for h in range(2):
                for i in range(NB):
                    sp.dma_start(k_parts[i, h].rearrange("g p k -> p g k"),
                                 f32(k_hl[:, h, :, M * i:M * i + M])).then_inc(st_k, 16)

        def sp_kload(sp, i):
            if i == 0:
                sp.wait_ge(st_k, 16 * 2 * NB)
                sp.wait_ge(S["pool_zero"], 1)
            else:
                sp.wait_ge(S["pe_s"], KD * SUB * BPB * i)
            for h in range(HG):
                for g in range(KD):
                    sp.dma_start(f32(kbd[HD * h:HD * h + HD, :, g, M * h:M * h + M]),
                                 k_parts[i, :, g, HD * h:HD * h + HD, :].rearrange("s p k -> p s k")
                                 ).then_inc(ld_k, 16)

        def sp_vload(sp, i):
            if i == 0:
                for n_, s_ in enumerate(st_vs):
                    sp.wait_ge(s_, 16 * (NB // 2))
                sp.wait_ge(S["pool_zero"], 2)
            else:
                sp.wait_ge(S["pe_av"], KD * BPB * i)
            for c, r, k, m, h in PIECES:
                for part in range(2):
                    src = v_parts[i, part, k:k + m, :].rearrange("k (g h f) -> k g h f", g=KD, h=HG)[:, :, h, :]
                    sp.dma_start(f32(vbd[r:r + m, part, :, c, HD * h:HD * h + HD]), src).then_inc(ld_v, 16)

        KLOADS, VLOADS = HG * KD, 2 * len(PIECES)

        def sp_vstore(sp, i):
            sp.wait_ge(S["act_v"], i + 1)
            sp.wait_ge(S["dve_v"], i + 1)
            sp.dma_start(v_parts[i].rearrange("s k f -> k s f"), f32(v_hl[i % 2][:])).then_inc(st_vs[i % 2], 16)

        def sp_e1load(sp):
            sp.wait_ge(S["pe_q"], KD * NBLK)
            sp.dma_start(e1[:], A["E1"]).then_inc(L["e1"], 16)

        def sp_ebload(sp):
            sp.wait_ge(S["pe_s"], KD * SUB * NBLK)
            sp.wait_ge(S["pe_av"], KD * NBLK)
            sp.dma_start(b1e[:], A["Eb1"].to_broadcast([P, NE, EH])).then_inc(L["eb"], 16)
            sp.dma_start(b2e[:], A["Eb2"].to_broadcast([P, NE, D])).then_inc(L["eb"], 16)

        def sp_e2load(sp):
            sp.wait_ge(S["pe_h"], MF * NBLK)
            sp.dma_start(e2_raw[:], A["E2"]).then_inc(L["e2"], 16)
            for s in range(SUB):
                sp.wait_ge(scat[0][s], 16 * (NBLK // 2))
            sp.wait_ge(S["pe_xT"], SUB * NBLK)
            sp.dma_start(lns[:], A["lns"]).then_inc(L["ln"], 16)
            sp.dma_start(lnb[:], A["lnb"]).then_inc(L["ln"], 16)
            sp.dma_start(padrow[:], A["padrow"]).then_inc(L["tab"], 16)
            sp.dma_start(regions[:], A["regions"]).then_inc(L["tab"], 16)
            sp.dma_start(jt[:], A["jt"]).then_inc(L["tab"], 16)
            sp.wait_ge(L["tab"], 48)
            sp.dma_start(region[NE * REG:NE * REG + P, :], padrow[:]).then_inc(L["pad0"], 16)

        def pool_setup(pool):
            z = lambda ap: nc.gpsimd.memset(ap, 0.0)
            z(f32(kbd[:])).then_inc(S["pool_zero"], 1)
            z(f32(vbd[:])).then_inc(S["pool_zero"], 1)
            z(rows[0][:, :, D:ROW]).then_inc(S["pool_zero"], 1)

        def dve_setup(dve):
            dve.memset(cum[:], 0.0)
            dve.wait_ge(L["first"], 16 * NFIRST)
            dve.tensor_scalar(bks[:], bk[:], SCALE, None, ALU.mult).then_inc(S["dve_bks"], 1)

        def dve_consts(dve):
            dve.wait_ge(L["consts"], 16 * NSMALL)
            dve.tensor_copy(tri[:], c_raw[:, 0:P])
            dve.tensor_copy(ones[:], c_raw[:, P:2 * P])
            wgr = wg_raw[:].rearrange("p (k e) -> p k e", e=NE)
            dve_link(dve, dve.tensor_copy(wg[:, :, 0, :], wgr))
            dve.tensor_tensor(wg[:, :, 1, :], wgr, f32(wg[:, :, 0, :]), ALU.subtract).then_inc(S["dve_const"], 1)

        def pe_kp(pe, m):
            p = own_bank(pe, "KP", m)
            if m == 0:
                pe.wait_ge(L["ctx"], 16)
                pe.wait_ge(L["wk"], 16)
            for k in range(KT):
                mm = pe.matmul(p[:, 0:NB * M], wk_raw[:, k, P * m:P * m + P], ctxT[:, k, :],
                               start=k == 0, stop=k == KT - 1)
            mm.then_inc(pe_k, 1)

        def act_kp(act, m):
            if m == 0:
                act.wait_ge(S["dve_bks"], 1)
            act.wait_ge(pe_k, m + 1)
            act.activation(k_f[:, m, :], of("KP", m)[:, 0:NB * M], ACT.Identity, bias=bks[:, m:m + 1], scale=SCALE
                           ).then_inc(S["act_kf"], 1)
            act.wait_ge(S["act_kf"], m + 1)
            act.activation(k_hl[:, 0, m, :], k_f[:, m, :], ACT.Identity).then_inc(S["act_k"], 1)

        def dve_kp(dve, m):
            dve.wait_ge(S["act_k"], m + 1)
            dve.tensor_tensor(k_hl[:, 1, m, :], k_f[:, m, :], f32(k_hl[:, 0, m, :]), ALU.subtract
                              ).then_inc(S["dve_k"], 1)

        def pe_vp(pe, i):
            p = own_bank(pe, "VP", i)
            if i == 0:
                pe.wait_ge(L["wv"], 16)
            for k in range(KT):
                mm = pe.matmul(p[0:M, :], ctxT[:, k, M * i:M * i + M], wv_raw[:, k, :],
                               start=k == 0, stop=k == KT - 1)
            mm.then_inc(pe_v, 1)

        def dve_vp(dve, i):
            dve.wait_ge(pe_v, i + 1)
            if i == 0:
                dve.wait_ge(L["first"], 16 * NFIRST)
            if i >= 2:
                dve.wait_ge(st_vs[i % 2], 16 * (i // 2))
            dve.tensor_tensor(v_f[i % 2][:], of("VP", i)[0:M, :], bvbc[:], ALU.add).then_inc(S["dve_vf"], 1)
            dve.wait_ge(S["act_v"], i + 1)
            dve.tensor_tensor(v_hl[i % 2][:, 1], v_f[i % 2][:], f32(v_hl[i % 2][:, 0]),
                              ALU.subtract).then_inc(S["dve_v"], 1)

        def act_vp(act, i):
            act.wait_ge(S["dve_vf"], i + 1)
            if i >= 2:
                act.wait_ge(st_vs[i % 2], 16 * (i // 2))
            act.activation(v_hl[i % 2][:, 0], v_f[i % 2][:], ACT.Identity).then_inc(S["act_v"], 1)

        def act_conv_wq(act):
            act.wait_ge(L["wq"], 16)
            act.activation(wq[:, 0].rearrange("p k n -> p (k n)"), wq_raw[:], ACT.Identity).then_inc(S["act_wq"], 1)

        def pool_conv_wq(pool):
            pool.wait_ge(S["act_wq"], 1)
            hi, lo = (wq[:, h].rearrange("p k n -> p (k n)") for h in range(2))
            pool.tensor_tensor(lo, wq_raw[:], f32(hi), ALU.subtract).then_inc(S["pool_wq"], 1)

        def w1_half(h, i):
            n = KD * F // 2
            return w1[:, h].rearrange("p k n -> p (k n)")[:, n * i:n * i + n], w1_raw[:, n * i:n * i + n]

        def act_conv_w1(act, i):
            act.wait_ge(L["w1"], 16)
            hi, raw = w1_half(0, i)
            act.activation(hi, raw, ACT.Identity).then_inc(S["act_w1"], 1)

        def pool_conv_w1(pool, i):
            pool.wait_ge(S["act_w1"], i + 1)
            lo, raw = w1_half(1, i)
            pool.tensor_tensor(lo, raw, f32(w1_half(0, i)[0]), ALU.subtract).then_inc(S["pool_w1"], 1)

        def w2_half(h, i):
            return w2[:, h, MF // 2 * i:MF // 2 * (i + 1)].rearrange("p k n -> p (k n)")

        def w2_low(eng, i):
            eng.wait_ge(S["dve_w2h"], i + 1)
            eng.tensor_tensor(w2_half(1, i), w2_raw[i][:], f32(w2_half(0, i)), ALU.subtract).then_inc(S["w2_lo"], 1)

        def dve_conv_w2(dve, i):
            if i == 0:
                dve.wait_ge(st_k, 16 * 2 * NB)
                for s_ in st_vs:
                    dve.wait_ge(s_, 16 * (NB // 2))
            dve.wait_ge(L["w2b" if i else "w2a"], 16)
            dve.tensor_copy(w2_half(0, i), w2_raw[i][:]).then_inc(S["dve_w2h"], 1)
            if i == 0:
                w2_low(dve, i)

        def pool_conv_w2(pool, i):
            if i == 1:
                pool.wait_ge(S["w2_lo"], 1)
                w2_low(pool, i)

        def pool_zero_row(pool):
            pool.wait_ge(S["w2_lo"], 2)
            nc.gpsimd.memset(rows[1][:, :, D:ROW], 0.0).then_inc(S["pool_zero"], 1)

        def rsqrt(dve, var, y, n):
            v, t = nw[:, 0, :], nw[:, 1, :]
            steps = [lambda: dve.tensor_scalar(v, var, EPS, None, ALU.add),
                     lambda: dve.tensor_scalar(t.bitcast(I32), v.bitcast(I32), 1, None, ALU.logical_shift_right),
                     lambda: dve.tensor_scalar(y.bitcast(I32), t.bitcast(I32), -1, float(0x5F3759DF),
                                               ALU.mult, ALU.add)]
            steps += [lambda: dve.tensor_tensor(t, y, y, ALU.mult),
                      lambda: dve.scalar_tensor_tensor(t, t, -0.5, v, ALU.mult, ALU.mult),
                      lambda: dve.scalar_tensor_tensor(y, t, 1.5, y, ALU.add, ALU.mult)] * 3
            for f in steps:
                dve.wait_ge(dve_chain, n)
                n = issued(f())
                yield
            return n

        def aggregate(dve, raw, into, n):
            dve.wait_ge(dve_chain, n)
            for s in range(SUB):
                n = issued(dve.bn_aggr(into[:, s, :], raw[:, s, :]))
                yield
            return n

        def dve_xstat(dve, b):
            def chain():
                for s in range(SUB):
                    dve.wait_ge(ld_x[b % 2][s], 16 * (b // 2 + 1))
                    n = issued(dve.bn_stats(bn[:, s, :], rows[b % 2][:, s, 0:D]))
                    yield
                n = yield from aggregate(dve, bn, mvx, n)
                n = yield from rsqrt(dve, mvx[:, :, 1], rx[:], n)
                dve.wait_ge(dve_chain, n)
                for s in range(2):
                    dve_xn(dve, b, s)
                    yield
            chains.append(chain())

        def dve_xn(dve, b, s):
            i = SUB * b + s
            if i >= 2:
                dve.wait_ge(S["pe_xT"], i - 1)
            dve.tensor_scalar(xn[s % 2][:], rows[b % 2][:, s, 0:D], mvx[:, s, 0:1], rx[:, s:s + 1],
                              ALU.subtract, ALU.mult).then_inc(S["dve_xn"], 1)

        def pe_xT(pe, b, s):
            p = own_bank(pe, "XT", b, s)
            if b == 0 and s == 0:
                pe.wait_ge(L["first"], 16 * NFIRST)
            pe.wait_ge(S["dve_xn"], SUB * b + s + 1)
            for k in range(KD):
                mm = pe.transpose(p[:, P * k:P * k + P], xn[s % 2][:, P * k:P * k + P], ident[:])
            mm.then_inc(S["pe_xT"], 1)

        def act_xT(act, b, s):
            act.wait_ge(S["pe_xT"], SUB * b + s + 1)
            act.activation(actA[:, 0, :, P * s:P * s + P], of("XT", b, s)[:].rearrange("p (k t) -> p k t", k=KD),
                           ACT.Identity).then_inc(S["act_xT"], 1)

        def dve_xT(dve, b, s):
            if s == 0:
                drain()
            dve.wait_ge(S["act_xT"], SUB * b + s + 1)
            dve.tensor_tensor(actA[:, 1, :, P * s:P * s + P], of("XT", b, s)[:].rearrange("p (k t) -> p k t", k=KD),
                              f32(actA[:, 0, :, P * s:P * s + P]), ALU.subtract).then_inc(S["dve_xT"], 1)
            if s + 2 < SUB:
                dve_xn(dve, b, s + 2)

        def pool_xT(pool, b, s):
            pool.wait_ge(S["dve_xn"], SUB * b + s + 1)
            if b == 0:
                pool.wait_ge(L["consts"], 16 * NSMALL)
            r = rows[b % 2][:, s, 0:D]
            nc.gpsimd.tensor_tensor(r, r, b2bc[:], ALU.add).then_inc(S["pool_xb"], 1)

        def pe_q(pe, b, m):
            p = own_bank(pe, "Q", b, m)
            if b == 0:
                pe.wait_ge(S["pool_wq"], 1)
            pe.wait_ge(S["dve_xT"], SUB * (b + 1))
            for k in range(KD):
                for j, (w, a) in enumerate(split3([wq[:, h, k, P * m:P * m + P] for h in range(2)],
                                                  [actA[:, h, k, :] for h in range(2)])):
                    mm = pe.matmul(p[:], w, a, start=k == 0 and j == 0, stop=k == KD - 1 and j == 2)
            mm.then_inc(S["pe_q"], 1)

        def act_q(act, b, m):
            act.wait_ge(S["pe_q"], KD * b + m + 1)
            if b == 0 and m == 0:
                act.wait_ge(L["consts"], 16 * NSMALL)
            if b >= 2:
                act.wait_ge(S["pe_l"], b - 1)
            act.activation(actQ[:, 0, m, :], of("Q", b, m)[:], ACT.Identity, bias=bq[:, m:m + 1]
                           ).then_inc(S["act_q"], 1)

        def dve_q(dve, b, m):
            dve.wait_ge(S["act_q"], KD * b + m + 1)
            dve.scalar_tensor_tensor(actQ[:, 1, m, :], of("Q", b, m)[:], bq[:, m:m + 1], f32(actQ[:, 0, m, :]),
                                     ALU.add, ALU.subtract).then_inc(S["dve_q"], 1)

        def pe_s(pe, b, g, s):
            p = own_bank(pe, "S", b, g, s)
            if s == 0:
                pe.wait_ge(S["dve_q"], KD * b + g + 1)
                pe.wait_ge(ld_k, 16 * KLOADS * (b // BPB + 1))
            for j, (q, k) in enumerate(split3([actQ[:, h, g, P * s:P * s + P] for h in range(2)],
                                              [kbd[:, h, g, :] for h in range(2)])):
                mm = pe.matmul(p[:, 0:SC], q, k, start=j == 0, stop=j == 2)
            mm.then_inc(S["pe_s"], 1)

        def dve_s(dve, b, g, s):
            dve.wait_ge(S["pe_s"], SUB * (KD * b + g) + s + 1)
            if b and s == 0 and g in ON_ACT:
                dve.wait_ge(S["act_es"], SUB * (len(ON_ACT) * (b - 1) + ON_ACT.index(g) + 1))
            p = grouped(of("S", b, g, s)[:, 0:SC], HG)
            dve.tensor_reduce(mx[:, SUB * g + s, :], p, AX, ALU.max, negate=True).then_inc(S["dve_max"], 1)
            if g in ON_DVE:
                if s:
                    dve_sub(dve, b, g, s - 1)
                if s == SUB - 1:
                    drip(1)
                    dve_sub(dve, b, g, s)

        def dve_sub(dve, b, g, s):
            if b and s == 0:
                dve.wait_ge(S["pe_pt"], NC * KD * b)
            dve.wait_ge(S["dve_max"], SUB * (KD * b + g) + s + 1)
            dve.tensor_tensor(grouped(E[:, g, s, :], HG), grouped(of("S", b, g, s)[:, 0:SC], HG),
                              spread(mx[:, SUB * g + s, :], M), ALU.add).then_inc(S["dve_sub"], 1)

        def act_s(act, b, g, s):
            if g not in ON_ACT:
                return
            if b and s == 0:
                act.wait_ge(S["pe_pt"], NC * KD * b)
                act.wait_ge(S["dve_rc"], KD * (b - 1) + g + 1)
            act.wait_ge(S["dve_max"], SUB * (KD * b + g) + s + 1)
            for h in range(HG):
                ins = act.activation(E[:, g, s, M * h:M * h + M], of("S", b, g, s)[:, M * h:M * h + M], ACT.Exp,
                                     bias=mx[:, SUB * g + s, h:h + 1],
                                     accum_out=sm[:, g, HG * s + h:HG * s + h + 1])
            ins.then_inc(S["act_es"], 1)

        def act_soft(act, b, g):
            if g in ON_DVE:
                act.wait_ge(score_done(b, g, SUB - 1)[0], score_done(b, g, SUB - 1)[1])
                act.activation(E[:, g], E[:, g], ACT.Exp).then_inc(S["act_exp"], 1)

        def dve_sum(dve, b, g):
            i = KD * b + g
            if g in ON_ACT:
                dve.wait_ge(score_done(b, g, SUB - 1)[0], score_done(b, g, SUB - 1)[1])
            else:
                dve.wait_ge(S["act_exp"], len(ON_DVE) * b + ON_DVE.index(g) + 1)
                n = issued(dve.tensor_reduce(sm[:, g, :], grouped(E[:, g].rearrange("p s c -> p (s c)"), SUB * HG),
                                             AX, ALU.add))
                drip(1)
                dve.wait_ge(dve_chain, n)
            if i >= KD:
                dve.wait_ge(S["pool_p"], i - KD + 1)
            dve.reciprocal(rc[:, g, :], sm[:, g, :]).then_inc(S["dve_rc"], 1)

        def pool_soft(pool, b, g):
            pool.wait_ge(S["dve_rc"], KD * b + g + 1)
            e = grouped(E[:, g].rearrange("p s c -> p (s c)"), SUB * HG)
            nc.gpsimd.tensor_tensor(e, e, spread(rc[:, g, :], M), ALU.mult).then_inc(S["pool_p"], 1)

        def pe_pt(pe, b, g, c):
            p = own_bank(pe, "PT", b, g, c)
            pe.wait_ge(S["pool_p"], KD * b + g + 1)
            for s in range(SUB):
                mm = pe.transpose(p[0:CH[c], P * s:P * s + P], E[:, g, s, CO[c]:CO[c] + CH[c]], ident[:])
            mm.then_inc(S["pe_pt"], 1)

        def act_pt(act, b, g, c):
            j = NC * g + c
            if b == 0 and j == 0:
                act.wait_ge(S["pool_wq"], 1)
                act.wait_ge(S["pool_w1"], 2)
                act.wait_ge(S["w2_lo"], 1)
            if j >= SLOTS:
                act.wait_ge(S["pe_av"], KD * b + (j - SLOTS) // NC + 1)
            act.wait_ge(S["pe_pt"], NC * KD * b + j + 1)
            act.activation(actH[0:CH[c], 0, j % SLOTS, :], of("PT", b, g, c)[0:CH[c], :], ACT.Identity
                           ).then_inc(S["act_pt"], 1)

        def dve_pt(dve, b, g, c):
            j = NC * g + c
            dve.wait_ge(S["act_pt"], NC * KD * b + j + 1)
            dve.tensor_tensor(actH[0:CH[c], 1, j % SLOTS, :], of("PT", b, g, c)[0:CH[c], :],
                              f32(actH[0:CH[c], 0, j % SLOTS, :]), ALU.subtract).then_inc(S["dve_pt"], 1)

        def pe_av(pe, b, g):
            p = own_bank(pe, "AV", b, g)
            pe.wait_ge(ld_v, 16 * VLOADS * (b // BPB + 1))
            for c in range(NC):
                j = NC * g + c
                pe.wait_ge(S["dve_pt"], NC * KD * b + j + 1)
                for i, (v, w) in enumerate(split3([vbd[0:CH[c], h, g, c, :] for h in range(2)],
                                                  [actH[0:CH[c], h, j % SLOTS, :] for h in range(2)])):
                    mm = pe.matmul(p[:], v, w, start=c == 0 and i == 0, stop=c == NC - 1 and i == 2)
            mm.then_inc(S["pe_av"], 1)

        def act_av(act, b, g):
            act.wait_ge(S["pe_av"], KD * b + g + 1)
            act.activation(actA[:, 0, g, :], of("AV", b, g)[:], ACT.Identity).then_inc(S["act_o"], 1)

        def dve_av(dve, b, g):
            dve.wait_ge(S["act_o"], KD * b + g + 1)
            dve.tensor_tensor(actA[:, 1, g, :], of("AV", b, g)[:], f32(actA[:, 0, g, :]), ALU.subtract
                              ).then_inc(S["dve_o"], 1)

        def pe_h(pe, b, m):
            p = own_bank(pe, "H", b, m)
            if b == 0:
                pe.wait_ge(S["pool_w1"], 2)
            for k in range(KD):
                pe.wait_ge(S["dve_o"], KD * b + k + 1)
                for j, (w, a) in enumerate(split3([w1[:, h, k, P * m:P * m + P] for h in range(2)],
                                                  [actA[:, h, k, :] for h in range(2)])):
                    mm = pe.matmul(p[:], w, a, start=k == 0 and j == 0, stop=k == KD - 1 and j == 2)
            mm.then_inc(S["pe_h"], 1)

        def act_h(act, b, m):
            i = MF * b + m
            act.wait_ge(S["pe_h"], i + 1)
            if i >= 2:
                act.wait_ge(S["dve_h"], i - 1)
            act.activation(htmp[m % 2][:], of("H", b, m)[:], ACT.Relu, bias=b1[:, m:m + 1]).then_inc(S["act_h"], 1)
            act.activation(actH[:, 0, m, :], of("H", b, m)[:], ACT.Relu, bias=b1[:, m:m + 1]).then_inc(S["act_hh"], 1)

        def dve_h(dve, b, m):
            dve.wait_ge(S["act_hh"], MF * b + m + 1)
            dve.tensor_tensor(actH[:, 1, m, :], htmp[m % 2][:], f32(actH[:, 0, m, :]), ALU.subtract
                              ).then_inc(S["dve_h"], 1)

        def y_products(pe, b, s, chunks_):
            p = of("YA", b, s)
            for m in chunks_:
                pe.wait_ge(S["dve_h"], MF * b + m + 1)
                for j, (a, w) in enumerate(split3([actH[:, h, m, P * s:P * s + P] for h in range(2)],
                                                  [w2[:, h, m, :] for h in range(2)])):
                    mm = pe.matmul(p[:], a, w, start=m == 0 and j == 0, stop=m == MF - 1 and j == 2)
            return mm

        def pe_ya(pe, b, s):
            own_bank(pe, "YA", b, s)
            if b == 0:
                pe.wait_ge(S["w2_lo"], 2)
            y_products(pe, b, s, range(MF // 2))

        def pe_y(pe, b, s):
            y_products(pe, b, s, range(MF // 2, MF)).then_inc(S["pe_y"], 1)

        bn2_done = {}

        def dve_y(dve, b, s):
            dve.wait_ge(S["pe_y"], SUB * b + s + 1)
            dve.wait_ge(S["pool_xb"], SUB * b + s + 1)
            r = rows[b % 2][:, s, 0:D]
            dve.tensor_tensor(r, of("YA", b, s)[:], r, ALU.add).then_inc(S["dve_x2"], 1)

            def chain():
                dve.wait_ge(S["dve_x2"], SUB * b + s + 1)
                bn2_done[b] = issued(dve.bn_stats(bn2[:, s, :], r))
                yield
            chains.append(chain())

        def dve_x2stat(dve, b):
            def chain():
                n = yield from aggregate(dve, bn2, mv, bn2_done[b])
                n = yield from rsqrt(dve, mv[:, :, 1], r1[:], n)
                dve.wait_ge(dve_chain, n)
                dve.scalar_tensor_tensor(nmr[:], mv[:, :, 0], -1.0, r1[:], ALU.mult, ALU.mult
                                         ).then_inc(S["dve_s2"], 1)
                yield
            if bn2_done.get(b) is None:
                drain()
            chains.append(chain())

        def act_xt(act, b, s):
            act.wait_ge(S["dve_s2"], b + 1)
            if b + 1 < NBLK:
                act.wait_ge(S["pe_pt"], NC * KD * (b + 2))
            act.activation(xt(s), rows[b % 2][:, s, 0:D], ACT.Identity, bias=nmr[:, s:s + 1],
                           scale=r1[:, s:s + 1]).then_inc(S["act_xt"], 1)

        def pe_tt(pe, b, s):
            p = own_bank(pe, "TT", b, s)
            pe.wait_ge(S["act_xt"], SUB * b + s + 1)
            for k in range(KD):
                mm = pe.transpose(p[:, P * k:P * k + P], xt(s)[:, P * k:P * k + P], ident[:])
            mm.then_inc(S["pe_tt"], 1)

        def act_tt(act, b, s):
            act.wait_ge(S["pe_tt"], SUB * b + s + 1)
            act.activation(actQ[:, 0, :, P * s:P * s + P], of("TT", b, s)[:].rearrange("p (k t) -> p k t", k=KD),
                           ACT.Identity).then_inc(S["act_tt"], 1)

        def dve_tt(dve, b, s):
            dve.wait_ge(S["act_tt"], SUB * b + s + 1)
            dve.tensor_tensor(actQ[:, 1, :, P * s:P * s + P], of("TT", b, s)[:].rearrange("p (k t) -> p k t", k=KD),
                              f32(actQ[:, 0, :, P * s:P * s + P]), ALU.subtract).then_inc(S["dve_tt"], 1)

        def dve_rowtail(dve, b):
            def chain():
                for s in range(SUB):
                    dve.wait_ge(S["act_xt"], SUB * b + s + 1)
                    n = issued(dve.bn_stats(bn[:, s, :], xt(s)))
                    yield
                n = yield from aggregate(dve, bn, mv, n)
                n = yield from rsqrt(dve, mv[:, :, 1], r2[:], n)
                r = rows[b % 2]
                dve.wait_ge(dve_chain, n)
                dve.tensor_tensor(r[:, :, D], r1[:], r2[:], ALU.mult)
                n = issued(dve.tensor_tensor(tB[:], nmr[:], mv[:, :, 0], ALU.subtract))
                yield
                dve.wait_ge(dve_chain, n)
                dve.tensor_tensor(r[:, :, D + 1], tB[:], r2[:], ALU.mult)
                dve.tensor_copy(r[:, :, D + 2].bitcast(U32), ids[:, SUB * b:SUB * b + SUB]).then_inc(S["dve_row"], 1)
                yield
            chains.append(chain())

        def pe_l(pe, b):
            p = own_bank(pe, "L", b)
            if b == 0:
                pe.wait_ge(S["dve_const"], 1)
            pe.wait_ge(S["dve_tt"], SUB * (b + 1))
            for k in range(KD):
                for h in range(2):
                    mm = pe.matmul(p[0:2 * NE, :], wg[:, k].rearrange("p h e -> p (h e)"), actQ[:, h, k, :],
                                   start=k == 0 and h == 0, stop=k == KD - 1 and h == 1)
            mm.then_inc(S["pe_l"], 1)

        def act_l(act, b):
            act.wait_ge(S["pe_l"], b + 1)
            act.activation(lgT, of("L", b)[0:2 * NE, :], ACT.Identity).then_inc(S["act_l"], 1)

        def pe_lt(pe, b):
            p = own_bank(pe, "LT", b)
            pe.wait_ge(S["act_l"], b + 1)
            for s in range(SUB):
                mm = pe.transpose(p[:, 2 * NE * s:2 * NE * (s + 1)], lgT[:, P * s:P * s + P],
                                  ident[0:2 * NE, 0:2 * NE])
            mm.then_inc(S["pe_lt"], 1)

        def dve_lt(dve, b):
            dve.wait_ge(S["pe_lt"], b + 1)
            parts_ = of("LT", b)[:, 0:SUB * 2 * NE].rearrange("p (s h e) -> p s h e", h=2, e=NE)
            n = issued(dve.tensor_copy(lg[:], parts_[:, :, 0, :]))
            dve.wait_ge(dve_chain, n)
            dve.tensor_tensor(lg[:], lg[:], parts_[:, :, 1, :], ALU.add).then_inc(S["dve_lg"], 1)
            drip(1)
            dve.wait_ge(S["dve_lg"], b + 1)
            for f in (lambda: dve.tensor_reduce(lm[:], lg[:], AX, ALU.max),
                      lambda: dve.tensor_tensor(lw[:], lg[:], spread(lm[:], NE), ALU.is_equal),
                      lambda: dve.tensor_tensor(lw[:], lw[:], prio[:], ALU.mult),
                      lambda: dve.tensor_reduce(lm[:], lw[:], AX, ALU.max)):
                n = issued(f())
                drip(1)
                dve.wait_ge(dve_chain, n)
            dve.tensor_tensor(oh[:], prio[:], spread(lm[:], NE), ALU.is_equal).then_inc(S["dve_oh"], 1)

        def pe_rk(pe, b):
            p = own_bank(pe, "RK", b)
            w = SUB * NE
            pe.wait_ge(S["dve_oh"], b + 1)
            if b:
                pe.wait_ge(S["dve_cum"], b)
            o_ = oh[:].rearrange("p s e -> p (s e)")
            pe.matmul(p[:, 0:w], tri[:], o_, start=True, stop=False)
            for s in range(1, SUB):
                pe.matmul(p[:, NE * s:w], ones[:], o_[:, 0:w - NE * s], start=False, stop=False)
            for s in range(SUB):
                mm = pe.matmul(p[:, NE * s:NE * s + NE], ones[:], cum[:], start=False, stop=s == SUB - 1)
            mm.then_inc(S["pe_rk"], 1)

        def dve_rk(dve, b):
            dve.wait_ge(S["pe_rk"], b + 1)
            if b >= 2:
                for s in range(SUB):
                    dve.wait_ge(scat[b % 2][s], 16 * (b // 2))
            dve.tensor_tensor(rk[:], of("RK", b)[:, 0:SUB * NE].rearrange("p (s e) -> p s e", e=NE), base[:], ALU.add
                              ).then_inc(S["dve_rk"], 1)
            n1 = issued(dve.tensor_reduce(lw[:, 0, :], oh[:].rearrange("p s e -> p e s"), AX, ALU.add))
            dve.wait_ge(S["dve_rk"], b + 1)
            n2 = issued(dve.tensor_tensor(rk[:], rk[:], oh[:], ALU.mult))
            dve.wait_ge(dve_chain, n1)
            dve.tensor_tensor(cum[:], cum[:], lw[:, 0, :], ALU.add).then_inc(S["dve_cum"], 1)
            dve.wait_ge(dve_chain, n2)
            n3 = issued(dve.tensor_reduce(posf[:], rk[:], AX, ALU.add))
            drip(1)
            dve.wait_ge(dve_chain, n3)
            dve.tensor_copy(pos[b % 2][:], posf[:]).then_inc(S["dve_pos"], 1)

        def pool_scat(pool, b):
            pool.wait_ge(S["dve_pos"], b + 1)
            pool.wait_ge(S["dve_row"], b + 1)
            for s in range(SUB):
                nc.gpsimd.indirect_dma_start(
                    out=region, out_offset=bass.IndirectOffsetOnAxis(ap=pos[b % 2][:, s:s + 1], axis=0),
                    in_=rows[b % 2][:, s, :], in_offset=None).then_inc(scat[b % 2][s], 16)

        def pe_b1(pe):
            own_bank(pe, "B1")
            pe.wait_ge(L["ln"], 32)
            pe.wait_ge(L["e1"], 16)
            for e in range(NE):
                p = bank[bank_of[("B1",)][e // 4]][:, EH * (e % 4):EH * (e % 4) + EH]
                for k in range(KD):
                    mm = pe.matmul(p, lnb[:, k, e:e + 1].to_broadcast([P, P]), e1[:, k, e, :], start=k == 0, stop=k == KD - 1)
            mm.then_inc(S["pe_b1"], 1)

        def dve_b1(dve):
            dve.wait_ge(S["pe_b1"], 1)
            dve.wait_ge(L["eb"], 32)
            for j in range(2):
                t = b1e[:, 4 * j:4 * j + 4, :].rearrange("p e h -> p (e h)")
                ins = dve.tensor_tensor(t, bank[bank_of[("B1",)][j]][:], t, ALU.add)
            ins.then_inc(S["dve_b1"], 1)
            for k in range(KD):
                ins = dve.tensor_tensor(e1[:, k], e1[:, k], spread(lns[:, k, :], EH), ALU.mult)
            ins.then_inc(S["dve_e1"], 1)

        def act_e2conv(act):
            act.wait_ge(S["pe_h"], MF * NBLK)
            act.wait_ge(L["e2"], 16)
            act.activation(e2[:, 0], e2_raw[:], ACT.Identity).then_inc(S["act_e2"], 1)

        def dve_e2conv(dve):
            dve.wait_ge(S["act_e2"], 1)
            dve.tensor_tensor(e2[:, 1], e2_raw[:], f32(e2[:, 0]), ALU.subtract).then_inc(S["dve_e2"], 1)

        def pe_pads(pe):
            p = own_bank(pe, "PADS")
            pe.wait_ge(S["dve_cum"], NBLK)
            pe.matmul(p[:, 0:NE], ones[:], cum[:], start=True, stop=True).then_inc(S["pe_cnt"], 1)

        def dve_pads(dve):
            dve.wait_ge(S["pe_cnt"], 1)
            dve.wait_ge(L["tab"], 48)
            dve.tensor_copy(cnt[:], of("PADS")[:, 0:NE]).then_inc(S["dve_cnt"], 1)
            dve.wait_ge(S["dve_cnt"], 1)
            dve_link(dve, dve.tensor_tensor(padf[:], regions[:], cnt[:], ALU.add))
            dve.tensor_copy(padi[:], padf[:]).then_inc(S["dve_pad"], 1)

        def dve_table(dve):
            dve_link(dve, dve.tensor_scalar(cti[:], cnt[:], float(P - 1), None, ALU.add))
            dve_link(dve, dve.tensor_scalar(cti[:], cti[:], 7, None, ALU.logical_shift_right))
            dve_link(dve, dve.tensor_copy(ctl[:], cti[:]))
            dve.tensor_scalar(stp[:], ctl[:], -float(P), float(REG), ALU.mult, ALU.add)
            dve_link(dve, dve.tensor_copy(cinc[:], ctl[:]))
            for e in range(1, NE):
                dve_link(dve, dve.tensor_tensor(cinc[:, e:e + 1], cinc[:, e:e + 1], cinc[:, e - 1:e], ALU.add))
            bc = lambda t: t[0:1, :].unsqueeze(1).to_broadcast([1, NT, NE])
            dve_link(dve, dve.tensor_tensor(ge[:], jt[:], bc(cinc), ALU.is_ge))
            dve_link(dve, dve.tensor_reduce(ex[:], ge[:], AX, ALU.add))
            dve_link(dve, dve.tensor_scalar(exi[:], ex[:], float(NE - 1), None, ALU.min))
            dve_link(dve, dve.tensor_tensor(ge[:], ge[:], bc(stp), ALU.mult))
            dve_link(dve, dve.tensor_reduce(rw[:], ge[:], AX, ALU.add))
            dve_link(dve, dve.scalar_tensor_tensor(rw[:], jt[:, :, 0], float(P), rw[:], ALU.mult, ALU.add))
            dve.tensor_scalar(rwi[:], rw[:], float(NE * REG), None, ALU.min).then_inc(S["dve_tab"], 1)

        def sp_pads(sp):
            sp.wait_ge(S["dve_pad"], 1)
            reg = sp.alloc_register("pad_row")
            for e in range(NE):
                sp.reg_load(reg, padi[0:1, e:e + 1])
                r = sp.snap(reg, min_val=REG * e, max_val=REG * e + N)
                sp.dma_start(region[bass.ds(r, P), :], padrow[:]).then_inc(st_pad, 16)

        regs = {}

        def load_reg(eng, name, ap, hi):
            if name not in regs:
                regs[name] = eng.alloc_register(name)
                eng.wait_ge(S["dve_tab"], 1)
            eng.reg_load(regs[name], ap)
            return eng.snap(regs[name], min_val=0, max_val=hi)

        experts = {}

        def expert(eng, who, t):
            if (who, t) not in experts:
                experts[who, t] = load_reg(eng, f"{who}_expert{t % NREG}", exi[0:1, t:t + 1], NE - 1)
            return experts[who, t]

        NREG = 4

        def pick(ap, e):
            return ap[:, bass.ds(e, 1), :].rearrange("p e n -> p (e n)")

        def sp_bload(sp, t):
            if t == 0:
                for s in range(SUB):
                    for i in range(2):
                        sp.wait_ge(scat[i][s], 16 * (NBLK // 2))
                sp.wait_ge(st_pad, 16 * NE)
                sp.wait_ge(L["pad0"], 16)
                sp.wait_ge(S["pe_y"], SUB * NBLK)
            if t >= NROW:
                sp.wait_ge(st_out[t % NROW], 16 * (t // NROW))
            r = load_reg(sp, "row", rwi[0:1, t:t + 1], NE * REG)
            sp.dma_start(rowB[t % NROW][:], region[bass.ds(r, P), :]).then_inc(ld_row[t % NROW], 16)

        def dve_bx(dve, t):
            r = rowB[t % NROW]
            dve.wait_ge(ld_row[t % NROW], 16 * (t // NROW + 1))
            if t >= 2:
                dve.wait_ge(S["b_xT"], t - 1)
            dve.tensor_scalar(xh[t % 2][:], r[:, 0:D], r[:, D:D + 1], r[:, D + 1:D + 2], ALU.mult, ALU.add
                              ).then_inc(S["b_xh"], 1)

            expert(dve, "dve", t)

        def add_b2(eng, who, t):
            eng.wait_ge(S["b_xh"], t + 1)
            if t < 2:
                eng.wait_ge(L["eb"], 32)
            r = rowB[t % NROW][:, 0:D]
            eng.tensor_tensor(r, r, pick(b2e, expert(eng, who, t)), ALU.add).then_inc(b_xb[t % 2], 1)

        def pool_bx(pool, t):
            if t % 2 == 0:
                add_b2(pool, "pool", t)

        def dve_b2(dve, t):
            if t % 2:
                add_b2(dve, "dve", t)

        def pe_bx(pe, t):
            p = own_bank(pe, "B_XT", t)
            pe.wait_ge(S["b_xh"], t + 1)
            for k in range(KD):
                mm = pe.transpose(p[:, P * k:P * k + P], xh[t % 2][:, P * k:P * k + P], ident[:])
            mm.then_inc(S["b_xT"], 1)

        def act_bx(act, t):
            act.wait_ge(S["b_xT"], t + 1)
            if t >= 2:
                act.wait_ge(S["b_h"], t - 1)
            act.activation(xhT[t % 2][:], of("B_XT", t)[:].rearrange("p (k t) -> p k t", k=KD), ACT.Identity
                           ).then_inc(S["b_xTs"], 1)

        def pe_bh(pe, t):
            p = own_bank(pe, "B_H", t)[:, 0:EH]
            pe.wait_ge(S["b_xTs"], t + 1)
            if t == 0:
                pe.wait_ge(S["dve_e1"], 1)
            e = expert(pe, "pe", t)
            for k in range(KD):
                mm = pe.matmul(p, xhT[t % 2][:, k, :], pick(e1[:, k], e), start=k == 0, stop=k == KD - 1)
            mm.then_inc(S["b_h"], 1)
            if t + 1 < NT:
                expert(pe, "pe", t + 1)

        def dve_bh(dve, t):
            dve.wait_ge(S["b_h"], t + 1)
            if t >= 2:
                dve.wait_ge(S["b_gl"], t - 1)
            dve.tensor_tensor(hb[t % 2][:], of("B_H", t)[:, 0:EH], pick(b1e, expert(dve, "dve", t)), ALU.add
                              ).then_inc(S["b_hb"], 1)

        def act_bh(act, t):
            act.wait_ge(S["b_hb"], t + 1)
            if t >= 2:
                act.wait_ge(S["b_g"], t - 1)
            act.activation(gl[t % 2][:], hb[t % 2][:], ACT.Gelu).then_inc(S["b_gl"], 1)

        def pe_bg(pe, t):
            p = own_bank(pe, "B_G", t)
            pe.wait_ge(S["b_gl"], t + 1)
            pe.transpose(p[:, 0:P], gl[t % 2][:], ident[:]).then_inc(S["b_g"], 1)

        def act_bg(act, t):
            act.wait_ge(S["b_g"], t + 1)
            if t >= 2:
                act.wait_ge(S["b_y"], t - 1)
            act.activation(gT[t % 2][:, 0, :], of("B_G", t)[:, 0:P], ACT.Identity).then_inc(S["b_ghi"], 1)

        def dve_bg(dve, t):
            dve.wait_ge(S["b_ghi"], t + 1)
            dve.tensor_tensor(gT[t % 2][:, 1, :], of("B_G", t)[:, 0:P], f32(gT[t % 2][:, 0, :]), ALU.subtract
                              ).then_inc(S["b_glo"], 1)

        def pe_by(pe, t):
            p = own_bank(pe, "B_Y", t)
            pe.wait_ge(S["b_glo"], t + 1)
            if t == 0:
                pe.wait_ge(S["dve_e2"], 1)
            e = expert(pe, "pe", t)
            for j, (g, w) in enumerate(split3([gT[t % 2][:, h, :] for h in range(2)],
                                              [pick(e2[:, h], e) for h in range(2)])):
                mm = pe.matmul(p[:], g, w, start=j == 0, stop=j == 2)
            mm.then_inc(S["b_y"], 1)

        def dve_by(dve, t):
            dve.wait_ge(S["b_y"], t + 1)
            dve.wait_ge(b_xb[t % 2], t // 2 + 1)
            r = rowB[t % NROW][:, 0:D]
            dve.tensor_tensor(r, of("B_Y", t)[:], r, ALU.add).then_inc(S["b_out"], 1)

        def pool_by(pool, t):
            pool.wait_ge(S["b_out"], t + 1)
            r = rowB[t % NROW]
            nc.gpsimd.indirect_dma_start(
                out=out, out_offset=bass.IndirectOffsetOnAxis(ap=r[:, D + 2:D + 3].bitcast(U32), axis=0),
                in_=r[:, 0:D], in_offset=None, bounds_check=N - 1, oob_is_err=False).then_inc(st_out[t % NROW], 16)

        parts = {
            "SETUP": {"sp": sp_setup, "pool": pool_setup, "dve": dve_setup},
            "XLOAD": {"sp": sp_xload},
            "KP": {"pe": pe_kp, "act": act_kp, "dve": dve_kp},
            "KSTORE": {"sp": sp_kstore},
            "CONV_WQ": {"act": act_conv_wq, "pool": pool_conv_wq},
            "W1_LOAD": {"sp": sp_w1load},
            "CONV_W1": {"act": act_conv_w1, "pool": pool_conv_w1},
            "W2_LOAD": {"sp": sp_w2load},
            "CONV_W2": {"dve": dve_conv_w2, "pool": pool_conv_w2},
            "ZERO_ROWS": {"pool": pool_zero_row},
            "CONSTS": {"dve": dve_consts},
            "KLOAD": {"sp": sp_kload},
            "VP": {"pe": pe_vp, "dve": dve_vp, "act": act_vp},
            "VSTORE": {"sp": sp_vstore},
            "VLOAD": {"sp": sp_vload},
            "XSTAT": {"dve": dve_xstat},
            "XT": {"pe": pe_xT, "act": act_xT, "dve": dve_xT, "pool": pool_xT},
            "Q": {"pe": pe_q, "act": act_q, "dve": dve_q},
            "S": {"pe": pe_s, "dve": dve_s, "act": act_s},
            "EXP": {"act": act_soft},
            "SUM": {"dve": dve_sum, "pool": pool_soft},
            "PT": {"pe": pe_pt, "act": act_pt, "dve": dve_pt},
            "AV": {"pe": pe_av, "act": act_av, "dve": dve_av},
            "H": {"pe": pe_h, "act": act_h},
            "HLO": {"dve": dve_h},
            "YA": {"pe": pe_ya},
            "Y": {"pe": pe_y, "dve": dve_y},
            "X2STAT": {"dve": dve_x2stat},
            "XTT": {"act": act_xt},
            "TT": {"pe": pe_tt, "act": act_tt, "dve": dve_tt},
            "L": {"pe": pe_l, "act": act_l},
            "ROWTAIL": {"dve": dve_rowtail},
            "DRIP": {"dve": lambda dve, n: drip(n)},
            "DRAIN": {"dve": lambda dve: drain()},
            "LT": {"pe": pe_lt, "dve": dve_lt},
            "RK": {"pe": pe_rk, "dve": dve_rk},
            "SCAT": {"pool": pool_scat},
            "E1_LOAD": {"sp": sp_e1load},
            "E2_LOAD": {"sp": sp_e2load},
            "E2_CONV": {"act": act_e2conv, "dve": dve_e2conv},
            "B1": {"pe": pe_b1, "dve": dve_b1},
            "PADS": {"pe": pe_pads, "dve": dve_pads, "sp": sp_pads},
            "TABLE": {"dve": dve_table},
            "EB_LOAD": {"sp": sp_ebload},
            "B_X": {"sp": sp_bload, "dve": dve_bx},
            "B_XT": {"pe": pe_bx, "act": act_bx, "dve": dve_b2, "pool": pool_bx},
            "B_H": {"pe": pe_bh, "act": act_bh, "dve": dve_bh},
            "B_G": {"pe": pe_bg, "act": act_bg, "dve": dve_bg},
            "B_Y": {"pe": pe_by, "dve": dve_by, "pool": pool_by},
        }

        def walk(eng, who):
            for kind, *i in sched:
                if who in parts[kind]:
                    parts[kind][who](eng, *i)
                if who == "dve":
                    drip(DRIP.get(kind, 0))

        block = ctx.enter_context(nc.Block())

        @block.sync
        def _(sp):
            walk(sp, "sp")
            for i in range(NROW):
                sp.wait_ge(st_out[i], 16 * len(range(i, NT, NROW)))

        @block.gpsimd
        def _(pool):
            walk(pool, "pool")

        @block.scalar
        def _(act):
            walk(act, "act")

        @block.vector
        def _(dve):
            walk(dve, "dve")

        @block.tensor
        def _(pe):
            walk(pe, "pe")


def kernel(**inputs):
    import numpy as np
    import concourse.bacc as _bacc
    from concourse import mybir as _mybir
    from concourse.bass_utils import run_bass_kernel_spmd as _run

    a = {k: np.asarray(v) for k, v in inputs.items()}

    def chunks(w, k):
        return w.reshape(k, P, -1).transpose(1, 0, 2)

    p = np.arange(P)
    f = np.float32
    dev = {
        "x": a["x"].reshape(N, D),
        "ctxT": chunks(a["ctx_768"].transpose(2, 0, 1).reshape(TD, NB * M), KT),
        "Wq": chunks(a["L0_xattn_Wq"], KD).reshape(P, -1),
        "Wk": chunks(a["L0_xattn_Wk"], KT),
        "Wv": chunks(a["L0_xattn_Wv"], KT),
        "W1": chunks(a["L0_xattn_W1"], KD).reshape(P, -1),
        "W2": chunks(a["L0_xattn_W2"], MF).reshape(P, -1),
        "bq": a["L0_xattn_bq"].reshape(KD, P).T,
        "bk": a["L0_xattn_bk"].reshape(KD, P).T,
        "bv": a["L0_xattn_bv"].reshape(1, D),
        "b1": a["L0_xattn_b1"].reshape(MF, P).T,
        "b2": a["L0_xattn_b2"].reshape(1, D),
        "WgT": chunks(a["L0_ffn_Wg"].T, KD).reshape(P, -1),
        "lns": chunks(a["L0_ffn_ln_scale"].T, KD),
        "lnb": chunks(a["L0_ffn_ln_bias"].T, KD),
        "E1": a["L0_ffn_W1"].reshape(NE, KD, P, EH).transpose(2, 1, 0, 3),
        "Eb1": a["L0_ffn_b1"].reshape(1, NE, EH),
        "E2": a["L0_ffn_W2"].transpose(1, 0, 2),
        "Eb2": a["L0_ffn_b2"].reshape(1, NE, D),
        "ident": np.eye(P, dtype=f),
        "masks": np.concatenate([(p[:, None] < p[None, :]).astype(f), np.ones((P, P), f)], 1),
        "prio": np.broadcast_to((NE - np.arange(NE)).astype(f), (P, SUB, NE)),
        "base": np.broadcast_to((REG * np.arange(NE)).astype(f), (P, SUB, NE)),
        "ids": (p[:, None] + P * np.arange(N // P)[None, :]).astype(np.uint32),
        "regions": np.broadcast_to((REG * np.arange(NE)).astype(f), (P, NE)),
        "jt": np.broadcast_to(np.arange(NT, dtype=f)[None, :, None], (1, NT, NE)),
    }
    pad = np.zeros((P, ROW), f)
    pad[:, D + 2] = np.full(P, N, np.uint32).view(f)
    dev["padrow"] = pad
    dev = {k: np.ascontiguousarray(v) for k, v in dev.items()}

    nc = _bacc.Bacc("TRN2", target_bir_lowering=False, num_devices=1, dynamic_dma_scratch_size=8192)
    A = {k: nc.dram_tensor(f"in_{k}", v.shape, _mybir.dt.from_np(v.dtype), kind="ExternalInput").ap()
         for k, v in dev.items()}
    out = nc.dram_tensor("out_0", (N, D), F32, kind="ExternalOutput").ap()
    xattn_moe_kernel(nc, A, out)
    r = _run(nc, [{f"in_{k}": v for k, v in dev.items()}], core_ids=[0])
    return r.results[0]["out_0"].reshape(NB, TOK, D)
```
